# Optimizing a Trainium2 kernel written in Bass

```python
import numpy as np
import jax
import jax.numpy as jnp

def _softmax(x, axis=-1):
    return jax.nn.softmax(x, axis=axis)

def _gelu(x):
    return jax.nn.gelu(x, approximate=True)

def _silu(x):
    return jax.nn.silu(x)

def _sigmoid(x):
    return jax.nn.sigmoid(x)

def _layernorm(x, axis=-1, eps=1e-05):
    m = jnp.mean(x, axis=axis, keepdims=True)
    v = jnp.var(x, axis=axis, keepdims=True)
    return (x - m) / jnp.sqrt(v + eps)

def _scatter_add(tgt, idx, src, axis=0):
    return tgt.at[idx].add(src)

def _segment_sum(src, seg, n):
    return jax.ops.segment_sum(src, seg, n)
kernel_name = 'mk_gnn_resnorm_d4_gnn_r8_18ac4e'

def setup_inputs(seed: int=0):
    np.random.seed(seed)
    _w = jnp.asarray

    def _rec_inputs():
        import jax
        import jax.numpy as jnp
        _gk = jax.random.key(seed)
        x = -0.0001006 + 1 * jax.random.normal(jax.random.fold_in(_gk, 1), (6250, 96), jnp.float32)
        _s = jax.random.randint(jax.random.fold_in(_gk, 2), (100000,), 0, 6250, jnp.int32)
        _d = jax.random.randint(jax.random.fold_in(_gk, 3), (100000,), 0, 6250, jnp.int32)
        _loop = jnp.arange(6250, dtype=jnp.int32)
        src = jnp.concatenate([_s, _d, _loop])
        dst = jnp.concatenate([_d, _s, _loop])
        _o = jnp.argsort(dst, stable=True)
        src = src[_o]
        dst = dst[_o]
        edge_attr_32 = 0.000196303 + 1.00016 * jax.random.normal(jax.random.fold_in(_gk, 12), (206250, 32), jnp.float32)
        return (x, src, dst, edge_attr_32)
    x, src, dst, edge_attr_32 = _rec_inputs()

    def _L0_gnn_setup():
        import jax, jax.numpy as jnp
        import numpy as np
        N_NODES = 6250
        N_EDGES = 100000
        D_MODEL = 96
        HEADS = 4
        key = jax.random.key(seed)
        ks = jax.random.split(key, 6)
        scale = 1.0 / np.sqrt(D_MODEL)
        return {'embeds': jax.random.normal(ks[0], (N_NODES, D_MODEL), dtype=jnp.float32), 'qW': jax.random.normal(ks[1], (D_MODEL, D_MODEL), dtype=jnp.float32) * scale, 'kW': jax.random.normal(ks[2], (D_MODEL, D_MODEL), dtype=jnp.float32) * scale, 'vW': jax.random.normal(ks[3], (D_MODEL, D_MODEL), dtype=jnp.float32) * scale, 'rows': jax.random.randint(ks[4], (N_EDGES,), 0, N_NODES, dtype=jnp.int32), 'cols': jax.random.randint(ks[5], (N_EDGES,), 0, N_NODES, dtype=jnp.int32)}
    _L0_gnn_all = _L0_gnn_setup()
    _L0_gnn_in = {k: v for k, v in _L0_gnn_all.items() if k in ('qW', 'kW', 'vW')}
    del _L0_gnn_all

    def _L1_gnn_setup():
        import jax, jax.numpy as jnp
        import numpy as np
        N_NODES = 6250
        N_EDGES = 100000
        IN_DIM = 96
        OUT_DIM = 96
        EDGE_DIM = 32
        BN_EPS = 1e-05
        key = jax.random.key(seed)
        ks = jax.random.split(key, 12)
        x = jax.random.normal(ks[0], (N_NODES, IN_DIM), dtype=jnp.float32)
        edge_index = jax.random.randint(ks[1], (2, N_EDGES), 0, N_NODES, dtype=jnp.int64)
        edge_attr = jax.random.normal(ks[2], (N_EDGES, EDGE_DIM), dtype=jnp.float32)
        We = jax.random.normal(ks[3], (EDGE_DIM, IN_DIM), dtype=jnp.float32) / np.sqrt(EDGE_DIM)
        be = jnp.zeros((IN_DIM,), dtype=jnp.float32)
        W1 = jax.random.normal(ks[4], (IN_DIM, OUT_DIM), dtype=jnp.float32) / np.sqrt(IN_DIM)
        b1 = jnp.zeros((OUT_DIM,), dtype=jnp.float32)
        W2 = jax.random.normal(ks[5], (OUT_DIM, OUT_DIM), dtype=jnp.float32) / np.sqrt(OUT_DIM)
        b2 = jnp.zeros((OUT_DIM,), dtype=jnp.float32)
        gamma = jnp.ones((OUT_DIM,), dtype=jnp.float32)
        beta = jnp.zeros((OUT_DIM,), dtype=jnp.float32)
        return {'x': x, 'edge_index': edge_index, 'edge_attr': edge_attr, 'We': We, 'be': be, 'W1': W1, 'b1': b1, 'W2': W2, 'b2': b2, 'gamma': gamma, 'beta': beta}
    _L1_gnn_all = _L1_gnn_setup()
    _L1_gnn_in = {k: v for k, v in _L1_gnn_all.items() if k in ('We', 'be', 'W1', 'b1', 'W2', 'b2', 'gamma', 'beta')}
    del _L1_gnn_all

    def _L2_gnn_setup():
        import jax, jax.numpy as jnp
        import numpy as np
        N, E = (6250, 100000)
        DIN = DOUT = 96
        DE = 32

        def _egnn_conv(x, src, dst, edge_attr, W_msg, W_edge, W_root, b):
            msg = x[src] @ W_msg + edge_attr @ W_edge
            agg = jax.ops.segment_max(msg, dst, num_segments=x.shape[0])
            agg = jnp.where(jnp.isneginf(agg), 0.0, agg)
            return agg + x @ W_root + b
        key = jax.random.key(seed)
        ks = jax.random.split(key, 10)
        rn = lambda k, sh, sc: jax.random.normal(k, sh, jnp.float32) * sc
        return {'X': rn(ks[0], (N, DIN), 1.0), 'edge_index': jax.random.randint(ks[1], (2, E), 0, N, jnp.int32), 'edge_attr': rn(ks[2], (E, DE), 1.0), 'W1_msg': rn(ks[3], (DIN, DOUT), DIN ** (-0.5)), 'W1_edge': rn(ks[4], (DE, DOUT), DE ** (-0.5)), 'W1_root': rn(ks[5], (DIN, DOUT), DIN ** (-0.5)), 'b1': jnp.zeros((DOUT,), jnp.float32), 'W2_msg': rn(ks[6], (DOUT, DOUT), DOUT ** (-0.5)), 'W2_edge': rn(ks[7], (DE, DOUT), DE ** (-0.5)), 'W2_root': rn(ks[8], (DOUT, DOUT), DOUT ** (-0.5)), 'b2': jnp.zeros((DOUT,), jnp.float32)}
    _L2_gnn_all = _L2_gnn_setup()
    _L2_gnn_in = {k: v for k, v in _L2_gnn_all.items() if k in ('W1_msg', 'W1_edge', 'W1_root', 'b1', 'W2_msg', 'W2_edge', 'W2_root', 'b2')}
    del _L2_gnn_all

    def _L3_gnn_setup():
        import jax, jax.numpy as jnp
        import numpy as np
        N_NODES = 6250
        N_EDGES = 100000
        D_IN = 96
        D_OUT = 96
        NEG_SLOPE = 0.2
        key = jax.random.key(seed)
        k1, k2, k3, k4, k5 = jax.random.split(key, 5)
        x = jax.random.normal(k1, (N_NODES, D_IN), dtype=jnp.float32)
        W = jax.random.normal(k2, (D_IN, D_OUT), dtype=jnp.float32) * (1.0 / np.sqrt(D_IN))
        att_src = jax.random.normal(k3, (D_OUT,), dtype=jnp.float32) * 0.1
        att_dst = jax.random.normal(k4, (D_OUT,), dtype=jnp.float32) * 0.1
        bias = jnp.zeros((D_OUT,), dtype=jnp.float32)
        edge_index = jax.random.randint(k5, (2, N_EDGES), 0, N_NODES, dtype=jnp.int64)
        return {'x': x, 'W': W, 'att_src': att_src, 'att_dst': att_dst, 'bias': bias, 'edge_index': edge_index}
    _L3_gnn_all = _L3_gnn_setup()
    _L3_gnn_in = {k: v for k, v in _L3_gnn_all.items() if k in ('W', 'att_src', 'att_dst', 'bias')}
    del _L3_gnn_all
    return {'x': x, 'src': src, 'dst': dst, 'edge_attr_32': edge_attr_32, 'L0_gnn_qW': _L0_gnn_in['qW'], 'L0_gnn_kW': _L0_gnn_in['kW'], 'L0_gnn_vW': _L0_gnn_in['vW'], 'L1_gnn_We': _L1_gnn_in['We'], 'L1_gnn_be': _L1_gnn_in['be'], 'L1_gnn_W1': _L1_gnn_in['W1'], 'L1_gnn_b1': _L1_gnn_in['b1'], 'L1_gnn_W2': _L1_gnn_in['W2'], 'L1_gnn_b2': _L1_gnn_in['b2'], 'L1_gnn_gamma': _L1_gnn_in['gamma'], 'L1_gnn_beta': _L1_gnn_in['beta'], 'L2_gnn_W1_msg': _L2_gnn_in['W1_msg'], 'L2_gnn_W1_edge': _L2_gnn_in['W1_edge'], 'L2_gnn_W1_root': _L2_gnn_in['W1_root'], 'L2_gnn_b1': _L2_gnn_in['b1'], 'L2_gnn_W2_msg': _L2_gnn_in['W2_msg'], 'L2_gnn_W2_edge': _L2_gnn_in['W2_edge'], 'L2_gnn_W2_root': _L2_gnn_in['W2_root'], 'L2_gnn_b2': _L2_gnn_in['b2'], 'L3_gnn_W': _L3_gnn_in['W'], 'L3_gnn_att_src': _L3_gnn_in['att_src'], 'L3_gnn_att_dst': _L3_gnn_in['att_dst'], 'L3_gnn_bias': _L3_gnn_in['bias']}

def reference(x, src, dst, edge_attr_32, L0_gnn_qW, L0_gnn_kW, L0_gnn_vW, L1_gnn_We, L1_gnn_be, L1_gnn_W1, L1_gnn_b1, L1_gnn_W2, L1_gnn_b2, L1_gnn_gamma, L1_gnn_beta, L2_gnn_W1_msg, L2_gnn_W1_edge, L2_gnn_W1_root, L2_gnn_b1, L2_gnn_W2_msg, L2_gnn_W2_edge, L2_gnn_W2_root, L2_gnn_b2, L3_gnn_W, L3_gnn_att_src, L3_gnn_att_dst, L3_gnn_bias):
    import jax
    import jax.numpy as jnp

    def _L0_gnn_ref(embeds, qW, kW, vW, rows, cols):
        import jax, jax.numpy as jnp
        import numpy as np
        N_NODES = 6250
        N_EDGES = 100000
        D_MODEL = 96
        HEADS = 4
        nvar, d = embeds.shape
        dh = d // HEADS
        e = rows.shape[0]
        q = (embeds[rows] @ qW).reshape(e, HEADS, dh)
        k = (embeds[cols] @ kW).reshape(e, HEADS, dh)
        v = (embeds[cols] @ vW).reshape(e, HEADS, dh)
        scores = jnp.clip(jnp.einsum('ehd,ehd->eh', q, k), -10.0, 10.0)
        exp_s = jnp.exp(scores)
        norms = jax.ops.segment_sum(exp_s, rows, num_segments=nvar)[rows]
        w = exp_s / (norms + 1e-08)
        res = jax.ops.segment_sum(w[:, :, None] * v, rows, num_segments=nvar).reshape(nvar, d)
        return embeds + res

    def _L1_gnn_ref(x, edge_index, edge_attr, We, be, W1, b1, W2, b2, gamma, beta):
        import jax, jax.numpy as jnp
        import numpy as np
        N_NODES = 6250
        N_EDGES = 100000
        IN_DIM = 96
        OUT_DIM = 96
        EDGE_DIM = 32
        BN_EPS = 1e-05
        src = edge_index[0]
        dst = edge_index[1]
        msg = jax.nn.relu(x[src] + edge_attr @ We + be)
        aggr = jax.ops.segment_sum(msg, dst, num_segments=x.shape[0])
        h = x + aggr
        h = jax.nn.relu(h @ W1 + b1) @ W2 + b2
        mean = jnp.mean(h, axis=0)
        var = jnp.mean(jnp.square(h - mean), axis=0)
        h = (h - mean) * jax.lax.rsqrt(var + BN_EPS) * gamma + beta
        return jax.nn.relu(h)

    def _L2_gnn_ref(X, edge_index, edge_attr, W1_msg, W1_edge, W1_root, b1, W2_msg, W2_edge, W2_root, b2):
        import jax, jax.numpy as jnp
        import numpy as np
        N, E = (6250, 100000)
        DIN = DOUT = 96
        DE = 32

        def _egnn_conv(x, src, dst, edge_attr, W_msg, W_edge, W_root, b):
            msg = x[src] @ W_msg + edge_attr @ W_edge
            agg = jax.ops.segment_max(msg, dst, num_segments=x.shape[0])
            agg = jnp.where(jnp.isneginf(agg), 0.0, agg)
            return agg + x @ W_root + b
        src, dst = (edge_index[0], edge_index[1])
        c1 = jax.nn.leaky_relu(_egnn_conv(X, src, dst, edge_attr, W1_msg, W1_edge, W1_root, b1))
        c2 = jax.nn.leaky_relu(_egnn_conv(c1, src, dst, edge_attr, W2_msg, W2_edge, W2_root, b2))
        return c2

    def _L3_gnn_ref(x, W, att_src, att_dst, bias, edge_index):
        import jax, jax.numpy as jnp
        import numpy as np
        N_NODES = 6250
        N_EDGES = 100000
        D_IN = 96
        D_OUT = 96
        NEG_SLOPE = 0.2
        N = x.shape[0]
        h = x @ W
        loops = jnp.arange(N, dtype=edge_index.dtype)
        src = jnp.concatenate([edge_index[0], loops])
        dst = jnp.concatenate([edge_index[1], loops])
        a_src = h @ att_src
        a_dst = h @ att_dst
        e = jax.nn.leaky_relu(a_src[src] + a_dst[dst], NEG_SLOPE)
        m = jax.ops.segment_max(e, dst, num_segments=N)
        e = jnp.exp(e - m[dst])
        denom = jax.ops.segment_sum(e, dst, num_segments=N)
        alpha = e / (denom[dst] + 1e-16)
        out = jax.ops.segment_sum(h[src] * alpha[:, None], dst, num_segments=N)
        return jnp.tanh(out + bias)
    edge_index = jnp.stack([src, dst])
    x = _layernorm(x + _L0_gnn_ref(x, L0_gnn_qW, L0_gnn_kW, L0_gnn_vW, src, dst), axis=-1)
    x = _layernorm(x + _L1_gnn_ref(x, edge_index, edge_attr_32, L1_gnn_We, L1_gnn_be, L1_gnn_W1, L1_gnn_b1, L1_gnn_W2, L1_gnn_b2, L1_gnn_gamma, L1_gnn_beta), axis=-1)
    x = _layernorm(x + _L2_gnn_ref(x, edge_index, edge_attr_32, L2_gnn_W1_msg, L2_gnn_W1_edge, L2_gnn_W1_root, L2_gnn_b1, L2_gnn_W2_msg, L2_gnn_W2_edge, L2_gnn_W2_root, L2_gnn_b2), axis=-1)
    x = _layernorm(x + _L3_gnn_ref(x, L3_gnn_W, L3_gnn_att_src, L3_gnn_att_dst, L3_gnn_bias, edge_index), axis=-1)
    return x

_drawn_inputs = setup_inputs


def setup_inputs(seed=0):
    import zlib

    import numpy as np

    out = dict(_drawn_inputs(seed))
    spreads = {'L1_gnn_be': (0.0, 0.282),
     'L1_gnn_b1': (0.0, 2.0),
     'L1_gnn_b2': (0.0, 2.0),
     'L1_gnn_gamma': (1.0, 0.2),
     'L1_gnn_beta': (0.0, 0.274),
     'L2_gnn_b1': (0.0, 0.274),
     'L2_gnn_b2': (0.0, 0.359),
     'L3_gnn_bias': (0.0, 0.1)}
    factors = {'L3_gnn_att_dst': 200.0, 'L3_gnn_att_src': 2.715}
    for name, (base, spread) in spreads.items():
        noise = np.random.default_rng([zlib.crc32(name.encode()), seed]).standard_normal(out[name].shape)
        drawn = base * np.exp(spread * noise) if base else spread * noise
        out[name] = jnp.asarray(drawn.astype(out[name].dtype))
    for name, factor in factors.items():
        out[name] = (out[name] * factor).astype(out[name].dtype)
    return out
```

```python
from contextlib import ExitStack

import numpy as np

import concourse.bass as bass
from concourse import mybir

F32 = mybir.dt.float32
BF16 = mybir.dt.bfloat16
I32 = mybir.dt.int32
ALU = mybir.AluOpType
ACT = mybir.ActivationFunctionType
AX_X = mybir.AxisListType.X

P = 128
K = 4
CH = P * K
G = 7
HEADS = 4
LANES = 2
NEG = -2.9e38
EPS = 1e-5


def padded_sizes(n_nodes, n_edges):
    n_tiles = -(-(n_nodes + 1) // (P * G)) * G
    n_chunks = -(-n_edges // (CH * LANES)) * LANES
    return n_tiles, n_chunks


PASSED = {}


def loop(eng, n, body):
    body(0)
    if n > 1:
        with eng.Fori(1, n) as it:
            body(it)


class Steps:

    def __init__(self, sem, names):
        self.sem, self.names = sem, list(names)

    def give(self, instruction, name):
        assert name in self.names
        instruction.then_inc(self.sem, 1)

    def wait(self, eng, name, it, back=0):
        n, at = len(self.names), self.names.index(name) + 1
        wait_count(eng, self.sem, it, n, at - back * n)


def wait_count(eng, sem, it, per, plus):
    if isinstance(it, int):
        if it * per + plus > 0:
            eng.wait_ge(sem, it * per + plus)
    else:
        eng.wait_ge(sem, it * per + plus)
        if id(eng) in PASSED:
            eng.sem_inc(PASSED[id(eng)], 1)


def build(nc, t, n_nodes, n_edges, D, DE):
    NT, NCH = padded_sizes(n_nodes, n_edges)
    NG = NT // G
    NROW = NT * P
    EP = NCH * CH
    EC = EP // P
    DH = D // HEADS
    PAY = D + HEADS
    TROW = NROW + P
    NTAB = LANES * K
    HW = D + 2
    DN = D + 1
    NQ = 2 * NT
    NQB = NQ // G
    assert TROW % P == 0 and D % HEADS == 0 and NT <= P and CH == 512

    def scratch(name, shape, dt=F32):
        return nc.dram_tensor(name, shape, dt, kind="Internal").ap()

    q_tab = scratch("q_tab", (NROW, D))
    kv_tab = scratch("kv_tab", (NROW, 2 * D))
    sum_tab = [scratch(f"sum_tab{j}", (TROW, PAY)) for j in range(NTAB)]
    x_tab = scratch("x_tab", (NROW, D))
    h_tab = scratch("h_tab", (NROW, HW))
    keep_row = scratch("keep_row", (EP,), BF16)
    neg_row = scratch("neg_row", (EP,), BF16)
    decay_row = scratch("decay_row", (EP,))
    weight_lin = scratch("weight_lin", (EP,))
    asrc_lin = scratch("asrc_lin", (EP,))
    adst_lin = scratch("adst_lin", (EP, 1))
    rmax_lin = scratch("rmax_lin", (EP, 1))
    carry_dram = scratch("carry_dram", (8, P))
    h_lin = scratch("h_lin", (EP, HW))
    scan_out = scratch("scan_out", (EP, D))
    scan_out3 = scratch("scan_out3", (EP, DN))

    def bcast_row(ap1d, parts, n):
        return ap1d.rearrange("(a n) -> a n", a=1).to_broadcast([parts, n])

    with ExitStack() as top:
        for eng, name in ((nc.sync, "passed_sp"), (nc.gpsimd, "passed_pool")):
            PASSED[id(eng)] = top.enter_context(nc.semaphore(name))

        def keepb(name, shape, dt=F32):
            return top.enter_context(nc.sbuf_tensor(name, shape, dt))

        X = keepb("X", [P, NT, D])
        R = keepb("R", [P, NT, D])
        ident = keepb("ident", [P, P])
        tri = keepb("tri", [P, P])
        ones_f = keepb("ones_f", [1, P])
        ones_b = keepb("ones_b", [1, P], BF16)
        eps_col = keepb("eps_col", [P, 1])
        dump_col = keepb("dump_col", [P, 1])
        node_q = keepb("node_q", [P, NQ])
        end_idx = keepb("end_idx", [P, NT], I32)
        start_idx = keepb("start_idx", [P, NT], I32)
        flag = keepb("flag", [P, NT])
        asrc = keepb("asrc", [P, NT])
        adst = keepb("adst", [P, NT])
        w96 = {n: keepb("w_" + n, [D, D]) for n in
               ("qW", "kW", "vW", "W1", "W2", "W1_msg", "W1_root", "W2_msg", "W2_root", "W")}
        we = {n: keepb("we_" + n, [DE + 1, D]) for n in ("We", "W1_edge", "W2_edge")}
        cols = {n: keepb("c_" + n, [D, 1]) for n in ("b1", "b2", "gamma", "beta")}
        rows = {n: keepb("r_" + n, [P, D]) for n in ("l2b1", "l2b2", "att_src", "att_dst", "bias")}

        class Phase:

            def __init__(self, name):
                self.name = name

            def __enter__(self):
                self.ctx = ExitStack()
                self.ctx.__enter__()
                return self

            def __exit__(self, *a):
                return self.ctx.__exit__(*a)

            def sb(self, n, shape, dt=F32):
                return self.ctx.enter_context(nc.sbuf_tensor(f"{self.name}_{n}", shape, dt))

            def ps(self, n, shape):
                return self.ctx.enter_context(nc.psum_tensor(f"{self.name}_{n}", shape, F32))

            def sem(self, n):
                return self.ctx.enter_context(nc.semaphore(f"{self.name}_{n}"))

            def steps(self, n, names):
                return Steps(self.sem(n), names)

            def block(self):
                return self.ctx.enter_context(nc.Block())

        with Phase("const") as ph:
            s_w, s_m, s_p, s_v = ph.sem("w"), ph.sem("m"), ph.sem("p"), ph.sem("v")
            qi = ph.sb("qi", [P, NQ], I32)
            di = ph.sb("di", [P, 1], I32)
            with nc.Block() as block:
                loads = [(X[:, :, :], t["x"].rearrange("(t p) d -> p t d", p=P))]
                for n, key in (("qW", "L0_gnn_qW"), ("kW", "L0_gnn_kW"), ("vW", "L0_gnn_vW"), ("W1", "L1_gnn_W1"),
                               ("W2", "L1_gnn_W2"), ("W1_msg", "L2_gnn_W1_msg"), ("W1_root", "L2_gnn_W1_root"),
                               ("W2_msg", "L2_gnn_W2_msg"), ("W2_root", "L2_gnn_W2_root"), ("W", "L3_gnn_W")):
                    loads.append((w96[n][:, :], t[key]))
                for n, key in (("We", "L1_gnn_We"), ("W1_edge", "L2_gnn_W1_edge"), ("W2_edge", "L2_gnn_W2_edge")):
                    loads.append((we[n][0:DE, :], t[key]))
                loads.append((we["We"][DE:DE + 1, :], t["L1_gnn_be"].rearrange("(a n) -> a n", a=1)))
                for n, key in (("b1", "L1_gnn_b1"), ("b2", "L1_gnn_b2"), ("gamma", "L1_gnn_gamma"), ("beta", "L1_gnn_beta")):
                    loads.append((cols[n][:, :], t[key].rearrange("(n a) -> n a", a=1)))
                for n, key in (("l2b1", "L2_gnn_b1"), ("l2b2", "L2_gnn_b2"), ("att_src", "L3_gnn_att_src"),
                               ("att_dst", "L3_gnn_att_dst"), ("bias", "L3_gnn_bias")):
                    loads.append((rows[n][:, :], bcast_row(t[key], P, D)))

                @block.sync
                def _(e):
                    for dst, src in loads:
                        e.dma_start(dst, src).then_inc(s_w, 16)
                    e.wait_ge(s_w, 16 * len(loads))

                @block.gpsimd
                def _(e):
                    e.memset(ident[:, :], 0.0).then_inc(s_p, 1)
                    e.memset(tri[:, :], 1.0).then_inc(s_p, 1)
                    e.iota(qi[:, :], pattern=[[-1, 2], [P, NT]], base=0, channel_multiplier=1).then_inc(s_p, 1)
                    e.iota(di[:, :], pattern=[[0, 1]], base=NROW, channel_multiplier=1).then_inc(s_p, 1)
                    e.wait_ge(s_p, 4)
                    e.affine_select(out=ident[:, :], in_=ident[:, :], compare_op=ALU.not_equal, fill=1.0, base=0,
                                    pattern=[[-1, P]], channel_multiplier=1).then_inc(s_p, 1)
                    e.affine_select(out=tri[:, :], in_=tri[:, :], compare_op=ALU.is_gt, fill=0.0, base=0,
                                    pattern=[[-1, P]], channel_multiplier=1).then_inc(s_p, 1)
                    e.wait_ge(s_p, 6)

                @block.vector
                def _(e):
                    e.memset(we["W1_edge"][DE:DE + 1, :], 0.0)
                    e.memset(we["W2_edge"][DE:DE + 1, :], 0.0)
                    e.memset(ones_f[:, :], 1.0)
                    e.memset(ones_b[:, :], 1.0)
                    e.memset(eps_col[:, :], EPS)
                    e.wait_ge(s_p, 4)
                    e.tensor_copy(node_q[:, :], qi[:, :]).then_inc(s_v, 1)
                    e.tensor_copy(dump_col[:, :], di[:, :]).then_inc(s_v, 1)
                    e.wait_ge(s_v, 2)

        with Phase("find") as ph:
            dst_rows = t["dst_pad"].rearrange("(r c) -> r c", c=CH)
            first_i = ph.sb("first_i", [1, NCH], I32)
            first_f = ph.sb("first_f", [1, NCH])
            firsts = ph.sb("firsts", [P, NCH])
            junk = ph.sb("junk", [P, NCH])
            rows_le = ph.sb("rows_le", [P, NQ])
            row_f = ph.sb("row_f", [P, NQ])
            row_i = ph.sb("row_i", [P, G], I32)
            got_i = ph.sb("got_i", [P, G, CH], I32)
            got_f = ph.sb("got_f", [P, G, CH])
            junk2 = ph.sb("junk2", [P, G, CH])
            in_row = ph.sb("in_row", [P, NQ])
            upto = ph.sb("upto", [P, NQ])
            tmp = ph.sb("tmp", [P, NT])
            tmp2 = ph.sb("tmp2", [P, NT])
            dst_i = ph.sb("dst_i", [P, EC], I32)
            prev_i = ph.sb("prev_i", [P, EC], I32)
            keep_b = ph.sb("keep_b", [P, EC], BF16)
            neg_b = ph.sb("neg_b", [P, EC], BF16)
            firsts_ps = ph.ps("firsts_ps", [P, 512])
            s_ld, s_g, s_st = ph.sem("ld"), ph.sem("g"), ph.sem("st")
            s_pre, s_pe = ph.sem("pre"), ph.sem("pe")
            vec = ph.steps("vec", ["rowidx"])
            assert NCH <= 512
            with nc.Block() as block:
                @block.sync
                def _(e):
                    with nc.allow_non_contiguous_dma(reason="one element of each row"):
                        e.dma_start(first_i[:, :], t["dst_pad"].rearrange("(a r c) -> a r c", a=1, c=CH)[:, :, 0:1]
                                    .rearrange("a r c -> a (r c)"), allow_slow_non_contiguous=True).then_inc(s_ld, 16)
                    e.dma_start(dst_i[:, :], t["dst_pad"].rearrange("(p c) -> p c", p=P)).then_inc(s_ld, 16)
                    e.dma_start(prev_i[:, :], t["dst_prev"].rearrange("(p c) -> p c", p=P)).then_inc(s_ld, 16)
                    e.wait_ge(s_pre, 2 + NQ + 3)
                    e.dma_start(keep_row.rearrange("(p c) -> p c", p=P), keep_b[:, :]).then_inc(s_st, 16)
                    e.dma_start(neg_row.rearrange("(p c) -> p c", p=P), neg_b[:, :]).then_inc(s_st, 16)
                    e.wait_ge(s_st, 32)

                @block.tensor
                def _(e):
                    e.wait_ge(s_pre, 1)
                    e.matmul(firsts_ps[:, 0:NCH], ones_f[:, :], first_f[:, :], start=True, stop=True).then_inc(s_pe, 1)

                @block.gpsimd
                def _(e):
                    def body(it):
                        vec.wait(e, "rowidx", it)
                        for g in range(G):
                            e.indirect_dma_start(got_i[:, g, :], None, dst_rows,
                                                 bass.IndirectOffsetOnAxis(row_i[:, g:g + 1], axis=0),
                                                 bounds_check=NCH - 1, oob_is_err=False).then_inc(s_g, 16)
                    loop(e, NQB, body)

                @block.vector
                def _(e):
                    e.wait_ge(s_ld, 48)
                    e.tensor_copy(first_f[:, :], first_i[:, :]).then_inc(s_pre, 1)
                    e.wait_ge(s_pe, 1)
                    e.tensor_copy(firsts[:, :], firsts_ps[:, 0:NCH]).then_inc(s_pre, 1)
                    e.wait_ge(s_pre, 2)
                    for q in range(NQ):
                        e.wait_ge(s_pre, 2 + q)
                        e.tensor_scalar(junk[:, :], firsts[:, :], node_q[:, q:q + 1], 0.0, ALU.is_le, ALU.add,
                                        accum_out=rows_le[:, q:q + 1]).then_inc(s_pre, 1)
                    e.tensor_tensor(keep_b[:, :], dst_i[:, :], prev_i[:, :], ALU.is_equal).then_inc(s_pre, 1)
                    e.wait_ge(s_pre, 2 + NQ + 1)
                    e.tensor_scalar(neg_b[:, :], keep_b[:, :], -NEG, NEG, ALU.mult, ALU.add).then_inc(s_pre, 1)
                    e.tensor_scalar(row_f[:, :], rows_le[:, :], -1.0, 0.0, ALU.add, ALU.max).then_inc(s_pre, 1)
                    e.wait_ge(s_pre, 2 + NQ + 3)

                    def body(it):
                        q0 = it * G
                        vec.give(e.tensor_scalar(row_i[:, :], row_f[:, bass.ds(q0, G)], 1.0, None, ALU.mult), "rowidx")
                        wait_count(e, s_g, it, 16 * G, 16 * G)
                        e.tensor_copy(got_f[:, :, :], got_i[:, :, :]).then_inc(s_chain, 1)
                        wait_count(e, s_chain, it, G + 1, 1)
                        for g in range(G):
                            e.tensor_scalar(junk2[:, g, :], got_f[:, g, :], node_q[:, bass.ds(q0 + g, 1)], 0.0, ALU.is_le,
                                            ALU.add, accum_out=in_row[:, bass.ds(q0 + g, 1)]).then_inc(s_chain, 1)
                        wait_count(e, s_chain, it, G + 1, G + 1)
                    s_chain = ph.sem("chain")
                    loop(e, NQB, body)
                    s_f = ph.sem("fin")
                    e.scalar_tensor_tensor(upto[:, :], row_f[:, :], float(CH), in_row[:, :], ALU.mult, ALU.add).then_inc(s_f, 1)
                    e.wait_ge(s_f, 1)
                    e.tensor_tensor(flag[:, :], upto[:, 0:NT], upto[:, NT:NQ], ALU.is_gt).then_inc(s_f, 1)
                    e.tensor_scalar(end_idx[:, :], upto[:, 0:NT], -1.0, 0.0, ALU.add, ALU.max).then_inc(s_f, 1)
                    e.wait_ge(s_f, 2)
                    e.tensor_scalar(tmp[:, :], flag[:, :], -2.0 * EP, 2.0 * EP, ALU.mult, ALU.add).then_inc(s_f, 1)
                    e.wait_ge(s_f, 4)
                    e.tensor_tensor(start_idx[:, :], tmp[:, :], upto[:, NT:NQ], ALU.add).then_inc(s_f, 1)
                    e.wait_ge(s_f, 5)

        def dve_layernorm(e, V, it, y, d, sq, s1, s2, out, y_step, act):
            V.wait(e, y_step, it)
            V.give(e.tensor_reduce(s1[:, :], y, AX_X, ALU.add), "ln_sum")
            V.wait(e, "ln_sum", it)
            V.give(e.tensor_scalar(s1[:, :], s1[:, :], 1.0 / D, None, ALU.mult), "ln_mean")
            V.wait(e, "ln_mean", it)
            V.give(e.tensor_tensor(d, y, s1[:, :].unsqueeze(2).to_broadcast([P, G, D]), ALU.subtract), "ln_cent")
            V.wait(e, "ln_cent", it)
            V.give(e.tensor_tensor(sq, d, d, ALU.mult), "ln_sq")
            V.wait(e, "ln_sq", it)
            V.give(e.tensor_reduce(s2[:, :], sq, AX_X, ALU.add), "ln_var")
            act.wait(e, "ln_std", it)
            V.give(e.reciprocal(s1[:, :], s2[:, :]), "ln_rstd")
            V.wait(e, "ln_rstd", it)
            V.give(e.tensor_tensor(out, d, s1[:, :].unsqueeze(2).to_broadcast([P, G, D]), ALU.mult), "ln_out")
            V.wait(e, "ln_out", it)

        LN = ["ln_sum", "ln_mean", "ln_cent", "ln_sq", "ln_var", "ln_rstd", "ln_out"]

        def act_std(e, A, V, it, s2):
            V.wait(e, "ln_var", it)
            A.give(e.activation(s2[:, :], s2[:, :], ACT.Sqrt, bias=eps_col[:, 0:1], scale=1.0 / D), "ln_std")

        def pe_transpose_group(e, T, TP, src, it, name):
            for g in range(G):
                ins = e.transpose(TP[0:D, g * P:(g + 1) * P], src[:, g, :], ident[:, :])
            T.give(ins, name)

        with Phase("n1") as ph:
            xg = ph.sb("xg", [P, G, D])
            xT = ph.sb("xT", [D, G * P])
            tab = [ph.sb(f"tab{i}", [P, G, D]) for i in range(3)]
            TP = ph.ps("TP", [P, 1024])
            O = [ph.ps(f"O{i}", [P, 2, 512]) for i in range(3)]
            V = ph.steps("V", ["xg"])
            T = ph.steps("T", ["tr", "mm0", "mm1", "mm2"])
            A = ph.steps("A", ["xT", "o0", "o1", "o2"])
            s_o = ph.sem("o")
            ph_zero = ph.sb("zero", [P, TROW // P * PAY])
            s_z, s_zd = ph.sem("z"), ph.sem("zd")
            with nc.Block() as block:
                @block.vector
                def _(e):
                    def body(it):
                        T.wait(e, "tr", it, 1)
                        V.give(e.tensor_scalar(xg[:, :, :], X[:, bass.ds(it * G, G), :], 1.0, None, ALU.mult), "xg")
                    loop(e, NG, body)

                @block.tensor
                def _(e):
                    def body(it):
                        V.wait(e, "xg", it)
                        A.wait(e, "xT", it, 1)
                        pe_transpose_group(e, T, TP, xg, it, "tr")
                        A.wait(e, "xT", it)
                        for i, n in enumerate(("qW", "kW", "vW")):
                            for g in range(G):
                                ins = e.matmul(O[i][:, g // 4, (g % 4) * P:(g % 4) * P + D], xT[:, g * P:(g + 1) * P],
                                               w96[n][:, :], start=True, stop=True)
                            T.give(ins, f"mm{i}")
                    loop(e, NG, body)

                @block.scalar
                def _(e):
                    def body(it):
                        T.wait(e, "tr", it)
                        A.give(e.activation(xT[:, :], TP[0:D, 0:G * P], ACT.Copy), "xT")
                        for i in range(3):
                            T.wait(e, f"mm{i}", it)
                            wait_count(e, s_o, it, 48, 0)
                            e.activation(tab[i][:, 0:4, :], O[i][:, 0, :].rearrange("p (g c) -> p g c", c=P)[:, :, 0:D], ACT.Copy)
                            A.give(e.activation(tab[i][:, 4:G, :], O[i][:, 1, :].rearrange("p (g c) -> p g c", c=P)[:, 0:G - 4, 0:D], ACT.Copy), f"o{i}")
                    loop(e, NG, body)

                @block.sync
                def _(e):
                    def body(it):
                        rows_at = bass.ds(it * (G * P), G * P)
                        for i, dst in enumerate((q_tab[rows_at, :], kv_tab[rows_at, 0:D], kv_tab[rows_at, D:2 * D])):
                            A.wait(e, f"o{i}", it)
                            e.dma_start(dst.rearrange("(g p) d -> p g d", p=P), tab[i][:, :, :]).then_inc(s_o, 16)
                    loop(e, NG, body)
                    e.wait_ge(s_o, 48 * NG)


                @block.gpsimd
                def _(e):
                    e.memset(ph_zero[:, :], 0.0).then_inc(s_z, 1)
                    e.wait_ge(s_z, 1)
                    for j in range(NTAB):
                        e.dma_start(sum_tab[j].rearrange("(p r) d -> p (r d)", p=P), ph_zero[:, :]).then_inc(s_zd, 16)
                    e.dma_start(adst_lin.rearrange("(p r) d -> p (r d)", p=P), ph_zero[:, 0:EC]).then_inc(s_zd, 16)
                    e.wait_ge(s_zd, 16 * (NTAB + 1))

        with Phase("e0") as ph:
            NI = NCH // LANES
            two = range(LANES)
            src_i = [ph.sb(f"src_i{s}", [P, K], I32) for s in two]
            dst_i = [ph.sb(f"dst_i{s}", [P, K], I32) for s in two]
            src_bc = [ph.sb(f"src_bc{s}", [P, CH], I32) for s in two]
            src_bf = [ph.sb(f"src_bf{s}", [P, CH]) for s in two]
            src_f = [ph.sb(f"src_f{s}", [P, K]) for s in two]
            qg = [ph.sb(f"qg{s}", [P, K, D]) for s in two]
            kvg = [ph.sb(f"kvg{s}", [P, K, 2 * D]) for s in two]
            prod = [ph.sb(f"prod{s}", [P, K, D]) for s in two]
            score = [ph.sb(f"score{s}", [P, K, HEADS]) for s in two]
            pay = [ph.sb(f"pay{s}", [P, K, PAY]) for s in two]
            same = [ph.sb(f"same{s}", [P, K, P]) for s in two]
            junk = [ph.sb(f"junk{s}", [P, K, P]) for s in two]
            dup = [ph.sb(f"dup{s}", [P, K]) for s in two]
            away = [ph.sb(f"away{s}", [P, K]) for s in two]
            srow = [ph.sb(f"srow{s}", [P, K], I32) for s in two]
            comb = [ph.sb(f"comb{s}", [P, K, PAY]) for s in two]
            C = [ph.ps(f"C{s}", [P, 512]) for s in two]
            s_ld = [ph.sem(f"ld{s}") for s in two]
            s_g = [ph.sem(f"g{s}") for s in two]
            s_tab = [ph.sem(f"tab{j}") for j in range(NTAB)]
            V = [ph.steps(f"V{s}", ["conv", "srcf", "prod", "red", "clip", "eq", "dup", "away", "f", "mul", "row", "pay"]) for s in two]
            A = [ph.steps(f"A{s}", ["exp", "comb"]) for s in two]
            T = [ph.steps(f"T{s}", ["mm"]) for s in two]
            src_c = t["src_pad"].rearrange("(c p k) -> c p k", p=P, k=K)
            dst_c = t["dst_pad"].rearrange("(c p k) -> c p k", p=P, k=K)
            src_r = t["src_pad"].rearrange("(c e) -> c e", e=CH)
            with nc.Block() as block:
                @block.sync
                def _(e):
                    def body(it):
                        for s in two:
                            c = it * LANES + s
                            V[s].wait(e, "row", it, 1)
                            wait_count(e, s_g[s], it, 32 * K, 0)
                            e.dma_start(src_i[s][:, :], src_c[bass.ds(c, 1)].rearrange("a p k -> (a p) k")).then_inc(s_ld[s], 16)
                            e.dma_start(dst_i[s][:, :], dst_c[bass.ds(c, 1)].rearrange("a p k -> (a p) k")).then_inc(s_ld[s], 16)
                            e.dma_start(src_bc[s][:, :], src_r[bass.ds(c, 1)].to_broadcast([P, CH])).then_inc(s_ld[s], 16)
                    loop(e, NI, body)

                @block.gpsimd
                def _(e):
                    def scatter(s, it):
                        A[s].wait(e, "comb", it)
                        for k in range(K):
                            wait_count(e, s_tab[s * K + k], it, 16, 0)
                            e.indirect_dma_start(sum_tab[s * K + k], bass.IndirectOffsetOnAxis(srow[s][:, k:k + 1], axis=0),
                                                 comb[s][:, k, :], None, bounds_check=TROW - 1, oob_is_err=True,
                                                 compute_op=ALU.add).then_inc(s_tab[s * K + k], 16)

                    def body(it):
                        for s in two:
                            wait_count(e, s_ld[s], it, 48, 48)
                            V[s].wait(e, "pay", it, 1)
                            for k in range(K):
                                e.indirect_dma_start(qg[s][:, k, :], None, q_tab,
                                                     bass.IndirectOffsetOnAxis(src_i[s][:, k:k + 1], axis=0),
                                                     bounds_check=NROW - 1, oob_is_err=False).then_inc(s_g[s], 16)
                                e.indirect_dma_start(kvg[s][:, k, :], None, kv_tab,
                                                     bass.IndirectOffsetOnAxis(dst_i[s][:, k:k + 1], axis=0),
                                                     bounds_check=NROW - 1, oob_is_err=False).then_inc(s_g[s], 16)
                            if s == 0:
                                if not isinstance(it, int):
                                    scatter_prev(it)
                            else:
                                scatter(0, it)

                    def scatter_prev(it):
                        A[1].wait(e, "comb", it, 1)
                        for k in range(K):
                            wait_count(e, s_tab[K + k], it, 16, -16)
                            e.indirect_dma_start(sum_tab[K + k], bass.IndirectOffsetOnAxis(srow[1][:, k:k + 1], axis=0),
                                                 comb[1][:, k, :], None, bounds_check=TROW - 1, oob_is_err=True,
                                                 compute_op=ALU.add).then_inc(s_tab[K + k], 16)
                    loop(e, NI, body)
                    scatter(1, NI - 1)
                    for j in range(NTAB):
                        e.wait_ge(s_tab[j], 16 * NI)

                @block.vector
                def _(e):
                    def body(it):
                        for s in two:
                            W = V[s]
                            wait_count(e, s_ld[s], it, 48, 48)
                            W.give(e.tensor_copy(src_bf[s][:, :], src_bc[s][:, :]), "conv")
                            W.give(e.tensor_copy(src_f[s][:, :], src_i[s][:, :]), "srcf")
                            wait_count(e, s_g[s], it, 32 * K, 32 * K)
                            W.give(e.tensor_tensor(prod[s][:, :, :], qg[s][:, :, :], kvg[s][:, :, 0:D], ALU.mult), "prod")
                            W.wait(e, "prod", it)
                            W.give(e.tensor_reduce(score[s][:, :, :], prod[s][:, :, :].rearrange("p k (h d) -> p k h d", h=HEADS),
                                                   AX_X, ALU.add), "red")
                            W.wait(e, "red", it)
                            W.give(e.tensor_scalar(score[s][:, :, :], score[s][:, :, :], -10.0, 10.0, ALU.max, ALU.min), "clip")
                            T[s].wait(e, "mm", it, 1)
                            for k in range(K):
                                ins = e.tensor_scalar(same[s][:, k, :], src_bf[s][:, k::K], src_f[s][:, k:k + 1], None, ALU.is_equal)
                            W.give(ins, "eq")
                            W.wait(e, "eq", it)
                            for k in range(K):
                                ins = e.scalar_tensor_tensor(junk[s][:, k, :], same[s][:, k, :], 1.0, tri[:, :], ALU.mult, ALU.mult,
                                                             accum_out=dup[s][:, k:k + 1])
                            W.give(ins, "dup")
                            W.give(e.tensor_scalar(away[s][:, :], src_f[s][:, :], -1.0, dump_col[:, 0:1], ALU.mult, ALU.add), "away")
                            W.wait(e, "away", it)
                            W.give(e.tensor_scalar(dup[s][:, :], dup[s][:, :], 1.0, None, ALU.min), "f")
                            W.wait(e, "f", it)
                            W.give(e.tensor_tensor(away[s][:, :], away[s][:, :], dup[s][:, :], ALU.mult), "mul")
                            W.wait(e, "mul", it)
                            for k in range(K):
                                wait_count(e, s_tab[s * K + k], it, 16, 0)
                            W.give(e.tensor_tensor(srow[s][:, :], src_f[s][:, :], away[s][:, :], ALU.add), "row")
                            A[s].wait(e, "exp", it)
                            W.give(e.tensor_tensor(pay[s][:, :, 0:D].rearrange("p k (h d) -> p k h d", h=HEADS),
                                                   kvg[s][:, :, D:2 * D].rearrange("p k (h d) -> p k h d", h=HEADS),
                                                   pay[s][:, :, D:PAY].unsqueeze(3).to_broadcast([P, K, HEADS, DH]), ALU.mult), "pay")
                    loop(e, NI, body)

                @block.scalar
                def _(e):
                    def body(it):
                        for s in two:
                            V[s].wait(e, "clip", it)
                            T[s].wait(e, "mm", it, 1)
                            A[s].give(e.activation(pay[s][:, :, D:PAY], score[s][:, :, :], ACT.Exp), "exp")
                            T[s].wait(e, "mm", it)
                            for k in range(K):
                                wait_count(e, s_tab[s * K + k], it, 16, 0)
                            A[s].give(e.activation(comb[s][:, :, :], C[s][:, 0:K * PAY].rearrange("p (k c) -> p k c", k=K), ACT.Copy), "comb")
                    loop(e, NI, body)

                @block.tensor
                def _(e):
                    def body(it):
                        for s in two:
                            V[s].wait(e, "pay", it)
                            A[s].wait(e, "comb", it, 1)
                            for k in range(K):
                                ins = e.matmul(C[s][:, k * PAY:(k + 1) * PAY], same[s][:, k, :], pay[s][:, k, :], start=True, stop=True)
                            T[s].give(ins, "mm")
                    loop(e, NI, body)

        with Phase("n2") as ph:
            part = [ph.sb(f"part{j}", [P, G, PAY]) for j in range(NTAB)]
            acc = ph.sb("acc", [P, G, PAY])
            den = ph.sb("den", [P, G, HEADS])
            y = ph.sb("y", [P, G, D])
            d = ph.sb("d", [P, G, D])
            sq = ph.sb("sq", [P, G, D])
            s1, s2 = ph.sb("s1", [P, G]), ph.sb("s2", [P, G])
            xo = ph.sb("xo", [P, G, D])
            V = ph.steps("V", [f"add{j}" for j in range(1, NTAB)] + ["den", "rden", "res", "x2", "y"] + LN + ["keep"])
            A = ph.steps("A", ["ln_std"])
            s_ld, s_o = ph.sem("ld"), ph.sem("o")
            with nc.Block() as block:
                @block.sync
                def _(e):
                    def body(it):
                        V.wait(e, f"add{NTAB - 1}", it, 1)
                        for j in range(NTAB):
                            e.dma_start(part[j][:, :, :], sum_tab[j][bass.ds(it * (G * P), G * P), :].rearrange("(g p) d -> p g d", p=P)).then_inc(s_ld, 16)
                    loop(e, NG, body)

                @block.vector
                def _(e):
                    def body(it):
                        wait_count(e, s_ld, it, 16 * NTAB, 16 * NTAB)
                        for j in range(1, NTAB):
                            a = part[0] if j == 1 else acc
                            if j > 1:
                                V.wait(e, f"add{j - 1}", it)
                            V.give(e.tensor_tensor(acc[:, :, :], a[:, :, :], part[j][:, :, :], ALU.add), f"add{j}")
                        V.wait(e, f"add{NTAB - 1}", it)
                        V.give(e.tensor_scalar(den[:, :, :], acc[:, :, D:PAY], 1e-8, None, ALU.add), "den")
                        V.wait(e, "den", it)
                        V.give(e.reciprocal(den[:, :, :], den[:, :, :]), "rden")
                        V.wait(e, "rden", it)
                        V.give(e.tensor_tensor(y[:, :, :].rearrange("p g (h d) -> p g h d", h=HEADS),
                                               acc[:, :, 0:D].rearrange("p g (h d) -> p g h d", h=HEADS),
                                               den[:, :, :].unsqueeze(3).to_broadcast([P, G, HEADS, DH]), ALU.mult), "res")
                        V.wait(e, "res", it)
                        V.give(e.tensor_tensor(y[:, :, :], y[:, :, :], X[:, bass.ds(it * G, G), :], ALU.add), "x2")
                        V.wait(e, "x2", it)
                        V.give(e.tensor_tensor(y[:, :, :], y[:, :, :], X[:, bass.ds(it * G, G), :], ALU.add), "y")
                        wait_count(e, s_o, it, 16, 0)
                        dve_layernorm(e, V, it, y[:, :, :], d[:, :, :], sq[:, :, :], s1, s2, xo[:, :, :], "y", A)
                        V.give(e.tensor_scalar(X[:, bass.ds(it * G, G), :], xo[:, :, :], 1.0, None, ALU.mult), "keep")
                    loop(e, NG, body)

                @block.scalar
                def _(e):
                    def body(it):
                        act_std(e, A, V, it, s2)
                        V.wait(e, "ln_out", it)
                        e.dma_start(x_tab[bass.ds(it * (G * P), G * P), :].rearrange("(g p) d -> p g d", p=P), xo[:, :, :]).then_inc(s_o, 16)
                    loop(e, NG, body)
                    e.wait_ge(s_o, 16 * NG)

        def edge_pass(name, table, width, func, mask_row, mask_dt, op0, op1, out_lin, edge_w=None, gather=True):
            with Phase(name) as ph:
                NI = NCH // LANES
                two = range(LANES)
                row_w = table.shape[1]
                idx = [ph.sb(f"idx{s}", [P, K], I32 if gather else F32) for s in two]
                got = [ph.sb(f"got{s}", [P, K, row_w]) for s in two]
                scaled = got if gather else [ph.sb(f"scaled{s}", [P, K, width]) for s in two]
                attr = [ph.sb(f"attr{s}", [DE + 1, CH]) for s in two] if edge_w is not None else None
                mask = [ph.sb(f"mask{s}", [1, CH], mask_dt) for s in two]
                msg = [ph.sb(f"msg{s}", [width, CH]) for s in two]
                run = [ph.sb(f"run{s}", [width, CH]) for s in two]
                back = [ph.sb(f"back{s}", [P, K, width]) for s in two]
                M = [ph.ps(f"M{s}", [P, CH]) for s in two]
                Z = [ph.ps(f"Z{s}", [P, CH]) for s in two]
                B = [ph.ps(f"B{s}", [P, CH]) for s in two]
                s_idx = [ph.sem(f"idx{s}") for s in two]
                s_ld = [ph.sem(f"ld{s}") for s in two]
                s_g = [ph.sem(f"g{s}") for s in two]
                s_st = [ph.sem(f"st{s}") for s in two]
                s_init = ph.sem("init")
                T = [ph.steps(f"T{s}", ["fwd", "back"]) for s in two]
                A = [ph.steps(f"A{s}", ["msg", "back"]) for s in two]
                V = [ph.steps(f"V{s}", ["scan"] if gather else ["scale", "scan"]) for s in two]
                NLD = 16 * (2 if edge_w is not None else 1)
                NGT = 16 * (K if gather else 1)
                src_c = (t["src_pad"] if gather else weight_lin).rearrange("(c p k) -> c p k", p=P, k=K)
                lin_c = None if gather else table.rearrange("(c p k) d -> c p (k d)", p=P, k=K)
                mask_c = mask_row.rearrange("(c e) -> c e", e=CH)
                out_c = out_lin.rearrange("(c p k) d -> c p (k d)", p=P, k=K)
                bc_lhs = ones_b if mask_dt == BF16 else ones_f
                with nc.Block() as block:
                    @block.sync
                    def _(e):
                        def body(it):
                            for s in two:
                                c = bass.ds(it * LANES + s, 1)
                                if gather:
                                    wait_count(e, s_g[s], it, NGT, 0)
                                else:
                                    V[s].wait(e, "scale", it, 1)
                                e.dma_start(idx[s][:, :], src_c[c].rearrange("a p k -> (a p) k")).then_inc(s_idx[s], 16)
                                if not gather:
                                    e.dma_start(got[s][:, :, :].rearrange("p k d -> p (k d)"), lin_c[c].rearrange("a p x -> (a p) x")).then_inc(s_g[s], 16)
                                T[s].wait(e, "fwd", it, 1)
                                e.dma_start(mask[s][:, :], mask_c[c]).then_inc(s_ld[s], 16)
                                if edge_w is not None:
                                    e.dma_start(attr[s][:, :], t["attr_T"][:, bass.ds((it * LANES + s) * CH, CH)]).then_inc(s_ld[s], 16)
                        loop(e, NI, body)

                    if gather:
                        @block.gpsimd
                        def _(e):
                            def body(it):
                                for s in two:
                                    wait_count(e, s_idx[s], it, 16, 16)
                                    T[s].wait(e, "fwd", it, 1)
                                    for k in range(K):
                                        e.indirect_dma_start(got[s][:, k, :], None, table,
                                                             bass.IndirectOffsetOnAxis(idx[s][:, k:k + 1], axis=0),
                                                             bounds_check=NROW - 1, oob_is_err=False).then_inc(s_g[s], 16)
                            loop(e, NI, body)

                    @block.tensor
                    def _(e):
                        def body(it):
                            for s in two:
                                wait_count(e, s_ld[s], it, NLD, NLD)
                                V[s].wait(e, "scan", it, 1)
                                e.matmul(Z[s][0:width, :], bc_lhs[:, 0:width], mask[s][:, :], start=True, stop=True)
                                A[s].wait(e, "msg", it, 1)
                                if edge_w is not None:
                                    e.matmul(M[s][0:width, :], edge_w[:, :], attr[s][:, :], start=True, stop=False, skip_group_check=True)
                                if gather:
                                    wait_count(e, s_g[s], it, NGT, NGT)
                                else:
                                    V[s].wait(e, "scale", it)
                                for k in range(K):
                                    ins = e.matmul(M[s][0:width, k::K], scaled[s][:, k, 0:width], ident[:, :],
                                                   start=edge_w is None, stop=True, skip_group_check=True)
                                T[s].give(ins, "fwd")
                            for s in two:
                                V[s].wait(e, "scan", it)
                                A[s].wait(e, "back", it, 1)
                                for k in range(K):
                                    ins = e.transpose(B[s][:, k * width:(k + 1) * width], run[s][:, k::K], ident[0:width, 0:width])
                                T[s].give(ins, "back")
                        loop(e, NI, body)

                    @block.vector
                    def _(e):
                        e.memset(run[1][:, :], 0.0).then_inc(s_init, 1)
                        e.wait_ge(s_init, 1)

                        def scale(s, it):
                            wait_count(e, s_g[s], it, NGT, NGT)
                            wait_count(e, s_idx[s], it, 16, 16)
                            T[s].wait(e, "fwd", it, 1)
                            V[s].give(e.tensor_tensor(scaled[s][:, :, :], got[s][:, :, 0:width],
                                                      idx[s][:, :].unsqueeze(2).to_broadcast([P, K, width]), ALU.mult), "scale")

                        def body(it):
                            for s in two:
                                if not gather:
                                    scale(s, it)
                            for s in two:
                                A[s].wait(e, "msg", it)
                                T[s].wait(e, "fwd", it)
                                V[1 - s].wait(e, "scan", it, 1 - s)
                                V[s].give(e.tensor_tensor_scan(run[s][:, :], Z[s][0:width, :], msg[s][:, :], run[1 - s][:, CH - 1:CH], op0, op1), "scan")
                        loop(e, NI, body)

                    @block.scalar
                    def _(e):
                        def body(it):
                            for s in two:
                                T[s].wait(e, "fwd", it)
                                V[s].wait(e, "scan", it, 1)
                                A[s].give(e.activation(msg[s][:, :], M[s][0:width, :], func), "msg")
                            for s in two:
                                T[s].wait(e, "back", it)
                                wait_count(e, s_st[s], it, 16, 0)
                                A[s].give(e.activation(back[s][:, :, :], B[s][:, 0:K * width].rearrange("p (k d) -> p k d", k=K), ACT.Copy), "back")
                                A[s].wait(e, "back", it)
                                e.dma_start(out_c[bass.ds(it * LANES + s, 1)].rearrange("a p x -> (a p) x"),
                                            back[s][:, :, :].rearrange("p k d -> p (k d)")).then_inc(s_st[s], 16)
                        loop(e, NI, body)
                        for s in two:
                            e.wait_ge(s_st[s], 16 * NI)

        def pool_gather_ends(e, ends, dst, lin, sem, g_wait, it):
            g_wait(it)
            for g in range(G):
                e.indirect_dma_start(dst[:, g, :], None, lin, bass.IndirectOffsetOnAxis(ends[:, g:g + 1], axis=0),
                                     bounds_check=EP - 1, oob_is_err=False).then_inc(sem, 16)

        edge_pass("e1", x_tab, D, ACT.Relu, keep_row, BF16, ALU.mult, ALU.add, scan_out, edge_w=we["We"])

        with Phase("n3") as ph:
            ends = ph.sb("ends", [P, G], I32)
            agg = ph.sb("agg", [P, G, D])
            hT = ph.sb("hT", [D, G * P])
            rT = ph.sb("rT", [D, G * P])
            HT = ph.sb("HT", [D, NT * P])
            TP = ph.ps("TP", [P, 1024])
            O1 = ph.ps("O1", [P, 1024])
            O2 = ph.ps("O2", [P, 1024])
            V = ph.steps("V", ["ends", "flag", "h"])
            T = ph.steps("T", ["tr", "m1", "m2"])
            A = ph.steps("A", ["hT", "r1", "h2"])
            s_g = ph.sem("g")
            HALF = [(0, 512), (512, G * P)]
            with nc.Block() as block:
                @block.gpsimd
                def _(e):
                    loop(e, NG, lambda it: pool_gather_ends(e, ends, agg, scan_out, s_g, lambda i: (V.wait(e, "ends", i), T.wait(e, "tr", i, 1)), it))

                @block.vector
                def _(e):
                    def body(it):
                        wait_count(e, s_g, it, 16 * G, 0)
                        V.give(e.tensor_scalar(ends[:, :], end_idx[:, bass.ds(it * G, G)], 1.0, None, ALU.mult), "ends")
                        wait_count(e, s_g, it, 16 * G, 16 * G)
                        V.give(e.tensor_tensor(agg[:, :, :], agg[:, :, :], flag[:, bass.ds(it * G, G)].unsqueeze(2).to_broadcast([P, G, D]), ALU.mult), "flag")
                        V.wait(e, "flag", it)
                        V.give(e.tensor_tensor(agg[:, :, :], agg[:, :, :], X[:, bass.ds(it * G, G), :], ALU.add), "h")
                    loop(e, NG, body)

                @block.tensor
                def _(e):
                    def body(it):
                        V.wait(e, "h", it)
                        A.wait(e, "hT", it, 1)
                        pe_transpose_group(e, T, TP, agg, it, "tr")
                        A.wait(e, "hT", it)
                        for a, b in HALF:
                            ins = e.matmul(O1[0:D, a:b], w96["W1"][:, :], hT[:, a:b], start=True, stop=True)
                        T.give(ins, "m1")
                        A.wait(e, "r1", it)
                        for a, b in HALF:
                            ins = e.matmul(O2[0:D, a:b], w96["W2"][:, :], rT[:, a:b], start=True, stop=True)
                        T.give(ins, "m2")
                    loop(e, NG, body)

                @block.scalar
                def _(e):
                    def body(it):
                        T.wait(e, "tr", it)
                        A.give(e.activation(hT[:, :], TP[0:D, 0:G * P], ACT.Copy), "hT")
                        T.wait(e, "m1", it)
                        A.give(e.activation(rT[:, :], O1[0:D, 0:G * P], ACT.Relu, bias=cols["b1"][:, 0:1]), "r1")
                        T.wait(e, "m2", it)
                        A.give(e.activation(HT[:, bass.ds(it * (G * P), G * P)], O2[0:D, 0:G * P], ACT.Identity, bias=cols["b2"][:, 0:1]), "h2")
                    loop(e, NG, body)

            mean = ph.sb("mean", [D, 1])
            var = ph.sb("var", [D, 1])
            gain = ph.sb("gain", [D, 1])
            shift = ph.sb("shift", [D, 1])
            SQ = ph.sb("SQ", [D, NT * P])
            s_v, s_a = ph.sem("bv"), ph.sem("ba")
            with nc.Block() as block:
                @block.vector
                def _(e):
                    e.tensor_reduce(mean[:, :], HT[:, 0:n_nodes], AX_X, ALU.add).then_inc(s_v, 1)
                    e.wait_ge(s_v, 1)
                    e.tensor_scalar(mean[:, :], mean[:, :], 1.0 / n_nodes, None, ALU.mult).then_inc(s_v, 1)
                    e.wait_ge(s_v, 2)
                    e.tensor_scalar(HT[:, :], HT[:, :], mean[:, 0:1], None, ALU.subtract).then_inc(s_v, 1)
                    e.wait_ge(s_v, 3)
                    e.tensor_tensor(SQ[:, 0:n_nodes], HT[:, 0:n_nodes], HT[:, 0:n_nodes], ALU.mult).then_inc(s_v, 1)
                    e.wait_ge(s_v, 4)
                    e.tensor_reduce(var[:, :], SQ[:, 0:n_nodes], AX_X, ALU.add).then_inc(s_v, 1)
                    e.wait_ge(s_a, 1)
                    e.reciprocal(var[:, :], var[:, :]).then_inc(s_v, 1)
                    e.wait_ge(s_v, 6)
                    e.tensor_tensor(gain[:, :], var[:, :], cols["gamma"][:, :], ALU.mult).then_inc(s_v, 1)
                    e.wait_ge(s_v, 7)

                @block.scalar
                def _(e):
                    e.wait_ge(s_v, 5)
                    e.activation(var[:, :], var[:, :], ACT.Sqrt, bias=eps_col[0:D, 0:1], scale=1.0 / n_nodes).then_inc(s_a, 1)
                    e.wait_ge(s_v, 7)
                    e.activation(SQ[:, :], HT[:, :], ACT.Relu, bias=cols["beta"][:, 0:1], scale=gain[:, 0:1]).then_inc(s_a, 1)
                    e.wait_ge(s_a, 2)

            y_src = ph.sb("y_src", [D, G * P])
            with Phase("n3b") as p2:
                y = p2.sb("y", [P, G, D])
                d = p2.sb("d", [P, G, D])
                sq = p2.sb("sq", [P, G, D])
                s1, s2 = p2.sb("s1", [P, G]), p2.sb("s2", [P, G])
                V = p2.steps("V", ["ysrc", "y"] + LN + ["keep"])
                A = p2.steps("A", ["ln_std"])
                T = p2.steps("T", ["tr"])
                with nc.Block() as block:
                    @block.tensor
                    def _(e):
                        def body(it):
                            V.wait(e, "ysrc", it)
                            for g in range(G):
                                ins = e.transpose(TP[:, g * P:g * P + D], y_src[:, g * P:(g + 1) * P], ident[0:D, 0:D])
                            T.give(ins, "tr")
                        loop(e, NG, body)

                    @block.vector
                    def _(e):
                        def body(it):
                            T.wait(e, "tr", it, 1)
                            V.give(e.tensor_scalar(y_src[:, :], SQ[:, bass.ds(it * (G * P), G * P)], 1.0, None, ALU.mult), "ysrc")
                            T.wait(e, "tr", it)
                            V.give(e.tensor_tensor(y[:, :, :], TP[:, 0:G * P].rearrange("p (g c) -> p g c", c=P)[:, :, 0:D],
                                                   X[:, bass.ds(it * G, G), :], ALU.add), "y")
                            dve_layernorm(e, V, it, y[:, :, :], d[:, :, :], sq[:, :, :], s1, s2, sq[:, :, :], "y", A)
                            V.give(e.tensor_scalar(X[:, bass.ds(it * G, G), :], sq[:, :, :], 1.0, None, ALU.mult), "keep")
                            V.wait(e, "keep", it)
                        loop(e, NG, body)

                    @block.scalar
                    def _(e):
                        loop(e, NG, lambda it: act_std(e, A, V, it, s2))

        def project(name, S, w_msg, w_root, bias_row, tab_dram):
            with Phase(name) as ph:
                xg = ph.sb("xg", [P, G, D])
                xT = ph.sb("xT", [D, G * P])
                tab = ph.sb("tab", [P, G, D])
                TP = ph.ps("TP", [P, 1024])
                O = [ph.ps(f"O{i}", [P, 1024]) for i in range(2)]
                V = ph.steps("V", ["xg", "root"])
                T = ph.steps("T", ["tr", "mm0", "mm1"])
                A = ph.steps("A", ["xT", "tab"])
                s_o = ph.sem("o")
                with nc.Block() as block:
                    @block.vector
                    def _(e):
                        def body(it):
                            T.wait(e, "tr", it, 1)
                            V.give(e.tensor_scalar(xg[:, :, :], S[:, bass.ds(it * G, G), :], 1.0, None, ALU.mult), "xg")
                            V.wait(e, "xg", it)
                            T.wait(e, "mm1", it)
                            V.give(e.tensor_tensor(R[:, bass.ds(it * G, G), :], O[1][:, 0:G * P].rearrange("p (g c) -> p g c", c=P)[:, :, 0:D],
                                                   bias_row[:, :].unsqueeze(1).to_broadcast([P, G, D]), ALU.add), "root")
                        loop(e, NG, body)

                    @block.tensor
                    def _(e):
                        def body(it):
                            V.wait(e, "xg", it)
                            A.wait(e, "xT", it, 1)
                            pe_transpose_group(e, T, TP, xg, it, "tr")
                            A.wait(e, "xT", it)
                            for i, w in enumerate((w_msg, w_root)):
                                for g in range(G):
                                    ins = e.matmul(O[i][:, g * P:g * P + D], xT[:, g * P:(g + 1) * P], w[:, :], start=True, stop=True)
                                T.give(ins, f"mm{i}")
                        loop(e, NG, body)

                    @block.scalar
                    def _(e):
                        def body(it):
                            T.wait(e, "tr", it)
                            A.give(e.activation(xT[:, :], TP[0:D, 0:G * P], ACT.Copy), "xT")
                            T.wait(e, "mm0", it)
                            wait_count(e, s_o, it, 16, 0)
                            A.give(e.activation(tab[:, :, :], O[0][:, 0:G * P].rearrange("p (g c) -> p g c", c=P)[:, :, 0:D], ACT.Copy), "tab")
                            A.wait(e, "tab", it)
                            e.dma_start(tab_dram[bass.ds(it * (G * P), G * P), :].rearrange("(g p) d -> p g d", p=P), tab[:, :, :]).then_inc(s_o, 16)
                        loop(e, NG, body)
                        e.wait_ge(s_o, 16 * NG)

        def conv_nodes(name, dest, residual):
            with Phase(name) as ph:
                ends = ph.sb("ends", [P, G], I32)
                agg = ph.sb("agg", [P, G, D])
                d = ph.sb("d", [P, G, D])
                sq = ph.sb("sq", [P, G, D])
                s1, s2 = ph.sb("s1", [P, G]), ph.sb("s2", [P, G])
                V = ph.steps("V", ["ends", "flag", "root", "leaky"] + (["y"] + LN if residual else []) + ["keep"])
                A = ph.steps("A", ["ln_std"])
                s_g = ph.sem("g")
                with nc.Block() as block:
                    @block.gpsimd
                    def _(e):
                        loop(e, NG, lambda it: pool_gather_ends(e, ends, agg, scan_out, s_g, lambda i: V.wait(e, "ends", i), it))

                    @block.vector
                    def _(e):
                        def body(it):
                            at = bass.ds(it * G, G)
                            wait_count(e, s_g, it, 16 * G, 0)
                            V.give(e.tensor_scalar(ends[:, :], end_idx[:, at], 1.0, None, ALU.mult), "ends")
                            wait_count(e, s_g, it, 16 * G, 16 * G)
                            V.give(e.tensor_tensor(agg[:, :, :], agg[:, :, :], flag[:, at].unsqueeze(2).to_broadcast([P, G, D]), ALU.mult), "flag")
                            V.wait(e, "flag", it)
                            V.give(e.tensor_tensor(d[:, :, :], agg[:, :, :], R[:, at, :], ALU.add), "root")
                            V.wait(e, "root", it)
                            V.give(e.scalar_tensor_tensor(sq[:, :, :], d[:, :, :], 0.01, d[:, :, :], ALU.mult, ALU.max), "leaky")
                            V.wait(e, "leaky", it)
                            if residual:
                                V.give(e.tensor_tensor(agg[:, :, :], sq[:, :, :], X[:, at, :], ALU.add), "y")
                                dve_layernorm(e, V, it, agg[:, :, :], d[:, :, :], sq[:, :, :], s1, s2, sq[:, :, :], "y", A)
                            V.give(e.tensor_scalar(dest[:, at, :], sq[:, :, :], 1.0, None, ALU.mult), "keep")
                            V.wait(e, "keep", it)
                        loop(e, NG, body)

                    if residual:
                        @block.scalar
                        def _(e):
                            loop(e, NG, lambda it: act_std(e, A, V, it, s2))

        project("p1", X, w96["W1_msg"], w96["W1_root"], rows["l2b1"], x_tab)
        edge_pass("e2a", x_tab, D, ACT.Copy, neg_row, BF16, ALU.add, ALU.max, scan_out, edge_w=we["W1_edge"])
        with Phase("c1") as keep_c1:
            C1 = keep_c1.sb("C1", [P, NT, D])
            conv_nodes("n4", C1, False)
            project("p2", C1, w96["W2_msg"], w96["W2_root"], rows["l2b2"], x_tab)
        edge_pass("e2b", x_tab, D, ACT.Copy, neg_row, BF16, ALU.add, ALU.max, scan_out, edge_w=we["W2_edge"])
        conv_nodes("n5", X, True)

        with Phase("n6") as ph:
            xg = ph.sb("xg", [P, G, D])
            xT = ph.sb("xT", [D, G * P])
            tab = ph.sb("tab", [P, G, HW])
            pr = ph.sb("pr", [P, G, D])
            starts = ph.sb("starts", [P, G], I32)
            ad = ph.sb("ad", [P, G])
            TP = ph.ps("TP", [P, 1024])
            O = ph.ps("O", [P, 1024])
            V = ph.steps("V", ["xg", "h", "ps", "as", "pd", "ad", "one", "tas", "kh", "kas", "kad", "st"])
            T = ph.steps("T", ["tr", "mm"])
            A = ph.steps("A", ["xT"])
            s_o, s_sc = ph.sem("o"), ph.sem("sc")
            with nc.Block() as block:
                @block.vector
                def _(e):
                    def body(it):
                        at = bass.ds(it * G, G)
                        T.wait(e, "tr", it, 1)
                        V.give(e.tensor_scalar(xg[:, :, :], X[:, at, :], 1.0, None, ALU.mult), "xg")
                        T.wait(e, "mm", it)
                        wait_count(e, s_o, it, 16, 0)
                        wait_count(e, s_sc, it, 16 * G, 0)
                        V.give(e.tensor_copy(tab[:, :, 0:D], O[:, 0:G * P].rearrange("p (g c) -> p g c", c=P)[:, :, 0:D]), "h")
                        V.wait(e, "h", it)
                        V.give(e.tensor_tensor(pr[:, :, :], tab[:, :, 0:D], rows["att_src"][:, :].unsqueeze(1).to_broadcast([P, G, D]), ALU.mult), "ps")
                        V.wait(e, "ps", it)
                        V.give(e.tensor_reduce(ad[:, :], pr[:, :, :], AX_X, ALU.add), "as")
                        V.wait(e, "as", it)
                        V.give(e.tensor_scalar(asrc[:, at], ad[:, :], 1.0, None, ALU.mult), "pd")
                        V.give(e.tensor_copy(tab[:, :, D + 1:D + 2], ad[:, :].unsqueeze(2)), "ad")
                        V.wait(e, "ad", it)
                        V.give(e.tensor_tensor(pr[:, :, :], tab[:, :, 0:D], rows["att_dst"][:, :].unsqueeze(1).to_broadcast([P, G, D]), ALU.mult), "one")
                        V.wait(e, "one", it)
                        V.give(e.tensor_reduce(ad[:, :], pr[:, :, :], AX_X, ALU.add), "tas")
                        V.wait(e, "tas", it)
                        V.give(e.tensor_scalar(adst[:, at], ad[:, :], 1.0, None, ALU.mult), "kh")
                        V.give(e.memset(tab[:, :, D:D + 1], 1.0), "kas")
                        V.give(e.tensor_scalar(R[:, at, :], tab[:, :, 0:D], 1.0, None, ALU.mult), "kad")
                        V.give(e.tensor_scalar(starts[:, :], start_idx[:, at], 1.0, None, ALU.mult), "st")
                    loop(e, NG, body)

                @block.tensor
                def _(e):
                    def body(it):
                        V.wait(e, "xg", it)
                        A.wait(e, "xT", it, 1)
                        pe_transpose_group(e, T, TP, xg, it, "tr")
                        A.wait(e, "xT", it)
                        for g in range(G):
                            ins = e.matmul(O[:, g * P:g * P + D], xT[:, g * P:(g + 1) * P], w96["W"][:, :], start=True, stop=True)
                        T.give(ins, "mm")
                    loop(e, NG, body)

                @block.scalar
                def _(e):
                    def body(it):
                        T.wait(e, "tr", it)
                        A.give(e.activation(xT[:, :], TP[0:D, 0:G * P], ACT.Copy), "xT")
                        V.wait(e, "st", it)
                        e.dma_start(h_tab[bass.ds(it * (G * P), G * P), :].rearrange("(g p) d -> p g d", p=P), tab[:, :, :]).then_inc(s_o, 16)
                    loop(e, NG, body)
                    e.wait_ge(s_o, 16 * NG)

                @block.gpsimd
                def _(e):
                    def body(it):
                        V.wait(e, "st", it)
                        for g in range(G):
                            e.indirect_dma_start(adst_lin, bass.IndirectOffsetOnAxis(starts[:, g:g + 1], axis=0), ad[:, g:g + 1],
                                                 None, bounds_check=EP - 1, oob_is_err=False).then_inc(s_sc, 16)
                    loop(e, NG, body)
                    e.wait_ge(s_sc, 16 * G * NG)

        with Phase("e3a") as ph:
            NI = NCH // LANES
            two = range(LANES)
            idx = [ph.sb(f"idx{s}", [P, K], I32) for s in two]
            got = [ph.sb(f"got{s}", [P, K, HW]) for s in two]
            sc = [ph.sb(f"sc{s}", [P, K]) for s in two]
            s_idx = [ph.sem(f"idx{s}") for s in two]
            s_g = [ph.sem(f"g{s}") for s in two]
            s_st = [ph.sem(f"st{s}") for s in two]
            V = [ph.steps(f"V{s}", ["sc"]) for s in two]
            src_c = t["src_pad"].rearrange("(c p k) -> c p k", p=P, k=K)
            lin_c = h_lin.rearrange("(c p k) d -> c p (k d)", p=P, k=K)
            as_c = asrc_lin.rearrange("(c p k) -> c p k", p=P, k=K)
            with nc.Block() as block:
                @block.sync
                def _(e):
                    def body(it):
                        for s in two:
                            wait_count(e, s_g[s], it, 16 * K, 0)
                            e.dma_start(idx[s][:, :], src_c[bass.ds(it * LANES + s, 1)].rearrange("a p k -> (a p) k")).then_inc(s_idx[s], 16)
                    loop(e, NI, body)

                @block.gpsimd
                def _(e):
                    def body(it):
                        for s in two:
                            wait_count(e, s_idx[s], it, 16, 16)
                            wait_count(e, s_st[s], it, 32, 0)
                            for k in range(K):
                                e.indirect_dma_start(got[s][:, k, :], None, h_tab, bass.IndirectOffsetOnAxis(idx[s][:, k:k + 1], axis=0),
                                                     bounds_check=NROW - 1, oob_is_err=False).then_inc(s_g[s], 16)
                    loop(e, NI, body)

                @block.vector
                def _(e):
                    def body(it):
                        for s in two:
                            wait_count(e, s_g[s], it, 16 * K, 16 * K)
                            wait_count(e, s_st[s], it, 32, 0)
                            V[s].give(e.tensor_copy(sc[s][:, :].unsqueeze(2), got[s][:, :, D + 1:D + 2]), "sc")
                    loop(e, NI, body)

                @block.scalar
                def _(e):
                    def body(it):
                        for s in two:
                            c = bass.ds(it * LANES + s, 1)
                            V[s].wait(e, "sc", it)
                            e.dma_start(lin_c[c].rearrange("a p x -> (a p) x"), got[s][:, :, :].rearrange("p k d -> p (k d)")).then_inc(s_st[s], 16)
                            e.dma_start(as_c[c].rearrange("a p k -> (a p) k"), sc[s][:, :]).then_inc(s_st[s], 16)
                    loop(e, NI, body)
                    for s in two:
                        e.wait_ge(s_st[s], 32 * NI)

        with Phase("s3") as ph:
            asr = ph.sb("asr", [P, EC])
            adr = ph.sb("adr", [P, EC])
            keep_b = ph.sb("keep_b", [P, EC], BF16)
            neg_b = ph.sb("neg_b", [P, EC], BF16)
            ad_e = ph.sb("ad_e", [P, EC])
            z = ph.sb("z", [P, EC])
            zl = ph.sb("zl", [P, EC])
            rm = ph.sb("rm", [P, EC + 1])
            prodk = ph.sb("prodk", [P, EC])
            zeros = ph.sb("zeros", [P, EC])
            lastc = ph.sb("lastc", [P, 3])
            row = ph.sb("row", [1, 4, P])
            prev = ph.sb("prev", [P, 2])
            s_ld, s_v, s_a, s_c, s_o = ph.sem("ld"), ph.sem("v"), ph.sem("a"), ph.sem("c"), ph.sem("o")
            pm = lambda ap: ap.rearrange("(p c) -> p c", p=P)
            count = [0]

            def then(e, ins):
                count[0] += 1
                ins.then_inc(s_v, 1)
                e.wait_ge(s_v, count[0])
                return count[0]

            marks = {}
            with nc.Block() as block:
                @block.vector
                def _(e):
                    e.wait_ge(s_ld, 80)
                    then(e, e.memset(zeros[:, :], 0.0))
                    then(e, e.tensor_tensor_scan(prodk[:, :], keep_b[:, :], zeros[:, :], 1.0, ALU.mult, ALU.add))
                    then(e, e.tensor_tensor_scan(ad_e[:, :], keep_b[:, :], adr[:, :], 0.0, ALU.mult, ALU.add))
                    then(e, e.tensor_copy(lastc[:, 0:1], ad_e[:, EC - 1:EC]))
                    marks["last1"] = then(e, e.tensor_copy(lastc[:, 1:2], prodk[:, EC - 1:EC]))
                    e.wait_ge(s_c, 64)
                    then(e, e.memset(row[:, 2, :], 0.0))
                    then(e, e.tensor_tensor_scan(row[:, 2, 1:P], row[:, 1, 0:P - 1], row[:, 0, 0:P - 1], 0.0, ALU.mult, ALU.add))
                    marks["carry1"] = count[0]
                    e.wait_ge(s_c, 80)
                    then(e, e.scalar_tensor_tensor(ad_e[:, :], prodk[:, :], prev[:, 0:1], ad_e[:, :], ALU.mult, ALU.add))
                    then(e, e.tensor_tensor(z[:, :], asr[:, :], ad_e[:, :], ALU.add))
                    then(e, e.scalar_tensor_tensor(zl[:, :], z[:, :], 0.2, z[:, :], ALU.mult, ALU.max))
                    then(e, e.tensor_tensor_scan(rm[:, 1:EC + 1], neg_b[:, :], zl[:, :], NEG, ALU.add, ALU.max))
                    then(e, e.tensor_copy(lastc[:, 0:1], rm[:, EC:EC + 1]))
                    then(e, e.tensor_scalar(lastc[:, 1:2], prodk[:, EC - 1:EC], -NEG, NEG, ALU.mult, ALU.add))
                    marks["last2"] = count[0]
                    e.wait_ge(s_c, 144)
                    then(e, e.memset(row[:, 2, :], NEG))
                    then(e, e.tensor_tensor_scan(row[:, 2, 1:P], row[:, 1, 0:P - 1], row[:, 0, 0:P - 1], NEG, ALU.add, ALU.max))
                    marks["carry2"] = count[0]
                    e.wait_ge(s_c, 160)
                    then(e, e.tensor_tensor_scan(rm[:, 1:EC + 1], neg_b[:, :], zl[:, :], prev[:, 1:2], ALU.add, ALU.max))
                    then(e, e.tensor_copy(rm[:, 0:1], prev[:, 1:2]))
                    then(e, e.tensor_tensor(z[:, :], zl[:, :], rm[:, 1:EC + 1], ALU.subtract))
                    then(e, e.tensor_tensor(ad_e[:, :], rm[:, 0:EC], rm[:, 1:EC + 1], ALU.subtract))
                    then(e, e.tensor_scalar(ad_e[:, :], ad_e[:, :], 0.0, None, ALU.min))
                    marks["exps"] = count[0]
                    e.wait_ge(s_a, 2)
                    then(e, e.tensor_tensor(ad_e[:, :], ad_e[:, :], keep_b[:, :], ALU.mult))
                    marks["decay"] = count[0]

                @block.scalar
                def _(e):
                    e.wait_ge(s_v, marks["exps"])
                    e.activation(z[:, :], z[:, :], ACT.Exp).then_inc(s_a, 1)
                    e.activation(ad_e[:, :], ad_e[:, :], ACT.Exp).then_inc(s_a, 1)

                @block.sync
                def _(e):
                    e.dma_start(asr[:, :], pm(asrc_lin)).then_inc(s_ld, 16)
                    e.dma_start(adr[:, :], adst_lin.rearrange("(p c) d -> p (c d)", p=P)).then_inc(s_ld, 16)
                    e.dma_start(keep_b[:, :], pm(keep_row)).then_inc(s_ld, 16)
                    e.dma_start(neg_b[:, :], pm(neg_row)).then_inc(s_ld, 16)
                    e.dma_start(prev[:, :], t["two_cols"]).then_inc(s_ld, 16) if "two_cols" in t else e.dma_start(
                        prev[:, :], adst_lin[0:2 * P, :].rearrange("(p c) d -> p (c d)", p=P)).then_inc(s_ld, 16)

                    def to_row(col, r, d):
                        e.dma_start(carry_dram[d, :].rearrange("(p a) -> p a", a=1), lastc[:, col:col + 1]).then_inc(s_c, 16)

                    def round_trip(mark_last, mark_carry, base, d, col):
                        e.wait_ge(s_v, marks[mark_last])
                        to_row(0, 0, d)
                        to_row(1, 1, d + 1)
                        e.wait_ge(s_c, base + 32)
                        e.dma_start(row[:, 0, :], carry_dram[d:d + 1, :]).then_inc(s_c, 16)
                        e.dma_start(row[:, 1, :], carry_dram[d + 1:d + 2, :]).then_inc(s_c, 16)
                        e.wait_ge(s_v, marks[mark_carry])
                        e.wait_ge(s_c, base + 64)
                        e.dma_start(carry_dram[d + 2:d + 3, :], row[:, 2, :]).then_inc(s_o, 16)
                        e.wait_ge(s_o, 16 if d == 0 else 32)
                        e.dma_start(prev[:, col:col + 1], carry_dram[d + 2, :].rearrange("(p a) -> p a", a=1)).then_inc(s_c, 16)

                    round_trip("last1", "carry1", 0, 0, 0)
                    round_trip("last2", "carry2", 80, 3, 1)
                    e.wait_ge(s_v, marks["decay"])
                    e.dma_start(pm(weight_lin), z[:, :]).then_inc(s_o, 16)
                    e.dma_start(pm(decay_row), ad_e[:, :]).then_inc(s_o, 16)
                    e.dma_start(rmax_lin.rearrange("(p c) d -> p (c d)", p=P), rm[:, 1:EC + 1]).then_inc(s_o, 16)
                    e.wait_ge(s_o, 80)

        edge_pass("e3", h_lin, DN, ACT.Copy, decay_row, F32, ALU.mult, ALU.add, scan_out3, gather=False)

        with Phase("n7") as ph:
            ends = ph.sb("ends", [P, G], I32)
            agg = ph.sb("agg", [P, G, DN])
            mx = ph.sb("mx", [P, G, 1])
            zs, z2, m2, em, es, fl = (ph.sb(n, [P, G]) for n in ("zs", "z2", "m2", "em", "es", "fl"))
            y = ph.sb("y", [P, G, D])
            d = ph.sb("d", [P, G, D])
            sq = ph.sb("sq", [P, G, D])
            ob = ph.sb("ob", [P, G, D])
            s1, s2 = ph.sb("s1", [P, G]), ph.sb("s2", [P, G])
            V = ph.steps("V", ["ends", "fl", "zsum", "zleaky", "mflag", "mneg", "mmax", "dm", "ds", "ef", "scale", "den", "hs", "num",
                               "rden", "out", "bias", "y"] + LN)
            A = ph.steps("A", ["em", "es", "tanh", "ln_std"])
            s_g, s_o = ph.sem("g"), ph.sem("o")
            bc = lambda ap, n: ap.unsqueeze(2).to_broadcast([P, G, n])
            with nc.Block() as block:
                @block.gpsimd
                def _(e):
                    def body(it):
                        V.wait(e, "ends", it)
                        for g in range(G):
                            off = bass.IndirectOffsetOnAxis(ends[:, g:g + 1], axis=0)
                            e.indirect_dma_start(agg[:, g, :], None, scan_out3, off, bounds_check=EP - 1, oob_is_err=False).then_inc(s_g, 16)
                            off = bass.IndirectOffsetOnAxis(ends[:, g:g + 1], axis=0)
                            e.indirect_dma_start(mx[:, g, :], None, rmax_lin, off, bounds_check=EP - 1, oob_is_err=False).then_inc(s_g, 16)
                    loop(e, NG, body)

                @block.vector
                def _(e):
                    def body(it):
                        at = bass.ds(it * G, G)

                        def op(ins, name):
                            V.give(ins, name)
                            V.wait(e, name, it)
                        wait_count(e, s_g, it, 32 * G, 0)
                        op(e.tensor_scalar(ends[:, :], end_idx[:, at], 1.0, None, ALU.mult), "ends")
                        op(e.tensor_scalar(fl[:, :], flag[:, at], 1.0, None, ALU.mult), "fl")
                        op(e.tensor_tensor(zs[:, :], asrc[:, at], adst[:, at], ALU.add), "zsum")
                        op(e.scalar_tensor_tensor(z2[:, :], zs[:, :], 0.2, zs[:, :], ALU.mult, ALU.max), "zleaky")
                        wait_count(e, s_g, it, 32 * G, 32 * G)
                        op(e.tensor_tensor(m2[:, :], mx[:, :, 0], fl[:, :], ALU.mult), "mflag")
                        op(e.tensor_scalar(zs[:, :], fl[:, :], -NEG, NEG, ALU.mult, ALU.add), "mneg")
                        op(e.tensor_tensor(m2[:, :], m2[:, :], zs[:, :], ALU.add), "mmax")
                        op(e.tensor_tensor(zs[:, :], m2[:, :], z2[:, :], ALU.max), "dm")
                        op(e.tensor_tensor(m2[:, :], m2[:, :], zs[:, :], ALU.subtract), "ds")
                        op(e.tensor_tensor(z2[:, :], z2[:, :], zs[:, :], ALU.subtract), "ef")
                        A.wait(e, "es", it)
                        op(e.tensor_tensor(em[:, :], em[:, :], fl[:, :], ALU.mult), "scale")
                        op(e.tensor_tensor(agg[:, :, :], agg[:, :, :], bc(em[:, :], DN), ALU.mult), "den")
                        op(e.tensor_tensor(d[:, :, :], R[:, at, :], bc(es[:, :], D), ALU.mult), "hs")
                        op(e.tensor_tensor(d[:, :, :], agg[:, :, 0:D], d[:, :, :], ALU.add), "num")
                        op(e.scalar_tensor_tensor(es[:, :], agg[:, :, D], 1e-16, es[:, :], ALU.add, ALU.add), "rden")
                        op(e.reciprocal(es[:, :], es[:, :]), "out")
                        op(e.tensor_tensor(d[:, :, :], d[:, :, :], bc(es[:, :], D), ALU.mult), "bias")
                        op(e.tensor_tensor(y[:, :, :], d[:, :, :], rows["bias"][:, :].unsqueeze(1).to_broadcast([P, G, D]), ALU.add), "y")
                        A.wait(e, "tanh", it)
                        wait_count(e, s_o, it, 16, 0)
                        e.tensor_tensor(sq[:, :, :], ob[:, :, :], X[:, at, :], ALU.add).then_inc(s_y, 1)
                        wait_count(e, s_y, it, 1, 1)
                        dve_layernorm(e, V, it, sq[:, :, :], d[:, :, :], y[:, :, :], s1, s2, sq[:, :, :], "y", A)
                    s_y = ph.sem("y")
                    loop(e, NG, body)

                @block.scalar
                def _(e):
                    def body(it):
                        V.wait(e, "ef", it)
                        A.give(e.activation(em[:, :], m2[:, :], ACT.Exp), "em")
                        A.give(e.activation(es[:, :], z2[:, :], ACT.Exp), "es")
                        V.wait(e, "y", it)
                        A.give(e.activation(ob[:, :, :], y[:, :, :], ACT.Tanh), "tanh")
                        act_std(e, A, V, it, s2)
                        V.wait(e, "ln_out", it)
                        e.dma_start(t["out"][bass.ds(it * (G * P), G * P), :].rearrange("(g p) d -> p g d", p=P), sq[:, :, :]).then_inc(s_o, 16)
                    loop(e, NG, body)
                    e.wait_ge(s_o, 16 * NG)


_WEIGHTS = ["L0_gnn_qW", "L0_gnn_kW", "L0_gnn_vW", "L1_gnn_We", "L1_gnn_be", "L1_gnn_W1", "L1_gnn_b1", "L1_gnn_W2", "L1_gnn_b2",
            "L1_gnn_gamma", "L1_gnn_beta", "L2_gnn_W1_msg", "L2_gnn_W1_edge", "L2_gnn_W1_root", "L2_gnn_b1", "L2_gnn_W2_msg",
            "L2_gnn_W2_edge", "L2_gnn_W2_root", "L2_gnn_b2", "L3_gnn_W", "L3_gnn_att_src", "L3_gnn_att_dst", "L3_gnn_bias"]


def kernel(**inputs):
    import concourse.bacc as bacc
    from concourse.bass_utils import run_bass_kernel_spmd

    x, src, dst, attr = (np.asarray(inputs[n]) for n in ("x", "src", "dst", "edge_attr_32"))
    n_nodes, D = x.shape
    n_edges, DE = attr.shape
    NT, NCH = padded_sizes(n_nodes, n_edges)
    n_rows, n_padded = NT * P, NCH * CH
    x_pad = np.zeros((n_rows, D), x.dtype)
    x_pad[:n_nodes] = x
    src_pad = np.full(n_padded, n_nodes, src.dtype)
    src_pad[:n_edges] = src
    dst_pad = np.full(n_padded, n_nodes, dst.dtype)
    dst_pad[:n_edges] = dst
    dst_prev = np.full(n_padded, -1, dst.dtype)
    dst_prev[1:] = dst_pad[:-1]
    attr_T = np.zeros((DE + 1, n_padded), attr.dtype)
    attr_T[:DE, :n_edges] = attr.T
    attr_T[DE] = 1
    arrays = {"x": x_pad, "src_pad": src_pad, "dst_pad": dst_pad, "dst_prev": dst_prev, "attr_T": attr_T}
    for n in _WEIGHTS:
        arrays[n] = np.ascontiguousarray(inputs[n])

    nc = bacc.Bacc("TRN2", target_bir_lowering=False, num_devices=1)
    t = {n: nc.dram_tensor(f"in_{n}", a.shape, mybir.dt.from_np(a.dtype), kind="ExternalInput").ap() for n, a in arrays.items()}
    t["out"] = nc.dram_tensor("out_nodes", (n_rows, D), F32, kind="ExternalOutput").ap()
    build(nc, t, n_nodes, n_edges, D, DE)
    r = run_bass_kernel_spmd(nc, [{f"in_{n}": a for n, a in arrays.items()}], core_ids=[0])
    return r.results[0]["out_nodes"][:n_nodes]
```

```python
from contextlib import ExitStack

import numpy as np

import concourse.bass as bass
from concourse import mybir

F32 = mybir.dt.float32
BF16 = mybir.dt.bfloat16
I32 = mybir.dt.int32
ALU = mybir.AluOpType
ACT = mybir.ActivationFunctionType
AX_X = mybir.AxisListType.X

P = 128
K = 4
U = 4
CH = P * K
G = 7
HEADS = 4
LANES = 2
NEG = -2.9e38
EPS = 1e-5


def padded_sizes(n_nodes, n_edges):
    n_tiles = -(-(n_nodes + 1) // (P * G)) * G
    n_chunks = -(-n_edges // (CH * U)) * U
    return n_tiles, n_chunks


PASSED = {}


def loop(eng, n, body, last_apart=False):
    body(0)
    end = n - 1 if last_apart else n
    if end > 1:
        with eng.Fori(1, end) as it:
            body(it)
    if last_apart and n > 1:
        body(n - 1)


class Steps:

    def __init__(self, sem, names):
        self.sem, self.names = sem, list(names)

    def give(self, instruction, name):
        assert name in self.names
        instruction.then_inc(self.sem, 1)

    def wait(self, eng, name, it, back=0):
        n, at = len(self.names), self.names.index(name) + 1
        wait_count(eng, self.sem, it, n, at - back * n)


def wait_count(eng, sem, it, per, plus):
    if isinstance(it, int):
        if it * per + plus > 0:
            eng.wait_ge(sem, it * per + plus)
    else:
        eng.wait_ge(sem, it * per + plus)
        if id(eng) in PASSED:
            eng.sem_inc(PASSED[id(eng)], 1)


def behind(u, lag):
    return (u - lag) % U, (U - 1 - u + lag) // U


def started(it, u, lag):
    return not isinstance(it, int) or it * U + u >= lag


def wait_stored(eng, sem, it, back):
    wait_count(eng, sem, it, 16, -16 * back)


def build(nc, t, n_nodes, n_edges, D, DE):
    NT, NCH = padded_sizes(n_nodes, n_edges)
    NG = NT // G
    NROW = NT * P
    EP = NCH * CH
    EC = EP // P
    DH = D // HEADS
    PAY = D + HEADS
    TROW = NROW + P
    NTAB = LANES * K
    HW = D + 2
    DN = D + 1
    NQ = 2 * NT
    NQB = NQ // G
    assert TROW % P == 0 and D % HEADS == 0 and NT <= P and CH == 512

    def scratch(name, shape, dt=F32):
        return nc.dram_tensor(name, shape, dt, kind="Internal").ap()

    q_tab = scratch("q_tab", (NROW, D))
    kv_tab = scratch("kv_tab", (NROW, 2 * D))
    sum_tab = [scratch(f"sum_tab{j}", (TROW, PAY)) for j in range(NTAB)]
    x_tab = scratch("x_tab", (NROW, D))
    h_tab = scratch("h_tab", (NROW, HW))
    keep_row = scratch("keep_row", (EP,), BF16)
    neg_row = scratch("neg_row", (EP,), BF16)
    decay_row = scratch("decay_row", (EP,))
    weight_lin = scratch("weight_lin", (EP,))
    asrc_lin = scratch("asrc_lin", (EP,))
    adst_lin = scratch("adst_lin", (EP, 1))
    rmax_lin = scratch("rmax_lin", (EP, 1))
    carry_dram = scratch("carry_dram", (8, P))
    h_lin = scratch("h_lin", (EP, HW))
    scan_out = scratch("scan_out", (EP, D))
    scan_out3 = scratch("scan_out3", (EP, DN))

    def bcast_row(ap1d, parts, n):
        return ap1d.rearrange("(a n) -> a n", a=1).to_broadcast([parts, n])

    with ExitStack() as top:
        for eng, name in ((nc.sync, "passed_sp"), (nc.gpsimd, "passed_pool")):
            PASSED[id(eng)] = top.enter_context(nc.semaphore(name))

        def keepb(name, shape, dt=F32):
            return top.enter_context(nc.sbuf_tensor(name, shape, dt))

        X = keepb("X", [P, NT, D])
        R = keepb("R", [P, NT, D])
        ident = keepb("ident", [P, P])
        tri = keepb("tri", [P, P])
        ones_f = keepb("ones_f", [1, P])
        ones_b = keepb("ones_b", [1, P], BF16)
        eps_col = keepb("eps_col", [P, 1])
        dump_col = keepb("dump_col", [P, 1])
        node_q = keepb("node_q", [P, NQ])
        end_idx = keepb("end_idx", [P, NT], I32)
        start_idx = keepb("start_idx", [P, NT], I32)
        flag = keepb("flag", [P, NT])
        src_cols = keepb("src_cols", [P, NCH * K + 2 * K], I32)
        asrc = keepb("asrc", [P, NT])
        adst = keepb("adst", [P, NT])
        w96 = {n: keepb("w_" + n, [D, D]) for n in
               ("qW", "kW", "vW", "W1", "W2", "W1_msg", "W1_root", "W2_msg", "W2_root", "W")}
        we = {n: keepb("we_" + n, [DE + 1, D]) for n in ("We", "W1_edge", "W2_edge")}
        cols = {n: keepb("c_" + n, [D, 1]) for n in ("b1", "b2", "gamma", "beta")}
        rows = {n: keepb("r_" + n, [P, D]) for n in ("l2b1", "l2b2", "att_src", "att_dst", "bias")}

        edge_sems = {}

        class Phase:

            def __init__(self, name, edge=False):
                self.name, self.edge = name, edge

            def __enter__(self):
                self.ctx = ExitStack()
                self.ctx.__enter__()
                return self

            def __exit__(self, *a):
                if self.edge:
                    for s in edge_sems.values():
                        nc.gpsimd.sem_clear(s)
                return self.ctx.__exit__(*a)

            def sb(self, n, shape, dt=F32):
                return self.ctx.enter_context(nc.sbuf_tensor(f"{self.name}_{n}", shape, dt))

            def ps(self, n, shape):
                return self.ctx.enter_context(nc.psum_tensor(f"{self.name}_{n}", shape, F32))

            def sem(self, n):
                if self.edge and not n.startswith("g"):
                    if n not in edge_sems:
                        edge_sems[n] = top.enter_context(nc.semaphore(f"edge_{n}"))
                    return edge_sems[n]
                return self.ctx.enter_context(nc.semaphore(f"{self.name}_{n}"))

            def steps(self, n, names):
                return Steps(self.sem(n), names)

            def block(self):
                return self.ctx.enter_context(nc.Block())

        with Phase("const") as ph:
            s_w, s_m, s_p, s_v = ph.sem("w"), ph.sem("m"), ph.sem("p"), ph.sem("v")
            qi = ph.sb("qi", [P, NQ], I32)
            di = ph.sb("di", [P, 1], I32)
            with nc.Block() as block:
                loads = [(X[:, :, :], t["x"].rearrange("(t p) d -> p t d", p=P)),
                         (src_cols[:, 0:NCH * K], t["src_cols"])]
                for n, key in (("qW", "L0_gnn_qW"), ("kW", "L0_gnn_kW"), ("vW", "L0_gnn_vW"), ("W1", "L1_gnn_W1"),
                               ("W2", "L1_gnn_W2"), ("W1_msg", "L2_gnn_W1_msg"), ("W1_root", "L2_gnn_W1_root"),
                               ("W2_msg", "L2_gnn_W2_msg"), ("W2_root", "L2_gnn_W2_root"), ("W", "L3_gnn_W")):
                    loads.append((w96[n][:, :], t[key]))
                for n, key in (("We", "L1_gnn_We"), ("W1_edge", "L2_gnn_W1_edge"), ("W2_edge", "L2_gnn_W2_edge")):
                    loads.append((we[n][0:DE, :], t[key]))
                loads.append((we["We"][DE:DE + 1, :], t["L1_gnn_be"].rearrange("(a n) -> a n", a=1)))
                for n, key in (("b1", "L1_gnn_b1"), ("b2", "L1_gnn_b2"), ("gamma", "L1_gnn_gamma"), ("beta", "L1_gnn_beta")):
                    loads.append((cols[n][:, :], t[key].rearrange("(n a) -> n a", a=1)))
                for n, key in (("l2b1", "L2_gnn_b1"), ("l2b2", "L2_gnn_b2"), ("att_src", "L3_gnn_att_src"),
                               ("att_dst", "L3_gnn_att_dst"), ("bias", "L3_gnn_bias")):
                    loads.append((rows[n][:, :], bcast_row(t[key], P, D)))

                @block.sync
                def _(e):
                    for dst, src in loads:
                        e.dma_start(dst, src).then_inc(s_w, 16)
                    e.wait_ge(s_w, 16 * len(loads))

                @block.gpsimd
                def _(e):
                    e.memset(ident[:, :], 0.0).then_inc(s_p, 1)
                    e.memset(tri[:, :], 1.0).then_inc(s_p, 1)
                    e.iota(qi[:, :], pattern=[[-1, 2], [P, NT]], base=0, channel_multiplier=1).then_inc(s_p, 1)
                    e.iota(di[:, :], pattern=[[0, 1]], base=NROW, channel_multiplier=1).then_inc(s_p, 1)
                    e.wait_ge(s_p, 4)
                    e.affine_select(out=ident[:, :], in_=ident[:, :], compare_op=ALU.not_equal, fill=1.0, base=0,
                                    pattern=[[-1, P]], channel_multiplier=1).then_inc(s_p, 1)
                    e.affine_select(out=tri[:, :], in_=tri[:, :], compare_op=ALU.is_gt, fill=0.0, base=0,
                                    pattern=[[-1, P]], channel_multiplier=1).then_inc(s_p, 1)
                    e.wait_ge(s_p, 6)

                @block.vector
                def _(e):
                    e.memset(we["W1_edge"][DE:DE + 1, :], 0.0)
                    e.memset(we["W2_edge"][DE:DE + 1, :], 0.0)
                    e.memset(src_cols[:, NCH * K:], 0)
                    e.memset(ones_f[:, :], 1.0)
                    e.memset(ones_b[:, :], 1.0)
                    e.memset(eps_col[:, :], EPS)
                    e.wait_ge(s_p, 4)
                    e.tensor_copy(node_q[:, :], qi[:, :]).then_inc(s_v, 1)
                    e.tensor_copy(dump_col[:, :], di[:, :]).then_inc(s_v, 1)
                    e.wait_ge(s_v, 2)

        with Phase("find") as ph:
            dst_rows = t["dst_pad"].rearrange("(r c) -> r c", c=CH)
            first_i = ph.sb("first_i", [1, NCH], I32)
            first_f = ph.sb("first_f", [1, NCH])
            firsts = ph.sb("firsts", [P, NCH])
            junk = ph.sb("junk", [P, NCH])
            rows_le = ph.sb("rows_le", [P, NQ])
            row_f = ph.sb("row_f", [P, NQ])
            row_i = ph.sb("row_i", [P, G], I32)
            got_i = ph.sb("got_i", [P, G, CH], I32)
            got_f = ph.sb("got_f", [P, G, CH])
            junk2 = ph.sb("junk2", [P, G, CH])
            in_row = ph.sb("in_row", [P, NQ])
            upto = ph.sb("upto", [P, NQ])
            tmp = ph.sb("tmp", [P, NT])
            tmp2 = ph.sb("tmp2", [P, NT])
            dst_i = ph.sb("dst_i", [P, EC], I32)
            prev_i = ph.sb("prev_i", [P, EC], I32)
            keep_b = ph.sb("keep_b", [P, EC], BF16)
            neg_b = ph.sb("neg_b", [P, EC], BF16)
            firsts_ps = ph.ps("firsts_ps", [P, 512])
            s_ld, s_g, s_st = ph.sem("ld"), ph.sem("g"), ph.sem("st")
            s_pre, s_pe = ph.sem("pre"), ph.sem("pe")
            vec = ph.steps("vec", ["rowidx"])
            assert NCH <= 512
            with nc.Block() as block:
                @block.sync
                def _(e):
                    with nc.allow_non_contiguous_dma(reason="one element of each row"):
                        e.dma_start(first_i[:, :], t["dst_pad"].rearrange("(a r c) -> a r c", a=1, c=CH)[:, :, 0:1]
                                    .rearrange("a r c -> a (r c)"), allow_slow_non_contiguous=True).then_inc(s_ld, 16)
                    e.dma_start(dst_i[:, :], t["dst_pad"].rearrange("(p c) -> p c", p=P)).then_inc(s_ld, 16)
                    e.dma_start(prev_i[:, :], t["dst_prev"].rearrange("(p c) -> p c", p=P)).then_inc(s_ld, 16)
                    e.wait_ge(s_pre, 2 + NQ + 3)
                    e.dma_start(keep_row.rearrange("(p c) -> p c", p=P), keep_b[:, :]).then_inc(s_st, 16)
                    e.dma_start(neg_row.rearrange("(p c) -> p c", p=P), neg_b[:, :]).then_inc(s_st, 16)
                    e.wait_ge(s_st, 32)

                @block.tensor
                def _(e):
                    e.wait_ge(s_pre, 1)
                    e.matmul(firsts_ps[:, 0:NCH], ones_f[:, :], first_f[:, :], start=True, stop=True).then_inc(s_pe, 1)

                @block.gpsimd
                def _(e):
                    def body(it):
                        vec.wait(e, "rowidx", it)
                        for g in range(G):
                            e.indirect_dma_start(got_i[:, g, :], None, dst_rows,
                                                 bass.IndirectOffsetOnAxis(row_i[:, g:g + 1], axis=0),
                                                 bounds_check=NCH - 1, oob_is_err=False).then_inc(s_g, 16)
                    loop(e, NQB, body)

                @block.vector
                def _(e):
                    e.wait_ge(s_ld, 48)
                    e.tensor_copy(first_f[:, :], first_i[:, :]).then_inc(s_pre, 1)
                    e.wait_ge(s_pe, 1)
                    e.tensor_copy(firsts[:, :], firsts_ps[:, 0:NCH]).then_inc(s_pre, 1)
                    e.wait_ge(s_pre, 2)
                    for q in range(NQ):
                        e.wait_ge(s_pre, 2 + q)
                        e.tensor_scalar(junk[:, :], firsts[:, :], node_q[:, q:q + 1], 0.0, ALU.is_le, ALU.add,
                                        accum_out=rows_le[:, q:q + 1]).then_inc(s_pre, 1)
                    e.tensor_tensor(keep_b[:, :], dst_i[:, :], prev_i[:, :], ALU.is_equal).then_inc(s_pre, 1)
                    e.wait_ge(s_pre, 2 + NQ + 1)
                    e.tensor_scalar(neg_b[:, :], keep_b[:, :], -NEG, NEG, ALU.mult, ALU.add).then_inc(s_pre, 1)
                    e.tensor_scalar(row_f[:, :], rows_le[:, :], -1.0, 0.0, ALU.add, ALU.max).then_inc(s_pre, 1)
                    e.wait_ge(s_pre, 2 + NQ + 3)

                    def body(it):
                        q0 = it * G
                        vec.give(e.tensor_scalar(row_i[:, :], row_f[:, bass.ds(q0, G)], 1.0, None, ALU.mult), "rowidx")
                        wait_count(e, s_g, it, 16 * G, 16 * G)
                        e.tensor_copy(got_f[:, :, :], got_i[:, :, :]).then_inc(s_chain, 1)
                        wait_count(e, s_chain, it, G + 1, 1)
                        for g in range(G):
                            e.tensor_scalar(junk2[:, g, :], got_f[:, g, :], node_q[:, bass.ds(q0 + g, 1)], 0.0, ALU.is_le,
                                            ALU.add, accum_out=in_row[:, bass.ds(q0 + g, 1)]).then_inc(s_chain, 1)
                        wait_count(e, s_chain, it, G + 1, G + 1)
                    s_chain = ph.sem("chain")
                    loop(e, NQB, body)
                    s_f = ph.sem("fin")
                    e.scalar_tensor_tensor(upto[:, :], row_f[:, :], float(CH), in_row[:, :], ALU.mult, ALU.add).then_inc(s_f, 1)
                    e.wait_ge(s_f, 1)
                    e.tensor_tensor(flag[:, :], upto[:, 0:NT], upto[:, NT:NQ], ALU.is_gt).then_inc(s_f, 1)
                    e.tensor_scalar(end_idx[:, :], upto[:, 0:NT], -1.0, 0.0, ALU.add, ALU.max).then_inc(s_f, 1)
                    e.wait_ge(s_f, 2)
                    e.tensor_scalar(tmp[:, :], flag[:, :], -2.0 * EP, 2.0 * EP, ALU.mult, ALU.add).then_inc(s_f, 1)
                    e.wait_ge(s_f, 4)
                    e.tensor_tensor(start_idx[:, :], tmp[:, :], upto[:, NT:NQ], ALU.add).then_inc(s_f, 1)
                    e.wait_ge(s_f, 5)

        def dve_layernorm(e, V, it, y, d, sq, s1, s2, out, y_step, act):
            V.wait(e, y_step, it)
            V.give(e.tensor_reduce(s1[:, :], y, AX_X, ALU.add), "ln_sum")
            V.wait(e, "ln_sum", it)
            V.give(e.tensor_scalar(s1[:, :], s1[:, :], 1.0 / D, None, ALU.mult), "ln_mean")
            V.wait(e, "ln_mean", it)
            V.give(e.tensor_tensor(d, y, s1[:, :].unsqueeze(2).to_broadcast([P, G, D]), ALU.subtract), "ln_cent")
            V.wait(e, "ln_cent", it)
            V.give(e.tensor_tensor(sq, d, d, ALU.mult), "ln_sq")
            V.wait(e, "ln_sq", it)
            V.give(e.tensor_reduce(s2[:, :], sq, AX_X, ALU.add), "ln_var")
            act.wait(e, "ln_std", it)
            V.give(e.reciprocal(s1[:, :], s2[:, :]), "ln_rstd")
            V.wait(e, "ln_rstd", it)
            V.give(e.tensor_tensor(out, d, s1[:, :].unsqueeze(2).to_broadcast([P, G, D]), ALU.mult), "ln_out")
            V.wait(e, "ln_out", it)

        LN = ["ln_sum", "ln_mean", "ln_cent", "ln_sq", "ln_var", "ln_rstd", "ln_out"]

        def act_std(e, A, V, it, s2):
            V.wait(e, "ln_var", it)
            A.give(e.activation(s2[:, :], s2[:, :], ACT.Sqrt, bias=eps_col[:, 0:1], scale=1.0 / D), "ln_std")

        def pe_transpose_group(e, T, TP, src, it, name):
            for g in range(G):
                ins = e.transpose(TP[0:D, g * P:(g + 1) * P], src[:, g, :], ident[:, :])
            T.give(ins, name)

        with Phase("n1") as ph:
            xg = ph.sb("xg", [P, G, D])
            xT = ph.sb("xT", [D, G * P])
            tab = [ph.sb(f"tab{i}", [P, G, D]) for i in range(3)]
            TP = ph.ps("TP", [P, 1024])
            O = [ph.ps(f"O{i}", [P, 2, 512]) for i in range(3)]
            V = ph.steps("V", ["xg"])
            T = ph.steps("T", ["tr", "mm0", "mm1", "mm2"])
            A = ph.steps("A", ["xT", "o0", "o1", "o2"])
            s_o = ph.sem("o")
            ph_zero = ph.sb("zero", [P, TROW // P * PAY])
            s_z, s_zd = ph.sem("z"), ph.sem("zd")
            with nc.Block() as block:
                @block.vector
                def _(e):
                    def body(it):
                        T.wait(e, "tr", it, 1)
                        V.give(e.tensor_scalar(xg[:, :, :], X[:, bass.ds(it * G, G), :], 1.0, None, ALU.mult), "xg")
                    loop(e, NG, body)

                @block.tensor
                def _(e):
                    def body(it):
                        V.wait(e, "xg", it)
                        A.wait(e, "xT", it, 1)
                        pe_transpose_group(e, T, TP, xg, it, "tr")
                        A.wait(e, "xT", it)
                        for i, n in enumerate(("qW", "kW", "vW")):
                            for g in range(G):
                                ins = e.matmul(O[i][:, g // 4, (g % 4) * P:(g % 4) * P + D], xT[:, g * P:(g + 1) * P],
                                               w96[n][:, :], start=True, stop=True)
                            T.give(ins, f"mm{i}")
                    loop(e, NG, body)

                @block.scalar
                def _(e):
                    def body(it):
                        T.wait(e, "tr", it)
                        A.give(e.activation(xT[:, :], TP[0:D, 0:G * P], ACT.Copy), "xT")
                        for i in range(3):
                            T.wait(e, f"mm{i}", it)
                            wait_count(e, s_o, it, 48, 0)
                            e.activation(tab[i][:, 0:4, :], O[i][:, 0, :].rearrange("p (g c) -> p g c", c=P)[:, :, 0:D], ACT.Copy)
                            A.give(e.activation(tab[i][:, 4:G, :], O[i][:, 1, :].rearrange("p (g c) -> p g c", c=P)[:, 0:G - 4, 0:D], ACT.Copy), f"o{i}")
                    loop(e, NG, body)

                @block.sync
                def _(e):
                    def body(it):
                        rows_at = bass.ds(it * (G * P), G * P)
                        for i, dst in enumerate((q_tab[rows_at, :], kv_tab[rows_at, 0:D], kv_tab[rows_at, D:2 * D])):
                            A.wait(e, f"o{i}", it)
                            e.dma_start(dst.rearrange("(g p) d -> p g d", p=P), tab[i][:, :, :]).then_inc(s_o, 16)
                    loop(e, NG, body)
                    e.wait_ge(s_o, 48 * NG)


                @block.gpsimd
                def _(e):
                    e.memset(ph_zero[:, :], 0.0).then_inc(s_z, 1)
                    e.wait_ge(s_z, 1)
                    for j in range(NTAB):
                        e.dma_start(sum_tab[j].rearrange("(p r) d -> p (r d)", p=P), ph_zero[:, :]).then_inc(s_zd, 16)
                    e.dma_start(adst_lin.rearrange("(p r) d -> p (r d)", p=P), ph_zero[:, 0:EC]).then_inc(s_zd, 16)
                    e.wait_ge(s_zd, 16 * (NTAB + 1))

        with Phase("e0") as ph:
            NI = NCH // LANES
            two = range(LANES)
            src_i = [ph.sb(f"src_i{s}", [P, K], I32) for s in two]
            dst_i = [ph.sb(f"dst_i{s}", [P, K], I32) for s in two]
            src_bc = [ph.sb(f"src_bc{s}", [P, CH], I32) for s in two]
            src_bf = [ph.sb(f"src_bf{s}", [P, CH]) for s in two]
            src_f = [ph.sb(f"src_f{s}", [P, K]) for s in two]
            qg = [ph.sb(f"qg{s}", [P, K, D]) for s in two]
            kvg = [ph.sb(f"kvg{s}", [P, K, 2 * D]) for s in two]
            prod = [ph.sb(f"prod{s}", [P, K, D]) for s in two]
            score = [ph.sb(f"score{s}", [P, K, HEADS]) for s in two]
            pay = [ph.sb(f"pay{s}", [P, K, PAY]) for s in two]
            same = [ph.sb(f"same{s}", [P, K, P]) for s in two]
            junk = [ph.sb(f"junk{s}", [P, K, P]) for s in two]
            dup = [ph.sb(f"dup{s}", [P, K]) for s in two]
            away = [ph.sb(f"away{s}", [P, K]) for s in two]
            srow = [ph.sb(f"srow{s}", [P, K], I32) for s in two]
            comb = [ph.sb(f"comb{s}", [P, K, PAY]) for s in two]
            C = [ph.ps(f"C{s}", [P, 512]) for s in two]
            s_ld = [ph.sem(f"ld{s}") for s in two]
            s_g = [ph.sem(f"g{s}") for s in two]
            s_tab = [ph.sem(f"tab{j}") for j in range(NTAB)]
            V = [ph.steps(f"V{s}", ["conv", "srcf", "prod", "red", "clip", "eq", "dup", "away", "f", "mul", "row", "pay"]) for s in two]
            A = [ph.steps(f"A{s}", ["exp", "comb"]) for s in two]
            T = [ph.steps(f"T{s}", ["mm"]) for s in two]
            src_c = t["src_pad"].rearrange("(c p k) -> c p k", p=P, k=K)
            dst_c = t["dst_pad"].rearrange("(c p k) -> c p k", p=P, k=K)
            src_r = t["src_pad"].rearrange("(c e) -> c e", e=CH)
            with nc.Block() as block:
                @block.sync
                def _(e):
                    def body(it):
                        for s in two:
                            c = it * LANES + s
                            V[s].wait(e, "row", it, 1)
                            wait_count(e, s_g[s], it, 32 * K, 0)
                            e.dma_start(src_i[s][:, :], src_c[bass.ds(c, 1)].rearrange("a p k -> (a p) k")).then_inc(s_ld[s], 16)
                            e.dma_start(dst_i[s][:, :], dst_c[bass.ds(c, 1)].rearrange("a p k -> (a p) k")).then_inc(s_ld[s], 16)
                            e.dma_start(src_bc[s][:, :], src_r[bass.ds(c, 1)].to_broadcast([P, CH])).then_inc(s_ld[s], 16)
                    loop(e, NI, body)

                @block.gpsimd
                def _(e):
                    def scatter(s, it):
                        A[s].wait(e, "comb", it)
                        for k in range(K):
                            wait_count(e, s_tab[s * K + k], it, 16, 0)
                            e.indirect_dma_start(sum_tab[s * K + k], bass.IndirectOffsetOnAxis(srow[s][:, k:k + 1], axis=0),
                                                 comb[s][:, k, :], None, bounds_check=TROW - 1, oob_is_err=True,
                                                 compute_op=ALU.add).then_inc(s_tab[s * K + k], 16)

                    def body(it):
                        for s in two:
                            wait_count(e, s_ld[s], it, 48, 48)
                            V[s].wait(e, "pay", it, 1)
                            for k in range(K):
                                e.indirect_dma_start(qg[s][:, k, :], None, q_tab,
                                                     bass.IndirectOffsetOnAxis(src_i[s][:, k:k + 1], axis=0),
                                                     bounds_check=NROW - 1, oob_is_err=False).then_inc(s_g[s], 16)
                                e.indirect_dma_start(kvg[s][:, k, :], None, kv_tab,
                                                     bass.IndirectOffsetOnAxis(dst_i[s][:, k:k + 1], axis=0),
                                                     bounds_check=NROW - 1, oob_is_err=False).then_inc(s_g[s], 16)
                            if s == 0:
                                if not isinstance(it, int):
                                    scatter_prev(it)
                            else:
                                scatter(0, it)

                    def scatter_prev(it):
                        A[1].wait(e, "comb", it, 1)
                        for k in range(K):
                            wait_count(e, s_tab[K + k], it, 16, -16)
                            e.indirect_dma_start(sum_tab[K + k], bass.IndirectOffsetOnAxis(srow[1][:, k:k + 1], axis=0),
                                                 comb[1][:, k, :], None, bounds_check=TROW - 1, oob_is_err=True,
                                                 compute_op=ALU.add).then_inc(s_tab[K + k], 16)
                    loop(e, NI, body)
                    scatter(1, NI - 1)
                    for j in range(NTAB):
                        e.wait_ge(s_tab[j], 16 * NI)

                @block.vector
                def _(e):
                    def body(it):
                        for s in two:
                            W = V[s]
                            wait_count(e, s_ld[s], it, 48, 48)
                            W.give(e.tensor_copy(src_bf[s][:, :], src_bc[s][:, :]), "conv")
                            W.give(e.tensor_copy(src_f[s][:, :], src_i[s][:, :]), "srcf")
                            wait_count(e, s_g[s], it, 32 * K, 32 * K)
                            W.give(e.tensor_tensor(prod[s][:, :, :], qg[s][:, :, :], kvg[s][:, :, 0:D], ALU.mult), "prod")
                            W.wait(e, "prod", it)
                            W.give(e.tensor_reduce(score[s][:, :, :], prod[s][:, :, :].rearrange("p k (h d) -> p k h d", h=HEADS),
                                                   AX_X, ALU.add), "red")
                            W.wait(e, "red", it)
                            W.give(e.tensor_scalar(score[s][:, :, :], score[s][:, :, :], -10.0, 10.0, ALU.max, ALU.min), "clip")
                            T[s].wait(e, "mm", it, 1)
                            for k in range(K):
                                ins = e.tensor_scalar(same[s][:, k, :], src_bf[s][:, k::K], src_f[s][:, k:k + 1], None, ALU.is_equal)
                            W.give(ins, "eq")
                            W.wait(e, "eq", it)
                            for k in range(K):
                                ins = e.scalar_tensor_tensor(junk[s][:, k, :], same[s][:, k, :], 1.0, tri[:, :], ALU.mult, ALU.mult,
                                                             accum_out=dup[s][:, k:k + 1])
                            W.give(ins, "dup")
                            W.give(e.tensor_scalar(away[s][:, :], src_f[s][:, :], -1.0, dump_col[:, 0:1], ALU.mult, ALU.add), "away")
                            W.wait(e, "away", it)
                            W.give(e.tensor_scalar(dup[s][:, :], dup[s][:, :], 1.0, None, ALU.min), "f")
                            W.wait(e, "f", it)
                            W.give(e.tensor_tensor(away[s][:, :], away[s][:, :], dup[s][:, :], ALU.mult), "mul")
                            W.wait(e, "mul", it)
                            for k in range(K):
                                wait_count(e, s_tab[s * K + k], it, 16, 0)
                            W.give(e.tensor_tensor(srow[s][:, :], src_f[s][:, :], away[s][:, :], ALU.add), "row")
                            A[s].wait(e, "exp", it)
                            W.give(e.tensor_tensor(pay[s][:, :, 0:D].rearrange("p k (h d) -> p k h d", h=HEADS),
                                                   kvg[s][:, :, D:2 * D].rearrange("p k (h d) -> p k h d", h=HEADS),
                                                   pay[s][:, :, D:PAY].unsqueeze(3).to_broadcast([P, K, HEADS, DH]), ALU.mult), "pay")
                    loop(e, NI, body)

                @block.scalar
                def _(e):
                    def body(it):
                        for s in two:
                            V[s].wait(e, "clip", it)
                            T[s].wait(e, "mm", it, 1)
                            A[s].give(e.activation(pay[s][:, :, D:PAY], score[s][:, :, :], ACT.Exp), "exp")
                            T[s].wait(e, "mm", it)
                            for k in range(K):
                                wait_count(e, s_tab[s * K + k], it, 16, 0)
                            A[s].give(e.activation(comb[s][:, :, :], C[s][:, 0:K * PAY].rearrange("p (k c) -> p k c", k=K), ACT.Copy), "comb")
                    loop(e, NI, body)

                @block.tensor
                def _(e):
                    def body(it):
                        for s in two:
                            V[s].wait(e, "pay", it)
                            A[s].wait(e, "comb", it, 1)
                            for k in range(K):
                                ins = e.matmul(C[s][:, k * PAY:(k + 1) * PAY], same[s][:, k, :], pay[s][:, k, :], start=True, stop=True)
                            T[s].give(ins, "mm")
                    loop(e, NI, body)

        with Phase("n2") as ph:
            part = [ph.sb(f"part{j}", [P, G, PAY]) for j in range(NTAB)]
            acc = ph.sb("acc", [P, G, PAY])
            den = ph.sb("den", [P, G, HEADS])
            y = ph.sb("y", [P, G, D])
            d = ph.sb("d", [P, G, D])
            sq = ph.sb("sq", [P, G, D])
            s1, s2 = ph.sb("s1", [P, G]), ph.sb("s2", [P, G])
            xo = ph.sb("xo", [P, G, D])
            V = ph.steps("V", [f"add{j}" for j in range(1, NTAB)] + ["den", "rden", "res", "x2", "y"] + LN + ["keep"])
            A = ph.steps("A", ["ln_std"])
            s_ld, s_o = ph.sem("ld"), ph.sem("o")
            with nc.Block() as block:
                @block.sync
                def _(e):
                    def body(it):
                        V.wait(e, f"add{NTAB - 1}", it, 1)
                        for j in range(NTAB):
                            e.dma_start(part[j][:, :, :], sum_tab[j][bass.ds(it * (G * P), G * P), :].rearrange("(g p) d -> p g d", p=P)).then_inc(s_ld, 16)
                    loop(e, NG, body)

                @block.vector
                def _(e):
                    def body(it):
                        wait_count(e, s_ld, it, 16 * NTAB, 16 * NTAB)
                        for j in range(1, NTAB):
                            a = part[0] if j == 1 else acc
                            if j > 1:
                                V.wait(e, f"add{j - 1}", it)
                            V.give(e.tensor_tensor(acc[:, :, :], a[:, :, :], part[j][:, :, :], ALU.add), f"add{j}")
                        V.wait(e, f"add{NTAB - 1}", it)
                        V.give(e.tensor_scalar(den[:, :, :], acc[:, :, D:PAY], 1e-8, None, ALU.add), "den")
                        V.wait(e, "den", it)
                        V.give(e.reciprocal(den[:, :, :], den[:, :, :]), "rden")
                        V.wait(e, "rden", it)
                        V.give(e.tensor_tensor(y[:, :, :].rearrange("p g (h d) -> p g h d", h=HEADS),
                                               acc[:, :, 0:D].rearrange("p g (h d) -> p g h d", h=HEADS),
                                               den[:, :, :].unsqueeze(3).to_broadcast([P, G, HEADS, DH]), ALU.mult), "res")
                        V.wait(e, "res", it)
                        V.give(e.tensor_tensor(y[:, :, :], y[:, :, :], X[:, bass.ds(it * G, G), :], ALU.add), "x2")
                        V.wait(e, "x2", it)
                        V.give(e.tensor_tensor(y[:, :, :], y[:, :, :], X[:, bass.ds(it * G, G), :], ALU.add), "y")
                        wait_count(e, s_o, it, 16, 0)
                        dve_layernorm(e, V, it, y[:, :, :], d[:, :, :], sq[:, :, :], s1, s2, xo[:, :, :], "y", A)
                        V.give(e.tensor_scalar(X[:, bass.ds(it * G, G), :], xo[:, :, :], 1.0, None, ALU.mult), "keep")
                    loop(e, NG, body)

                @block.scalar
                def _(e):
                    def body(it):
                        act_std(e, A, V, it, s2)
                        V.wait(e, "ln_out", it)
                        e.dma_start(x_tab[bass.ds(it * (G * P), G * P), :].rearrange("(g p) d -> p g d", p=P), xo[:, :, :]).then_inc(s_o, 16)
                    loop(e, NG, body)
                    e.wait_ge(s_o, 16 * NG)

        def edge_pass(name, table, width, func, mask_row, mask_dt, op0, op1, out_lin, edge_w=None, gather=True):
            with Phase(name, edge=True) as ph:
                NI = NCH // U

                def turn_back_last(e, part):
                    part(NI, 0)
                row_w = table.shape[1]
                idx = [ph.sb(f"idx{u}", [P, K], I32 if gather else F32) for u in range(U)]
                got = [ph.sb(f"got{u}", [P, K, row_w]) for u in range(U)]
                attr = [ph.sb(f"attr{u}", [DE + 1, CH]) for u in range(U)] if gather else None
                mask = [ph.sb(f"mask{u}", [1, CH], mask_dt) for u in range(U)]
                emsg = [ph.sb(f"emsg{s}", [P, K, width]) for s in range(2)]
                msg = [ph.sb(f"msg{s}", [width, CH]) for s in range(2)]
                run = [ph.sb(f"run{s}", [width, CH]) for s in range(2)]
                out = [ph.sb(f"out{u}", [P, K, width]) for u in range(U)]
                EA = [ph.ps(f"EA{s}", [P, CH]) for s in range(2)]
                M = [ph.ps(f"M{s}", [P, CH]) for s in range(2)]
                Z = [ph.ps(f"Z{s}", [P, CH]) for s in range(2)]
                B = [ph.ps(f"B{s}", [P, CH]) for s in range(2)]
                s_ix = ph.sem("ix")
                s_init = ph.sem("init")
                s_ld = [ph.sem(f"ld{u}") for u in range(U)]
                s_g = [ph.sem(f"g{u}") for u in range(U)]
                s_st = [ph.sem(f"st{u}") for u in range(U)]
                T = [ph.steps(f"T{u}", (["attr"] if gather else []) + ["fwd", "back"]) for u in range(U)]
                A = [ph.steps(f"A{u}", ["msg", "out"]) for u in range(U)]
                V = [ph.steps(f"V{u}", ["add", "scan"]) for u in range(U)]
                NLD = 16 * 2 if gather else 16
                NGT = 16 * K if gather else 32
                lin_c = None if gather else table.rearrange("(c p k) d -> c p (k d)", p=P, k=K)
                wgt_c = weight_lin.rearrange("(c p k) -> c p k", p=P, k=K)
                mask_c = mask_row.rearrange("(c e) -> c e", e=CH)
                out_c = out_lin.rearrange("(c p k) d -> c p (k d)", p=P, k=K)
                bc_lhs = ones_b if mask_dt == BF16 else ones_f
                with nc.Block() as block:
                    @block.sync
                    def _(e):
                        def store(it, u, lag):
                            v, back = behind(u, lag)
                            A[v].wait(e, "out", it, back)
                            e.dma_start(out_c[bass.ds(it * U + (u - lag), 1)].rearrange("a p x -> (a p) x"),
                                        out[v][:, :, :].rearrange("p k d -> p (k d)")).then_inc(s_st[v], 16)

                        def step(it, u):
                            c = it * U + u
                            T[u].wait(e, "fwd", it, 1)
                            e.dma_start(mask[u][:, :], mask_c[bass.ds(c, 1)]).then_inc(s_ld[u], 16)
                            if gather:
                                e.dma_start(attr[u][:, :], t["attr_T"][:, bass.ds(c * CH, CH)]).then_inc(s_ld[u], 16)
                            else:
                                V[u].wait(e, "add", it, 1)
                                e.dma_start(idx[u][:, :], wgt_c[bass.ds(c, 1)].rearrange("a p k -> (a p) k")).then_inc(s_g[u], 16)
                                e.dma_start(got[u][:, :, :].rearrange("p k d -> p (k d)"), lin_c[bass.ds(c, 1)].rearrange("a p x -> (a p) x")).then_inc(s_g[u], 16)
                            if started(it, u, U - 1):
                                store(it, u, U - 1)
                        loop(e, NI, lambda it: [step(it, u) for u in range(U)])
                        for lag in range(U - 2, -1, -1):
                            store(NI - 1, U - 1, lag)
                        for u in range(U):
                            e.wait_ge(s_st[u], 16 * NI)

                    if gather:
                        @block.gpsimd
                        def _(e):
                            def step(it, u):
                                wait_count(e, s_ix, it, U, u + 1)
                                V[u].wait(e, "add", it, 1)
                                for k in range(K):
                                    e.indirect_dma_start(got[u][:, k, :], None, table,
                                                         bass.IndirectOffsetOnAxis(idx[u][:, k:k + 1], axis=0),
                                                         bounds_check=NROW - 1, oob_is_err=False).then_inc(s_g[u], 16)
                            loop(e, NI, lambda it: [step(it, u) for u in range(U)])

                    @block.tensor
                    def _(e):
                        def turn_back(it, u):
                            v, back = behind(u, 1)
                            V[v].wait(e, "scan", it, back)
                            w, back2 = behind(u, 3)
                            A[w].wait(e, "out", it, back2)
                            for k in range(K):
                                ins = e.transpose(B[v % 2][:, k * width:(k + 1) * width], run[v % 2][:, k::K], ident[0:width, 0:width])
                            T[v].give(ins, "back")

                        def attributes(it, u, free):
                            wait_count(e, s_ld[u], it, NLD, NLD)
                            free()
                            for k in range(K):
                                ins = e.matmul(EA[u % 2][:, k * width:(k + 1) * width], attr[u][:, k::K], edge_w[:, :], start=True, stop=True)
                            T[u].give(ins, "attr")

                        def step(it, u):
                            s = u % 2
                            v, back = behind(u, 2)
                            w, back1 = behind(u, 1)
                            if gather:
                                if u + 1 < U:
                                    attributes(it, u + 1, lambda: V[w].wait(e, "add", it, back1))
                                elif not isinstance(it, int) or it + 1 < NI:
                                    attributes(it + 1, 0, lambda: V[w].wait(e, "add", it, back1))
                            else:
                                wait_count(e, s_ld[u], it, NLD, NLD)
                            V[v].wait(e, "scan", it, back)
                            e.matmul(Z[s][0:width, :], bc_lhs[:, 0:width], mask[u][:, :], start=True, stop=True)
                            V[u].wait(e, "add", it)
                            A[v].wait(e, "msg", it, back)
                            for k in range(K):
                                ins = e.transpose(M[s][0:width, k::K], emsg[s][:, k, :], ident[:, :])
                            T[u].give(ins, "fwd")
                            if started(it, u, 1):
                                turn_back(it, u)
                        if gather:
                            attributes(0, 0, lambda: None)
                        loop(e, NI, lambda it: [step(it, u) for u in range(U)], last_apart=True)
                        turn_back_last(e, turn_back)

                    @block.vector
                    def _(e):
                        e.memset(run[1][:, :], 0.0).then_inc(s_init, 1)
                        if gather:
                            for u in range(2):
                                e.tensor_scalar(idx[u][:, :], src_cols[:, u * K:(u + 1) * K], 1.0, None, ALU.mult).then_inc(s_ix, 1)
                        e.wait_ge(s_init, 1)

                        def scan(it, u):
                            v, back = behind(u, 1)
                            w, back2 = behind(u, 2)
                            x, back3 = behind(u, 3)
                            A[v].wait(e, "msg", it, back)
                            T[v].wait(e, "fwd", it, back)
                            V[w].wait(e, "scan", it, back2)
                            T[x].wait(e, "back", it, back3)
                            p, q = v % 2, w % 2
                            V[v].give(e.tensor_tensor_scan(run[p][:, :], Z[p][0:width, :], msg[p][:, :], run[q][:, CH - 1:CH], op0, op1), "scan")

                        def step(it, u):
                            s = u % 2
                            v, back = behind(u, 2)
                            if gather:
                                e.tensor_scalar(idx[(u + 2) % U][:, :], src_cols[:, bass.ds((it * U + u + 2) * K, K)], 1.0, None, ALU.mult).then_inc(s_ix, 1)
                                T[u].wait(e, "attr", it)
                            wait_count(e, s_g[u], it, NGT, NGT)
                            T[v].wait(e, "fwd", it, back)
                            if gather:
                                add = e.tensor_tensor(emsg[s][:, :, :], EA[s][:, 0:K * width].rearrange("p (k d) -> p k d", k=K),
                                                      got[u][:, :, :], ALU.add)
                            else:
                                add = e.tensor_tensor(emsg[s][:, :, :], got[u][:, :, 0:width],
                                                      idx[u][:, :].unsqueeze(2).to_broadcast([P, K, width]), ALU.mult)
                            V[u].give(add, "add")
                            if started(it, u, 1):
                                scan(it, u)
                        loop(e, NI, lambda it: [step(it, u) for u in range(U)])
                        turn_back_last(e, scan)

                    @block.scalar
                    def _(e):
                        def to_out(it, u):
                            v, back = behind(u, 1)
                            T[v].wait(e, "back", it, back)
                            wait_stored(e, s_st[v], it, back)
                            A[v].give(e.activation(out[v][:, :, :], B[v % 2][:, 0:K * width].rearrange("p (k d) -> p k d", k=K), ACT.Copy), "out")

                        def step(it, u):
                            v, back = behind(u, 2)
                            T[u].wait(e, "fwd", it)
                            V[v].wait(e, "scan", it, back)
                            A[u].give(e.activation(msg[u % 2][:, :], M[u % 2][0:width, :], func), "msg")
                            if started(it, u, 1):
                                to_out(it, u)
                        loop(e, NI, lambda it: [step(it, u) for u in range(U)])
                        turn_back_last(e, to_out)

        def pool_gather_ends(e, ends, dst, lin, sem, g_wait, it):
            g_wait(it)
            for g in range(G):
                e.indirect_dma_start(dst[:, g, :], None, lin, bass.IndirectOffsetOnAxis(ends[:, g:g + 1], axis=0),
                                     bounds_check=EP - 1, oob_is_err=False).then_inc(sem, 16)

        edge_pass("e1", x_tab, D, ACT.Relu, keep_row, BF16, ALU.mult, ALU.add, scan_out, edge_w=we["We"])

        with Phase("n3") as ph:
            ends = ph.sb("ends", [P, G], I32)
            agg = ph.sb("agg", [P, G, D])
            hT = ph.sb("hT", [D, G * P])
            rT = ph.sb("rT", [D, G * P])
            HT = ph.sb("HT", [D, NT * P])
            TP = ph.ps("TP", [P, 1024])
            O1 = ph.ps("O1", [P, 1024])
            O2 = ph.ps("O2", [P, 1024])
            V = ph.steps("V", ["ends", "flag", "h"])
            T = ph.steps("T", ["tr", "m1", "m2"])
            A = ph.steps("A", ["hT", "r1", "h2"])
            s_g = ph.sem("g")
            HALF = [(0, 512), (512, G * P)]
            with nc.Block() as block:
                @block.gpsimd
                def _(e):
                    loop(e, NG, lambda it: pool_gather_ends(e, ends, agg, scan_out, s_g, lambda i: (V.wait(e, "ends", i), T.wait(e, "tr", i, 1)), it))

                @block.vector
                def _(e):
                    def body(it):
                        wait_count(e, s_g, it, 16 * G, 0)
                        V.give(e.tensor_scalar(ends[:, :], end_idx[:, bass.ds(it * G, G)], 1.0, None, ALU.mult), "ends")
                        wait_count(e, s_g, it, 16 * G, 16 * G)
                        V.give(e.tensor_tensor(agg[:, :, :], agg[:, :, :], flag[:, bass.ds(it * G, G)].unsqueeze(2).to_broadcast([P, G, D]), ALU.mult), "flag")
                        V.wait(e, "flag", it)
                        V.give(e.tensor_tensor(agg[:, :, :], agg[:, :, :], X[:, bass.ds(it * G, G), :], ALU.add), "h")
                    loop(e, NG, body)

                @block.tensor
                def _(e):
                    def body(it):
                        V.wait(e, "h", it)
                        A.wait(e, "hT", it, 1)
                        pe_transpose_group(e, T, TP, agg, it, "tr")
                        A.wait(e, "hT", it)
                        for a, b in HALF:
                            ins = e.matmul(O1[0:D, a:b], w96["W1"][:, :], hT[:, a:b], start=True, stop=True)
                        T.give(ins, "m1")
                        A.wait(e, "r1", it)
                        for a, b in HALF:
                            ins = e.matmul(O2[0:D, a:b], w96["W2"][:, :], rT[:, a:b], start=True, stop=True)
                        T.give(ins, "m2")
                    loop(e, NG, body)

                @block.scalar
                def _(e):
                    def body(it):
                        T.wait(e, "tr", it)
                        A.give(e.activation(hT[:, :], TP[0:D, 0:G * P], ACT.Copy), "hT")
                        T.wait(e, "m1", it)
                        A.give(e.activation(rT[:, :], O1[0:D, 0:G * P], ACT.Relu, bias=cols["b1"][:, 0:1]), "r1")
                        T.wait(e, "m2", it)
                        A.give(e.activation(HT[:, bass.ds(it * (G * P), G * P)], O2[0:D, 0:G * P], ACT.Identity, bias=cols["b2"][:, 0:1]), "h2")
                    loop(e, NG, body)

            mean = ph.sb("mean", [D, 1])
            var = ph.sb("var", [D, 1])
            gain = ph.sb("gain", [D, 1])
            shift = ph.sb("shift", [D, 1])
            SQ = ph.sb("SQ", [D, NT * P])
            s_v, s_a = ph.sem("bv"), ph.sem("ba")
            with nc.Block() as block:
                @block.vector
                def _(e):
                    e.tensor_reduce(mean[:, :], HT[:, 0:n_nodes], AX_X, ALU.add).then_inc(s_v, 1)
                    e.wait_ge(s_v, 1)
                    e.tensor_scalar(mean[:, :], mean[:, :], 1.0 / n_nodes, None, ALU.mult).then_inc(s_v, 1)
                    e.wait_ge(s_v, 2)
                    e.tensor_scalar(HT[:, :], HT[:, :], mean[:, 0:1], None, ALU.subtract).then_inc(s_v, 1)
                    e.wait_ge(s_v, 3)
                    e.tensor_tensor(SQ[:, 0:n_nodes], HT[:, 0:n_nodes], HT[:, 0:n_nodes], ALU.mult).then_inc(s_v, 1)
                    e.wait_ge(s_v, 4)
                    e.tensor_reduce(var[:, :], SQ[:, 0:n_nodes], AX_X, ALU.add).then_inc(s_v, 1)
                    e.wait_ge(s_a, 1)
                    e.reciprocal(var[:, :], var[:, :]).then_inc(s_v, 1)
                    e.wait_ge(s_v, 6)
                    e.tensor_tensor(gain[:, :], var[:, :], cols["gamma"][:, :], ALU.mult).then_inc(s_v, 1)
                    e.wait_ge(s_v, 7)

                @block.scalar
                def _(e):
                    e.wait_ge(s_v, 5)
                    e.activation(var[:, :], var[:, :], ACT.Sqrt, bias=eps_col[0:D, 0:1], scale=1.0 / n_nodes).then_inc(s_a, 1)
                    e.wait_ge(s_v, 7)
                    e.activation(SQ[:, :], HT[:, :], ACT.Relu, bias=cols["beta"][:, 0:1], scale=gain[:, 0:1]).then_inc(s_a, 1)
                    e.wait_ge(s_a, 2)

            y_src = ph.sb("y_src", [D, G * P])
            with Phase("n3b") as p2:
                y = p2.sb("y", [P, G, D])
                d = p2.sb("d", [P, G, D])
                sq = p2.sb("sq", [P, G, D])
                s1, s2 = p2.sb("s1", [P, G]), p2.sb("s2", [P, G])
                V = p2.steps("V", ["ysrc", "y"] + LN + ["keep"])
                A = p2.steps("A", ["ln_std"])
                T = p2.steps("T", ["tr"])
                with nc.Block() as block:
                    @block.tensor
                    def _(e):
                        def body(it):
                            V.wait(e, "ysrc", it)
                            for g in range(G):
                                ins = e.transpose(TP[:, g * P:g * P + D], y_src[:, g * P:(g + 1) * P], ident[0:D, 0:D])
                            T.give(ins, "tr")
                        loop(e, NG, body)

                    @block.vector
                    def _(e):
                        def body(it):
                            T.wait(e, "tr", it, 1)
                            V.give(e.tensor_scalar(y_src[:, :], SQ[:, bass.ds(it * (G * P), G * P)], 1.0, None, ALU.mult), "ysrc")
                            T.wait(e, "tr", it)
                            V.give(e.tensor_tensor(y[:, :, :], TP[:, 0:G * P].rearrange("p (g c) -> p g c", c=P)[:, :, 0:D],
                                                   X[:, bass.ds(it * G, G), :], ALU.add), "y")
                            dve_layernorm(e, V, it, y[:, :, :], d[:, :, :], sq[:, :, :], s1, s2, sq[:, :, :], "y", A)
                            V.give(e.tensor_scalar(X[:, bass.ds(it * G, G), :], sq[:, :, :], 1.0, None, ALU.mult), "keep")
                            V.wait(e, "keep", it)
                        loop(e, NG, body)

                    @block.scalar
                    def _(e):
                        loop(e, NG, lambda it: act_std(e, A, V, it, s2))

        def project(name, S, w_msg, w_root, bias_row, tab_dram):
            with Phase(name) as ph:
                xg = ph.sb("xg", [P, G, D])
                xT = ph.sb("xT", [D, G * P])
                tab = ph.sb("tab", [P, G, D])
                TP = ph.ps("TP", [P, 1024])
                O = [ph.ps(f"O{i}", [P, 1024]) for i in range(2)]
                V = ph.steps("V", ["xg", "root"])
                T = ph.steps("T", ["tr", "mm0", "mm1"])
                A = ph.steps("A", ["xT", "tab"])
                s_o = ph.sem("o")
                with nc.Block() as block:
                    @block.vector
                    def _(e):
                        def body(it):
                            T.wait(e, "tr", it, 1)
                            V.give(e.tensor_scalar(xg[:, :, :], S[:, bass.ds(it * G, G), :], 1.0, None, ALU.mult), "xg")
                            V.wait(e, "xg", it)
                            T.wait(e, "mm1", it)
                            V.give(e.tensor_tensor(R[:, bass.ds(it * G, G), :], O[1][:, 0:G * P].rearrange("p (g c) -> p g c", c=P)[:, :, 0:D],
                                                   bias_row[:, :].unsqueeze(1).to_broadcast([P, G, D]), ALU.add), "root")
                        loop(e, NG, body)

                    @block.tensor
                    def _(e):
                        def body(it):
                            V.wait(e, "xg", it)
                            A.wait(e, "xT", it, 1)
                            pe_transpose_group(e, T, TP, xg, it, "tr")
                            A.wait(e, "xT", it)
                            for i, w in enumerate((w_msg, w_root)):
                                for g in range(G):
                                    ins = e.matmul(O[i][:, g * P:g * P + D], xT[:, g * P:(g + 1) * P], w[:, :], start=True, stop=True)
                                T.give(ins, f"mm{i}")
                        loop(e, NG, body)

                    @block.scalar
                    def _(e):
                        def body(it):
                            T.wait(e, "tr", it)
                            A.give(e.activation(xT[:, :], TP[0:D, 0:G * P], ACT.Copy), "xT")
                            T.wait(e, "mm0", it)
                            wait_count(e, s_o, it, 16, 0)
                            A.give(e.activation(tab[:, :, :], O[0][:, 0:G * P].rearrange("p (g c) -> p g c", c=P)[:, :, 0:D], ACT.Copy), "tab")
                            A.wait(e, "tab", it)
                            e.dma_start(tab_dram[bass.ds(it * (G * P), G * P), :].rearrange("(g p) d -> p g d", p=P), tab[:, :, :]).then_inc(s_o, 16)
                        loop(e, NG, body)
                        e.wait_ge(s_o, 16 * NG)

        def conv_nodes(name, dest, residual):
            with Phase(name) as ph:
                ends = ph.sb("ends", [P, G], I32)
                agg = ph.sb("agg", [P, G, D])
                d = ph.sb("d", [P, G, D])
                sq = ph.sb("sq", [P, G, D])
                s1, s2 = ph.sb("s1", [P, G]), ph.sb("s2", [P, G])
                V = ph.steps("V", ["ends", "flag", "root", "leaky"] + (["y"] + LN if residual else []) + ["keep"])
                A = ph.steps("A", ["ln_std"])
                s_g = ph.sem("g")
                with nc.Block() as block:
                    @block.gpsimd
                    def _(e):
                        loop(e, NG, lambda it: pool_gather_ends(e, ends, agg, scan_out, s_g, lambda i: V.wait(e, "ends", i), it))

                    @block.vector
                    def _(e):
                        def body(it):
                            at = bass.ds(it * G, G)
                            wait_count(e, s_g, it, 16 * G, 0)
                            V.give(e.tensor_scalar(ends[:, :], end_idx[:, at], 1.0, None, ALU.mult), "ends")
                            wait_count(e, s_g, it, 16 * G, 16 * G)
                            V.give(e.tensor_tensor(agg[:, :, :], agg[:, :, :], flag[:, at].unsqueeze(2).to_broadcast([P, G, D]), ALU.mult), "flag")
                            V.wait(e, "flag", it)
                            V.give(e.tensor_tensor(d[:, :, :], agg[:, :, :], R[:, at, :], ALU.add), "root")
                            V.wait(e, "root", it)
                            V.give(e.scalar_tensor_tensor(sq[:, :, :], d[:, :, :], 0.01, d[:, :, :], ALU.mult, ALU.max), "leaky")
                            V.wait(e, "leaky", it)
                            if residual:
                                V.give(e.tensor_tensor(agg[:, :, :], sq[:, :, :], X[:, at, :], ALU.add), "y")
                                dve_layernorm(e, V, it, agg[:, :, :], d[:, :, :], sq[:, :, :], s1, s2, sq[:, :, :], "y", A)
                            V.give(e.tensor_scalar(dest[:, at, :], sq[:, :, :], 1.0, None, ALU.mult), "keep")
                            V.wait(e, "keep", it)
                        loop(e, NG, body)

                    if residual:
                        @block.scalar
                        def _(e):
                            loop(e, NG, lambda it: act_std(e, A, V, it, s2))

        project("p1", X, w96["W1_msg"], w96["W1_root"], rows["l2b1"], x_tab)
        edge_pass("e2a", x_tab, D, ACT.Copy, neg_row, BF16, ALU.add, ALU.max, scan_out, edge_w=we["W1_edge"])
        with Phase("c1") as keep_c1:
            C1 = keep_c1.sb("C1", [P, NT, D])
            conv_nodes("n4", C1, False)
            project("p2", C1, w96["W2_msg"], w96["W2_root"], rows["l2b2"], x_tab)
        edge_pass("e2b", x_tab, D, ACT.Copy, neg_row, BF16, ALU.add, ALU.max, scan_out, edge_w=we["W2_edge"])
        conv_nodes("n5", X, True)

        with Phase("n6") as ph:
            xg = ph.sb("xg", [P, G, D])
            xT = ph.sb("xT", [D, G * P])
            tab = ph.sb("tab", [P, G, HW])
            pr = ph.sb("pr", [P, G, D])
            starts = ph.sb("starts", [P, G], I32)
            ad = ph.sb("ad", [P, G])
            TP = ph.ps("TP", [P, 1024])
            O = ph.ps("O", [P, 1024])
            V = ph.steps("V", ["xg", "h", "ps", "as", "pd", "ad", "one", "tas", "kh", "kas", "kad", "st"])
            T = ph.steps("T", ["tr", "mm"])
            A = ph.steps("A", ["xT"])
            s_o, s_sc = ph.sem("o"), ph.sem("sc")
            with nc.Block() as block:
                @block.vector
                def _(e):
                    def body(it):
                        at = bass.ds(it * G, G)
                        T.wait(e, "tr", it, 1)
                        V.give(e.tensor_scalar(xg[:, :, :], X[:, at, :], 1.0, None, ALU.mult), "xg")
                        T.wait(e, "mm", it)
                        wait_count(e, s_o, it, 16, 0)
                        wait_count(e, s_sc, it, 16 * G, 0)
                        V.give(e.tensor_copy(tab[:, :, 0:D], O[:, 0:G * P].rearrange("p (g c) -> p g c", c=P)[:, :, 0:D]), "h")
                        V.wait(e, "h", it)
                        V.give(e.tensor_tensor(pr[:, :, :], tab[:, :, 0:D], rows["att_src"][:, :].unsqueeze(1).to_broadcast([P, G, D]), ALU.mult), "ps")
                        V.wait(e, "ps", it)
                        V.give(e.tensor_reduce(ad[:, :], pr[:, :, :], AX_X, ALU.add), "as")
                        V.wait(e, "as", it)
                        V.give(e.tensor_scalar(asrc[:, at], ad[:, :], 1.0, None, ALU.mult), "pd")
                        V.give(e.tensor_copy(tab[:, :, D + 1:D + 2], ad[:, :].unsqueeze(2)), "ad")
                        V.wait(e, "ad", it)
                        V.give(e.tensor_tensor(pr[:, :, :], tab[:, :, 0:D], rows["att_dst"][:, :].unsqueeze(1).to_broadcast([P, G, D]), ALU.mult), "one")
                        V.wait(e, "one", it)
                        V.give(e.tensor_reduce(ad[:, :], pr[:, :, :], AX_X, ALU.add), "tas")
                        V.wait(e, "tas", it)
                        V.give(e.tensor_scalar(adst[:, at], ad[:, :], 1.0, None, ALU.mult), "kh")
                        V.give(e.memset(tab[:, :, D:D + 1], 1.0), "kas")
                        V.give(e.tensor_scalar(R[:, at, :], tab[:, :, 0:D], 1.0, None, ALU.mult), "kad")
                        V.give(e.tensor_scalar(starts[:, :], start_idx[:, at], 1.0, None, ALU.mult), "st")
                    loop(e, NG, body)

                @block.tensor
                def _(e):
                    def body(it):
                        V.wait(e, "xg", it)
                        A.wait(e, "xT", it, 1)
                        pe_transpose_group(e, T, TP, xg, it, "tr")
                        A.wait(e, "xT", it)
                        for g in range(G):
                            ins = e.matmul(O[:, g * P:g * P + D], xT[:, g * P:(g + 1) * P], w96["W"][:, :], start=True, stop=True)
                        T.give(ins, "mm")
                    loop(e, NG, body)

                @block.scalar
                def _(e):
                    def body(it):
                        T.wait(e, "tr", it)
                        A.give(e.activation(xT[:, :], TP[0:D, 0:G * P], ACT.Copy), "xT")
                        V.wait(e, "st", it)
                        e.dma_start(h_tab[bass.ds(it * (G * P), G * P), :].rearrange("(g p) d -> p g d", p=P), tab[:, :, :]).then_inc(s_o, 16)
                    loop(e, NG, body)
                    e.wait_ge(s_o, 16 * NG)

                @block.gpsimd
                def _(e):
                    def body(it):
                        V.wait(e, "st", it)
                        for g in range(G):
                            e.indirect_dma_start(adst_lin, bass.IndirectOffsetOnAxis(starts[:, g:g + 1], axis=0), ad[:, g:g + 1],
                                                 None, bounds_check=EP - 1, oob_is_err=False).then_inc(s_sc, 16)
                    loop(e, NG, body)
                    e.wait_ge(s_sc, 16 * G * NG)

        with Phase("e3a", edge=True) as ph:
            NI = NCH // U
            idx = [ph.sb(f"idx{u}", [P, K], I32) for u in range(U)]
            got = [ph.sb(f"got{u}", [P, K, HW]) for u in range(U)]
            score_cols = ph.sb("score_cols", [P, NCH, K])
            s_ix, s_as = ph.sem("ix"), ph.sem("as")
            s_g = [ph.sem(f"g{u}") for u in range(U)]
            s_st = [ph.sem(f"st{u}") for u in range(U)]
            V = [ph.steps(f"V{u}", ["score"]) for u in range(U)]
            lin_c = h_lin.rearrange("(c p k) d -> c p (k d)", p=P, k=K)
            with nc.Block() as block:
                @block.gpsimd
                def _(e):
                    def step(it, u):
                        wait_count(e, s_ix, it, U, u + 1)
                        V[u].wait(e, "score", it, 1)
                        wait_count(e, s_st[u], it, 16, 0)
                        for k in range(K):
                            e.indirect_dma_start(got[u][:, k, :], None, h_tab, bass.IndirectOffsetOnAxis(idx[u][:, k:k + 1], axis=0),
                                                 bounds_check=NROW - 1, oob_is_err=False).then_inc(s_g[u], 16)
                    loop(e, NI, lambda it: [step(it, u) for u in range(U)])

                @block.vector
                def _(e):
                    for u in range(2):
                        e.tensor_scalar(idx[u][:, :], src_cols[:, u * K:(u + 1) * K], 1.0, None, ALU.mult).then_inc(s_ix, 1)

                    def step(it, u):
                        e.tensor_scalar(idx[(u + 2) % U][:, :], src_cols[:, bass.ds((it * U + u + 2) * K, K)], 1.0, None, ALU.mult).then_inc(s_ix, 1)
                        wait_count(e, s_g[u], it, 16 * K, 16 * K)
                        V[u].give(e.tensor_scalar(score_cols[:, bass.ds(it * U + u, 1), :].rearrange("p a k -> p (a k)"), got[u][:, :, D + 1], 1.0, None, ALU.mult), "score")
                    loop(e, NI, lambda it: [step(it, u) for u in range(U)])

                @block.sync
                def _(e):
                    def step(it, u):
                        wait_count(e, s_g[u], it, 16 * K, 16 * K)
                        e.dma_start(lin_c[bass.ds(it * U + u, 1)].rearrange("a p x -> (a p) x"), got[u][:, :, :].rearrange("p k d -> p (k d)")).then_inc(s_st[u], 16)
                    loop(e, NI, lambda it: [step(it, u) for u in range(U)])
                    for u in range(U):
                        V[u].wait(e, "score", NI - 1)
                        e.wait_ge(s_st[u], 16 * NI)
                    e.dma_start(asrc_lin.rearrange("(c p k) -> p c k", p=P, k=K), score_cols[:, :, :]).then_inc(s_as, 16)
                    e.wait_ge(s_as, 16)

        with Phase("s3") as ph:
            asr = ph.sb("asr", [P, EC])
            adr = ph.sb("adr", [P, EC])
            keep_b = ph.sb("keep_b", [P, EC], BF16)
            neg_b = ph.sb("neg_b", [P, EC], BF16)
            ad_e = ph.sb("ad_e", [P, EC])
            z = ph.sb("z", [P, EC])
            zl = ph.sb("zl", [P, EC])
            rm = ph.sb("rm", [P, EC + 1])
            prodk = ph.sb("prodk", [P, EC])
            zeros = ph.sb("zeros", [P, EC])
            lastc = ph.sb("lastc", [P, 3])
            row = ph.sb("row", [1, 4, P])
            prev = ph.sb("prev", [P, 2])
            s_ld, s_v, s_a, s_c, s_o = ph.sem("ld"), ph.sem("v"), ph.sem("a"), ph.sem("c"), ph.sem("o")
            pm = lambda ap: ap.rearrange("(p c) -> p c", p=P)
            count = [0]

            def then(e, ins):
                count[0] += 1
                ins.then_inc(s_v, 1)
                e.wait_ge(s_v, count[0])
                return count[0]

            marks = {}
            with nc.Block() as block:
                @block.vector
                def _(e):
                    e.wait_ge(s_ld, 80)
                    then(e, e.memset(zeros[:, :], 0.0))
                    then(e, e.tensor_tensor_scan(prodk[:, :], keep_b[:, :], zeros[:, :], 1.0, ALU.mult, ALU.add))
                    then(e, e.tensor_tensor_scan(ad_e[:, :], keep_b[:, :], adr[:, :], 0.0, ALU.mult, ALU.add))
                    then(e, e.tensor_copy(lastc[:, 0:1], ad_e[:, EC - 1:EC]))
                    marks["last1"] = then(e, e.tensor_copy(lastc[:, 1:2], prodk[:, EC - 1:EC]))
                    e.wait_ge(s_c, 64)
                    then(e, e.memset(row[:, 2, :], 0.0))
                    then(e, e.tensor_tensor_scan(row[:, 2, 1:P], row[:, 1, 0:P - 1], row[:, 0, 0:P - 1], 0.0, ALU.mult, ALU.add))
                    marks["carry1"] = count[0]
                    e.wait_ge(s_c, 80)
                    then(e, e.scalar_tensor_tensor(ad_e[:, :], prodk[:, :], prev[:, 0:1], ad_e[:, :], ALU.mult, ALU.add))
                    then(e, e.tensor_tensor(z[:, :], asr[:, :], ad_e[:, :], ALU.add))
                    then(e, e.scalar_tensor_tensor(zl[:, :], z[:, :], 0.2, z[:, :], ALU.mult, ALU.max))
                    then(e, e.tensor_tensor_scan(rm[:, 1:EC + 1], neg_b[:, :], zl[:, :], NEG, ALU.add, ALU.max))
                    then(e, e.tensor_copy(lastc[:, 0:1], rm[:, EC:EC + 1]))
                    then(e, e.tensor_scalar(lastc[:, 1:2], prodk[:, EC - 1:EC], -NEG, NEG, ALU.mult, ALU.add))
                    marks["last2"] = count[0]
                    e.wait_ge(s_c, 144)
                    then(e, e.memset(row[:, 2, :], NEG))
                    then(e, e.tensor_tensor_scan(row[:, 2, 1:P], row[:, 1, 0:P - 1], row[:, 0, 0:P - 1], NEG, ALU.add, ALU.max))
                    marks["carry2"] = count[0]
                    e.wait_ge(s_c, 160)
                    then(e, e.tensor_tensor_scan(rm[:, 1:EC + 1], neg_b[:, :], zl[:, :], prev[:, 1:2], ALU.add, ALU.max))
                    then(e, e.tensor_copy(rm[:, 0:1], prev[:, 1:2]))
                    then(e, e.tensor_tensor(z[:, :], zl[:, :], rm[:, 1:EC + 1], ALU.subtract))
                    then(e, e.tensor_tensor(ad_e[:, :], rm[:, 0:EC], rm[:, 1:EC + 1], ALU.subtract))
                    then(e, e.tensor_scalar(ad_e[:, :], ad_e[:, :], 0.0, None, ALU.min))
                    marks["exps"] = count[0]
                    e.wait_ge(s_a, 2)
                    then(e, e.tensor_tensor(ad_e[:, :], ad_e[:, :], keep_b[:, :], ALU.mult))
                    marks["decay"] = count[0]

                @block.scalar
                def _(e):
                    e.wait_ge(s_v, marks["exps"])
                    e.activation(z[:, :], z[:, :], ACT.Exp).then_inc(s_a, 1)
                    e.activation(ad_e[:, :], ad_e[:, :], ACT.Exp).then_inc(s_a, 1)

                @block.sync
                def _(e):
                    e.dma_start(asr[:, :], pm(asrc_lin)).then_inc(s_ld, 16)
                    e.dma_start(adr[:, :], adst_lin.rearrange("(p c) d -> p (c d)", p=P)).then_inc(s_ld, 16)
                    e.dma_start(keep_b[:, :], pm(keep_row)).then_inc(s_ld, 16)
                    e.dma_start(neg_b[:, :], pm(neg_row)).then_inc(s_ld, 16)
                    e.dma_start(prev[:, :], t["two_cols"]).then_inc(s_ld, 16) if "two_cols" in t else e.dma_start(
                        prev[:, :], adst_lin[0:2 * P, :].rearrange("(p c) d -> p (c d)", p=P)).then_inc(s_ld, 16)

                    def to_row(col, r, d):
                        e.dma_start(carry_dram[d, :].rearrange("(p a) -> p a", a=1), lastc[:, col:col + 1]).then_inc(s_c, 16)

                    def round_trip(mark_last, mark_carry, base, d, col):
                        e.wait_ge(s_v, marks[mark_last])
                        to_row(0, 0, d)
                        to_row(1, 1, d + 1)
                        e.wait_ge(s_c, base + 32)
                        e.dma_start(row[:, 0, :], carry_dram[d:d + 1, :]).then_inc(s_c, 16)
                        e.dma_start(row[:, 1, :], carry_dram[d + 1:d + 2, :]).then_inc(s_c, 16)
                        e.wait_ge(s_v, marks[mark_carry])
                        e.wait_ge(s_c, base + 64)
                        e.dma_start(carry_dram[d + 2:d + 3, :], row[:, 2, :]).then_inc(s_o, 16)
                        e.wait_ge(s_o, 16 if d == 0 else 32)
                        e.dma_start(prev[:, col:col + 1], carry_dram[d + 2, :].rearrange("(p a) -> p a", a=1)).then_inc(s_c, 16)

                    round_trip("last1", "carry1", 0, 0, 0)
                    round_trip("last2", "carry2", 80, 3, 1)
                    e.wait_ge(s_v, marks["decay"])
                    e.dma_start(pm(weight_lin), z[:, :]).then_inc(s_o, 16)
                    e.dma_start(pm(decay_row), ad_e[:, :]).then_inc(s_o, 16)
                    e.dma_start(rmax_lin.rearrange("(p c) d -> p (c d)", p=P), rm[:, 1:EC + 1]).then_inc(s_o, 16)
                    e.wait_ge(s_o, 80)

        edge_pass("e3", h_lin, DN, ACT.Copy, decay_row, F32, ALU.mult, ALU.add, scan_out3, gather=False)

        with Phase("n7") as ph:
            ends = ph.sb("ends", [P, G], I32)
            agg = ph.sb("agg", [P, G, DN])
            mx = ph.sb("mx", [P, G, 1])
            zs, z2, m2, em, es, fl = (ph.sb(n, [P, G]) for n in ("zs", "z2", "m2", "em", "es", "fl"))
            y = ph.sb("y", [P, G, D])
            d = ph.sb("d", [P, G, D])
            sq = ph.sb("sq", [P, G, D])
            ob = ph.sb("ob", [P, G, D])
            s1, s2 = ph.sb("s1", [P, G]), ph.sb("s2", [P, G])
            V = ph.steps("V", ["ends", "fl", "zsum", "zleaky", "mflag", "mneg", "mmax", "dm", "ds", "ef", "scale", "den", "hs", "num",
                               "rden", "out", "bias", "y"] + LN)
            A = ph.steps("A", ["em", "es", "tanh", "ln_std"])
            s_g, s_o = ph.sem("g"), ph.sem("o")
            bc = lambda ap, n: ap.unsqueeze(2).to_broadcast([P, G, n])
            with nc.Block() as block:
                @block.gpsimd
                def _(e):
                    def body(it):
                        V.wait(e, "ends", it)
                        for g in range(G):
                            off = bass.IndirectOffsetOnAxis(ends[:, g:g + 1], axis=0)
                            e.indirect_dma_start(agg[:, g, :], None, scan_out3, off, bounds_check=EP - 1, oob_is_err=False).then_inc(s_g, 16)
                            off = bass.IndirectOffsetOnAxis(ends[:, g:g + 1], axis=0)
                            e.indirect_dma_start(mx[:, g, :], None, rmax_lin, off, bounds_check=EP - 1, oob_is_err=False).then_inc(s_g, 16)
                    loop(e, NG, body)

                @block.vector
                def _(e):
                    def body(it):
                        at = bass.ds(it * G, G)

                        def op(ins, name):
                            V.give(ins, name)
                            V.wait(e, name, it)
                        wait_count(e, s_g, it, 32 * G, 0)
                        op(e.tensor_scalar(ends[:, :], end_idx[:, at], 1.0, None, ALU.mult), "ends")
                        op(e.tensor_scalar(fl[:, :], flag[:, at], 1.0, None, ALU.mult), "fl")
                        op(e.tensor_tensor(zs[:, :], asrc[:, at], adst[:, at], ALU.add), "zsum")
                        op(e.scalar_tensor_tensor(z2[:, :], zs[:, :], 0.2, zs[:, :], ALU.mult, ALU.max), "zleaky")
                        wait_count(e, s_g, it, 32 * G, 32 * G)
                        op(e.tensor_tensor(m2[:, :], mx[:, :, 0], fl[:, :], ALU.mult), "mflag")
                        op(e.tensor_scalar(zs[:, :], fl[:, :], -NEG, NEG, ALU.mult, ALU.add), "mneg")
                        op(e.tensor_tensor(m2[:, :], m2[:, :], zs[:, :], ALU.add), "mmax")
                        op(e.tensor_tensor(zs[:, :], m2[:, :], z2[:, :], ALU.max), "dm")
                        op(e.tensor_tensor(m2[:, :], m2[:, :], zs[:, :], ALU.subtract), "ds")
                        op(e.tensor_tensor(z2[:, :], z2[:, :], zs[:, :], ALU.subtract), "ef")
                        A.wait(e, "es", it)
                        op(e.tensor_tensor(em[:, :], em[:, :], fl[:, :], ALU.mult), "scale")
                        op(e.tensor_tensor(agg[:, :, :], agg[:, :, :], bc(em[:, :], DN), ALU.mult), "den")
                        op(e.tensor_tensor(d[:, :, :], R[:, at, :], bc(es[:, :], D), ALU.mult), "hs")
                        op(e.tensor_tensor(d[:, :, :], agg[:, :, 0:D], d[:, :, :], ALU.add), "num")
                        op(e.scalar_tensor_tensor(es[:, :], agg[:, :, D], 1e-16, es[:, :], ALU.add, ALU.add), "rden")
                        op(e.reciprocal(es[:, :], es[:, :]), "out")
                        op(e.tensor_tensor(d[:, :, :], d[:, :, :], bc(es[:, :], D), ALU.mult), "bias")
                        op(e.tensor_tensor(y[:, :, :], d[:, :, :], rows["bias"][:, :].unsqueeze(1).to_broadcast([P, G, D]), ALU.add), "y")
                        A.wait(e, "tanh", it)
                        wait_count(e, s_o, it, 16, 0)
                        e.tensor_tensor(sq[:, :, :], ob[:, :, :], X[:, at, :], ALU.add).then_inc(s_y, 1)
                        wait_count(e, s_y, it, 1, 1)
                        dve_layernorm(e, V, it, sq[:, :, :], d[:, :, :], y[:, :, :], s1, s2, sq[:, :, :], "y", A)
                    s_y = ph.sem("y")
                    loop(e, NG, body)

                @block.scalar
                def _(e):
                    def body(it):
                        V.wait(e, "ef", it)
                        A.give(e.activation(em[:, :], m2[:, :], ACT.Exp), "em")
                        A.give(e.activation(es[:, :], z2[:, :], ACT.Exp), "es")
                        V.wait(e, "y", it)
                        A.give(e.activation(ob[:, :, :], y[:, :, :], ACT.Tanh), "tanh")
                        act_std(e, A, V, it, s2)
                        V.wait(e, "ln_out", it)
                        e.dma_start(t["out"][bass.ds(it * (G * P), G * P), :].rearrange("(g p) d -> p g d", p=P), sq[:, :, :]).then_inc(s_o, 16)
                    loop(e, NG, body)
                    e.wait_ge(s_o, 16 * NG)


_WEIGHTS = ["L0_gnn_qW", "L0_gnn_kW", "L0_gnn_vW", "L1_gnn_We", "L1_gnn_be", "L1_gnn_W1", "L1_gnn_b1", "L1_gnn_W2", "L1_gnn_b2",
            "L1_gnn_gamma", "L1_gnn_beta", "L2_gnn_W1_msg", "L2_gnn_W1_edge", "L2_gnn_W1_root", "L2_gnn_b1", "L2_gnn_W2_msg",
            "L2_gnn_W2_edge", "L2_gnn_W2_root", "L2_gnn_b2", "L3_gnn_W", "L3_gnn_att_src", "L3_gnn_att_dst", "L3_gnn_bias"]


def kernel(**inputs):
    import concourse.bacc as bacc
    from concourse.bass_utils import run_bass_kernel_spmd

    x, src, dst, attr = (np.asarray(inputs[n]) for n in ("x", "src", "dst", "edge_attr_32"))
    n_nodes, D = x.shape
    n_edges, DE = attr.shape
    NT, NCH = padded_sizes(n_nodes, n_edges)
    n_rows, n_padded = NT * P, NCH * CH
    x_pad = np.zeros((n_rows, D), x.dtype)
    x_pad[:n_nodes] = x
    src_pad = np.full(n_padded, n_nodes, src.dtype)
    src_pad[:n_edges] = src
    src_cols = np.ascontiguousarray(src_pad.reshape(NCH, P, K).transpose(1, 0, 2).reshape(P, NCH * K))
    dst_pad = np.full(n_padded, n_nodes, dst.dtype)
    dst_pad[:n_edges] = dst
    dst_prev = np.full(n_padded, -1, dst.dtype)
    dst_prev[1:] = dst_pad[:-1]
    attr_T = np.zeros((DE + 1, n_padded), attr.dtype)
    attr_T[:DE, :n_edges] = attr.T
    attr_T[DE] = 1
    arrays = {"x": x_pad, "src_pad": src_pad, "src_cols": src_cols, "dst_pad": dst_pad, "dst_prev": dst_prev, "attr_T": attr_T}
    for n in _WEIGHTS:
        arrays[n] = np.ascontiguousarray(inputs[n])

    nc = bacc.Bacc("TRN2", target_bir_lowering=False, num_devices=1)
    t = {n: nc.dram_tensor(f"in_{n}", a.shape, mybir.dt.from_np(a.dtype), kind="ExternalInput").ap() for n, a in arrays.items()}
    t["out"] = nc.dram_tensor("out_nodes", (n_rows, D), F32, kind="ExternalOutput").ap()
    build(nc, t, n_nodes, n_edges, D, DE)
    r = run_bass_kernel_spmd(nc, [{f"in_{n}": a for n, a in arrays.items()}], core_ids=[0])
    return r.results[0]["out_nodes"][:n_nodes]
```

```python
from contextlib import ExitStack

import numpy as np

import concourse.bass as bass
from concourse import mybir

F32 = mybir.dt.float32
BF16 = mybir.dt.bfloat16
I32 = mybir.dt.int32
ALU = mybir.AluOpType
ACT = mybir.ActivationFunctionType
AX_X = mybir.AxisListType.X

P = 128
K = 4
U = 4
CH = P * K
G = 7
HEADS = 4
LANES = 2
NEG = -2.9e38
EPS = 1e-5


def padded_sizes(n_nodes, n_edges):
    n_tiles = -(-(n_nodes + 1) // (P * G)) * G
    n_chunks = -(-n_edges // (CH * U)) * U
    return n_tiles, n_chunks


PASSED = {}
FIRST_PASS = [0]


def loop(eng, n, body, last_apart=False, apart=1):
    for i in range(min(apart, n)):
        body(i)
    end = n - 1 if last_apart else n
    if end > apart:
        FIRST_PASS[0] = apart
        with eng.Fori(apart, end) as it:
            body(it)
    if last_apart and n > apart:
        body(n - 1)


class Steps:

    def __init__(self, sem, names):
        self.sem, self.names = sem, list(names)

    def give(self, instruction, name):
        assert name in self.names
        instruction.then_inc(self.sem, 1)

    def wait(self, eng, name, it, back=0):
        n, at = len(self.names), self.names.index(name) + 1
        wait_count(eng, self.sem, it, n, at - back * n)


def wait_count(eng, sem, it, per, plus):
    if isinstance(it, int):
        if it * per + plus > 0:
            eng.wait_ge(sem, it * per + plus)
    else:
        assert FIRST_PASS[0] * per + plus > 0
        eng.wait_ge(sem, it * per + plus)
        if id(eng) in PASSED:
            eng.sem_inc(PASSED[id(eng)], 1)


def behind(u, lag):
    return (u - lag) % U, (U - 1 - u + lag) // U


def started(it, u, lag):
    return not isinstance(it, int) or it * U + u >= lag


def wait_stored(eng, sem, it, back):
    wait_count(eng, sem, it, 16, -16 * back)


def build(nc, t, n_nodes, n_edges, D, DE):
    NT, NCH = padded_sizes(n_nodes, n_edges)
    NG = NT // G
    NROW = NT * P
    EP = NCH * CH
    EC = EP // P
    DH = D // HEADS
    PAY = D + HEADS
    TROW = NROW + P
    NTAB = K
    HW = D + 2
    DN = D + 1
    NTL = NCH * K
    assert NTL <= 4 * 512
    assert TROW % P == 0 and D % HEADS == 0 and NT <= P and CH == 512

    def scratch(name, shape, dt=F32):
        return nc.dram_tensor(name, shape, dt, kind="Internal").ap()

    q_tab = scratch("q_tab", (NROW, D))
    kv_used = scratch("kv_used", (TROW, 2 * D))
    rel_row = scratch("rel_row", (EP,), BF16)
    sum_tab = [scratch(f"sum_tab{j}", (TROW, PAY)) for j in range(NTAB)]
    x_tab = scratch("x_tab", (NROW, D))
    h_tab = scratch("h_tab", (NROW, HW))
    keep_row = scratch("keep_row", (EP,), BF16)
    neg_row = scratch("neg_row", (EP,), BF16)
    ad_row = scratch("ad_row", (EP,))
    adst_lin = scratch("adst_lin", (EP, 1))
    rmax_lin = scratch("rmax_lin", (EP, 1))
    carry_dram = scratch("carry_dram", (3, P))
    scan_out = scratch("scan_out", (EP, D))
    scan_out3 = scratch("scan_out3", (EP, DN))

    def bcast_row(ap1d, parts, n):
        return ap1d.rearrange("(a n) -> a n", a=1).to_broadcast([parts, n])

    with ExitStack() as top:
        for eng, name in ((nc.sync, "passed_sp"), (nc.gpsimd, "passed_pool")):
            PASSED[id(eng)] = top.enter_context(nc.semaphore(name))

        def keepb(name, shape, dt=F32):
            return top.enter_context(nc.sbuf_tensor(name, shape, dt))

        X = keepb("X", [P, NT, D])
        R = keepb("R", [P, NT, D])
        ident = keepb("ident", [P, P])
        tri = keepb("tri", [P, P])
        ones_f = keepb("ones_f", [1, P])
        ones_b = keepb("ones_b", [1, P], BF16)
        eps_col = keepb("eps_col", [P, 1])
        dump_col = keepb("dump_col", [P, 1])
        part_col = keepb("part_col", [P, 1])
        node_q = keepb("node_q", [P, NT])
        end_idx = keepb("end_idx", [P, NT + G], I32)
        start_idx = keepb("start_idx", [P, NT], I32)
        flag = keepb("flag", [P, NT])
        src_cols = keepb("src_cols", [P, NCH * K + 2 * K], I32)
        src_tcols = keepb("src_tcols", [P, NTL + U * K], I32)
        win_row = keepb("win_row", [1, NTL], I32)
        used_idx = keepb("used_idx", [P, NT], I32)
        asrc = keepb("asrc", [P, NT])
        adst = keepb("adst", [P, NT])
        w96 = {n: keepb("w_" + n, [D, D]) for n in
               ("qW", "kW", "vW", "W1", "W2", "W1_msg", "W1_root", "W2_msg", "W2_root", "W")}
        we = {n: keepb("we_" + n, [DE + 1, D]) for n in ("We", "W1_edge", "W2_edge")}
        cols = {n: keepb("c_" + n, [D, 1]) for n in ("b1", "b2", "gamma", "beta")}
        rows = {n: keepb("r_" + n, [P, D]) for n in ("l2b1", "l2b2", "att_src", "att_dst", "bias")}

        edge_sems = {}

        class Phase:

            def __init__(self, name, edge=False):
                self.name, self.edge = name, edge

            def __enter__(self):
                self.ctx = ExitStack()
                self.ctx.__enter__()
                return self

            def __exit__(self, *a):
                if self.edge:
                    for s in edge_sems.values():
                        nc.gpsimd.sem_clear(s)
                return self.ctx.__exit__(*a)

            def sb(self, n, shape, dt=F32):
                return self.ctx.enter_context(nc.sbuf_tensor(f"{self.name}_{n}", shape, dt))

            def ps(self, n, shape):
                return self.ctx.enter_context(nc.psum_tensor(f"{self.name}_{n}", shape, F32))

            def sem(self, n):
                if self.edge and not n.startswith("g"):
                    if n not in edge_sems:
                        edge_sems[n] = top.enter_context(nc.semaphore(f"edge_{n}"))
                    return edge_sems[n]
                return self.ctx.enter_context(nc.semaphore(f"{self.name}_{n}"))

            def steps(self, n, names):
                return Steps(self.sem(n), names)

            def block(self):
                return self.ctx.enter_context(nc.Block())

        with Phase("const") as ph:
            s_w, s_m, s_p, s_v = ph.sem("w"), ph.sem("m"), ph.sem("p"), ph.sem("v")
            qi = ph.sb("qi", [P, NT], I32)
            di = ph.sb("di", [P, 1], I32)
            with nc.Block() as block:
                loads = [(X[:, :, :], t["x"].rearrange("(t p) d -> p t d", p=P)),
                         (src_cols[:, 0:NCH * K], t["src_cols"]), (src_tcols[:, 0:NTL], t["src_tcols"])]
                for n, key in (("qW", "L0_gnn_qW"), ("kW", "L0_gnn_kW"), ("vW", "L0_gnn_vW"), ("W1", "L1_gnn_W1"),
                               ("W2", "L1_gnn_W2"), ("W1_msg", "L2_gnn_W1_msg"), ("W1_root", "L2_gnn_W1_root"),
                               ("W2_msg", "L2_gnn_W2_msg"), ("W2_root", "L2_gnn_W2_root"), ("W", "L3_gnn_W")):
                    loads.append((w96[n][:, :], t[key]))
                for n, key in (("We", "L1_gnn_We"), ("W1_edge", "L2_gnn_W1_edge"), ("W2_edge", "L2_gnn_W2_edge")):
                    loads.append((we[n][0:DE, :], t[key]))
                loads.append((we["We"][DE:DE + 1, :], t["L1_gnn_be"].rearrange("(a n) -> a n", a=1)))
                for n, key in (("b1", "L1_gnn_b1"), ("b2", "L1_gnn_b2"), ("gamma", "L1_gnn_gamma"), ("beta", "L1_gnn_beta")):
                    loads.append((cols[n][:, :], t[key].rearrange("(n a) -> n a", a=1)))
                for n, key in (("l2b1", "L2_gnn_b1"), ("l2b2", "L2_gnn_b2"), ("att_src", "L3_gnn_att_src"),
                               ("att_dst", "L3_gnn_att_dst"), ("bias", "L3_gnn_bias")):
                    loads.append((rows[n][:, :], bcast_row(t[key], P, D)))

                @block.sync
                def _(e):
                    for dst, src in loads:
                        e.dma_start(dst, src).then_inc(s_w, 16)
                    e.wait_ge(s_w, 16 * len(loads))

                @block.gpsimd
                def _(e):
                    e.memset(ident[:, :], 0.0).then_inc(s_p, 1)
                    e.memset(tri[:, :], 1.0).then_inc(s_p, 1)
                    e.iota(qi[:, :], pattern=[[P, NT]], base=0, channel_multiplier=1).then_inc(s_p, 1)
                    e.iota(di[:, :], pattern=[[0, 1]], base=NROW, channel_multiplier=1).then_inc(s_p, 1)
                    e.wait_ge(s_p, 4)
                    e.affine_select(out=ident[:, :], in_=ident[:, :], compare_op=ALU.not_equal, fill=1.0, base=0,
                                    pattern=[[-1, P]], channel_multiplier=1).then_inc(s_p, 1)
                    e.affine_select(out=tri[:, :], in_=tri[:, :], compare_op=ALU.is_gt, fill=0.0, base=0,
                                    pattern=[[-1, P]], channel_multiplier=1).then_inc(s_p, 1)
                    e.wait_ge(s_p, 6)

                @block.vector
                def _(e):
                    e.memset(we["W1_edge"][DE:DE + 1, :], 0.0)
                    e.memset(we["W2_edge"][DE:DE + 1, :], 0.0)
                    e.memset(src_cols[:, NCH * K:], 0)
                    e.memset(src_tcols[:, NTL:], 0)
                    e.memset(end_idx[:, NT:], 0)
                    e.memset(ones_f[:, :], 1.0)
                    e.memset(ones_b[:, :], 1.0)
                    e.memset(eps_col[:, :], EPS)
                    e.wait_ge(s_p, 4)
                    e.tensor_copy(node_q[:, :], qi[:, :]).then_inc(s_v, 1)
                    e.tensor_copy(dump_col[:, :], di[:, :]).then_inc(s_v, 1)
                    e.wait_ge(s_v, 2)
                    e.tensor_scalar(part_col[:, :], dump_col[:, :], -float(NROW), None, ALU.add).then_inc(s_v, 1)
                    e.wait_ge(s_v, 3)

        with Phase("find") as ph:
            dst_rows = t["dst_pad"].rearrange("(r c) -> r c", c=CH)
            first_i = ph.sb("first_i", [1, NCH], I32)
            first_f = ph.sb("first_f", [1, NCH])
            firsts = ph.sb("firsts", [P, NCH])
            junk = ph.sb("junk", [P, NCH])
            rows_le = ph.sb("rows_le", [P, NT])
            row_f = ph.sb("row_f", [P, NT + G])
            row_i = ph.sb("row_i", [P, G], I32)
            got_i = ph.sb("got_i", [P, G, CH], I32)
            junk2 = ph.sb("junk2", [P, G, CH])
            in_row = ph.sb("in_row", [P, NT])
            upto = ph.sb("upto", [P, NT + 1])
            tmp = ph.sb("tmp", [P, NT])
            shift_m = ph.sb("shift_m", [P, P])
            corner_m = ph.sb("corner_m", [P, P])
            dst_i = ph.sb("dst_i", [P, EC], I32)
            prev_i = ph.sb("prev_i", [P, EC], I32)
            keep_b = ph.sb("keep_b", [P, EC], BF16)
            neg_b = ph.sb("neg_b", [P, EC], BF16)
            firsts_ps = ph.ps("firsts_ps", [P, 512])
            before_ps = ph.ps("before_ps", [P, 512])
            s_ld, s_st, s_m, s_f = ph.sem("ld"), ph.sem("st"), ph.sem("m"), ph.sem("fin")
            s_g = [ph.sem(f"g{g}") for g in range(G)]
            s_pre, s_pe, s_z, s_first = ph.sem("pre"), ph.sem("pe"), ph.sem("z"), ph.sem("first")
            vec = ph.steps("vec", [n + str(g) for g in range(G) for n in ("row", "count")])
            assert NCH <= 512
            with nc.Block() as block:
                @block.sync
                def _(e):
                    with nc.allow_non_contiguous_dma(reason="one element of each row"):
                        e.dma_start(first_i[:, :], t["dst_pad"].rearrange("(a r c) -> a r c", a=1, c=CH)[:, :, 0:1]
                                    .rearrange("a r c -> a (r c)"), allow_slow_non_contiguous=True).then_inc(s_ld, 16)
                    e.dma_start(dst_i[:, :], t["dst_pad"].rearrange("(p c) -> p c", p=P)).then_inc(s_ld, 16)
                    e.dma_start(prev_i[:, :], t["dst_prev"].rearrange("(p c) -> p c", p=P)).then_inc(s_ld, 16)
                    e.wait_ge(s_pre, 2 + NT + 3)
                    e.dma_start(keep_row.rearrange("(p c) -> p c", p=P), keep_b[:, :]).then_inc(s_st, 16)
                    e.dma_start(neg_row.rearrange("(p c) -> p c", p=P), neg_b[:, :]).then_inc(s_st, 16)
                    e.wait_ge(s_st, 32)

                @block.tensor
                def _(e):
                    e.wait_ge(s_pre, 1)
                    e.matmul(firsts_ps[:, 0:NCH], ones_f[:, :], first_f[:, :], start=True, stop=True).then_inc(s_pe, 1)
                    e.wait_ge(s_m, 4)
                    e.wait_ge(s_f, 1)
                    e.matmul(before_ps[:, 0:NT], shift_m[:, :], upto[:, 1:NT + 1], start=True, stop=False)
                    e.matmul(before_ps[:, 0:NT], corner_m[:, :], upto[:, 0:NT], start=False, stop=True).then_inc(s_pe, 1)

                @block.gpsimd
                def _(e):
                    e.memset(shift_m[:, :], 0.0).then_inc(s_m, 1)
                    e.memset(corner_m[:, :], 0.0).then_inc(s_m, 1)
                    e.wait_ge(s_m, 2)
                    e.affine_select(out=shift_m[:, :], in_=shift_m[:, :], compare_op=ALU.not_equal, fill=1.0, base=1,
                                    pattern=[[-1, P]], channel_multiplier=1).then_inc(s_m, 1)
                    e.affine_select(out=corner_m[:, :], in_=corner_m[:, :], compare_op=ALU.not_equal, fill=1.0, base=1 - P,
                                    pattern=[[P, P]], channel_multiplier=1).then_inc(s_m, 1)

                    def body(it):
                        for g in range(G):
                            vec.wait(e, f"count{g}", it, 1)
                            e.indirect_dma_start(got_i[:, g, :], None, dst_rows,
                                                 bass.IndirectOffsetOnAxis(row_i[:, g:g + 1], axis=0),
                                                 bounds_check=NCH - 1, oob_is_err=False).then_inc(s_g[g], 16)
                    e.wait_ge(s_first, 1)
                    loop(e, NG, body)

                @block.vector
                def _(e):
                    e.memset(upto[:, 0:1], 0.0).then_inc(s_z, 1)
                    e.memset(row_f[:, NT:], 0.0).then_inc(s_z, 1)
                    e.wait_ge(s_z, 2)
                    e.wait_ge(s_ld, 48)
                    e.tensor_copy(first_f[:, :], first_i[:, :]).then_inc(s_pre, 1)
                    e.wait_ge(s_pe, 1)
                    e.tensor_copy(firsts[:, :], firsts_ps[:, 0:NCH]).then_inc(s_pre, 1)
                    e.wait_ge(s_pre, 2)
                    for q in range(NT):
                        e.wait_ge(s_pre, 2 + q)
                        e.tensor_scalar(junk[:, :], firsts[:, :], node_q[:, q:q + 1], 0.0, ALU.is_le, ALU.add,
                                        accum_out=rows_le[:, q:q + 1]).then_inc(s_pre, 1)
                    e.tensor_tensor(keep_b[:, :], dst_i[:, :], prev_i[:, :], ALU.is_equal).then_inc(s_pre, 1)
                    e.wait_ge(s_pre, 2 + NT + 1)
                    e.tensor_scalar(neg_b[:, :], keep_b[:, :], -NEG, NEG, ALU.mult, ALU.add).then_inc(s_pre, 1)
                    e.tensor_scalar(row_f[:, 0:NT], rows_le[:, :], -1.0, 0.0, ALU.add, ALU.max).then_inc(s_pre, 1)
                    e.wait_ge(s_pre, 2 + NT + 3)
                    e.tensor_scalar(row_i[:, :], row_f[:, 0:G], 1.0, None, ALU.mult).then_inc(s_first, 1)

                    def body(it):
                        for g in range(G):
                            wait_count(e, s_g[g], it, 16, 16)
                            vec.give(e.tensor_scalar(row_i[:, g:g + 1], row_f[:, bass.ds(it * G + (G + g), 1)], 1.0, None, ALU.mult), f"row{g}")
                            vec.give(e.tensor_scalar(junk2[:, g, :], got_i[:, g, :], node_q[:, bass.ds(it * G + g, 1)], 0.0, ALU.is_le,
                                                     ALU.add, accum_out=in_row[:, bass.ds(it * G + g, 1)]), f"count{g}")
                    loop(e, NG, body)
                    vec.wait(e, f"count{G - 1}", NG - 1)
                    e.scalar_tensor_tensor(upto[:, 1:NT + 1], row_f[:, 0:NT], float(CH), in_row[:, :], ALU.mult, ALU.add).then_inc(s_f, 1)
                    e.wait_ge(s_f, 1)
                    e.tensor_scalar(end_idx[:, 0:NT], upto[:, 1:NT + 1], -1.0, 0.0, ALU.add, ALU.max).then_inc(s_f, 1)
                    e.wait_ge(s_pe, 2)
                    e.tensor_tensor(flag[:, :], upto[:, 1:NT + 1], before_ps[:, 0:NT], ALU.is_gt).then_inc(s_f, 1)
                    e.wait_ge(s_f, 3)
                    e.tensor_scalar(tmp[:, :], flag[:, :], -2.0 * EP, 2.0 * EP, ALU.mult, ALU.add).then_inc(s_f, 1)
                    e.wait_ge(s_f, 4)
                    e.tensor_tensor(start_idx[:, :], tmp[:, :], before_ps[:, 0:NT], ALU.add).then_inc(s_f, 1)
                    e.wait_ge(s_f, 5)

        def dve_layernorm(e, V, it, y, d, sq, s1, s2, out, y_step, act, out_free=lambda: None):
            V.wait(e, y_step, it)
            V.give(e.tensor_reduce(s1[:, :], y, AX_X, ALU.add), "ln_sum")
            V.wait(e, "ln_sum", it)
            V.give(e.tensor_scalar(s1[:, :], s1[:, :], 1.0 / D, None, ALU.mult), "ln_mean")
            V.wait(e, "ln_mean", it)
            V.give(e.tensor_tensor(d, y, s1[:, :].unsqueeze(2).to_broadcast([P, G, D]), ALU.subtract), "ln_cent")
            V.wait(e, "ln_cent", it)
            V.give(e.tensor_tensor(sq, d, d, ALU.mult), "ln_sq")
            V.wait(e, "ln_sq", it)
            V.give(e.tensor_reduce(s2[:, :], sq, AX_X, ALU.add), "ln_var")
            act.wait(e, "ln_std", it)
            V.give(e.reciprocal(s1[:, :], s2[:, :]), "ln_rstd")
            V.wait(e, "ln_rstd", it)
            out_free()
            V.give(e.tensor_tensor(out, d, s1[:, :].unsqueeze(2).to_broadcast([P, G, D]), ALU.mult), "ln_out")
            V.wait(e, "ln_out", it)

        LN = ["ln_sum", "ln_mean", "ln_cent", "ln_sq", "ln_var", "ln_rstd", "ln_out"]

        def act_std(e, A, V, it, s2):
            V.wait(e, "ln_var", it)
            A.give(e.activation(s2[:, :], s2[:, :], ACT.Sqrt, bias=eps_col[:, 0:1], scale=1.0 / D), "ln_std")

        def pe_transpose_group(e, T, TP, src, it, name):
            for g in range(G):
                ins = e.transpose(TP[0:D, g * P:(g + 1) * P], src[:, g, :], ident[:, :])
            T.give(ins, name)

        with Phase("rank") as ph:
            zero = ph.sb("zero", [P, TROW // P * PAY])
            dst_t = ph.sb("dst_t", [P, NTL], I32)
            prev_t = ph.sb("prev_t", [P, NTL], I32)
            begin = ph.sb("begin", [P, NTL], BF16)
            upto_m = ph.sb("upto_m", [P, P], BF16)
            before_m = ph.sb("before_m", [P, P])
            one_b = ph.sb("one_b", [P, 1], BF16)
            one_f = ph.sb("one_f", [P, 1])
            rel_f = ph.sb("rel_f", [P, NTL])
            rel_t = ph.sb("rel_t", [P, -(-NTL // P), P], BF16)
            cnt = ph.sb("cnt", [1, NTL])
            ones_row = ph.sb("ones_row", [1, NTL])
            incl = ph.sb("incl", [1, NTL])
            first = ph.sb("first", [1, NTL])
            tot = ph.sb("tot", [1, NT])
            toti = ph.sb("toti", [1, NT])
            rank_f = ph.sb("rank_f", [P, NT])
            rank_g = ph.sb("rank_g", [P, NT])
            CR = ph.ps("CR", [P, 4, 512])
            RT = [ph.ps(f"RT{i}", [P, 512]) for i in range(2)]
            NS = ph.ps("NS", [P, 512])
            s_ld, s_z, s_zd, s_p, s_v, s_t, s_o, s_a = (ph.sem(n) for n in ("ld", "z", "zd", "p", "v", "t", "o", "a"))
            NGR = -(-NTL // P)
            pieces = [(a, min(a + 512, NTL)) for a in range(0, NTL, 512)]
            with nc.Block() as block:
                @block.sync
                def _(e):
                    e.dma_start(dst_t[:, :], t["dst_tcols"]).then_inc(s_ld, 16)
                    e.dma_start(prev_t[:, :], t["prev_tcols"]).then_inc(s_ld, 16)
                    e.wait_ge(s_z, 1)
                    zeroed = [(tab.rearrange("(p r) d -> p (r d)", p=P), TROW // P * PAY) for tab in sum_tab]
                    half = TROW // P * D
                    kvz = kv_used.rearrange("(p r) d -> p (r d)", p=P)
                    zeroed += [(kvz[:, 0:half], half), (kvz[:, half:2 * half], half),
                               (adst_lin.rearrange("(p r) d -> p (r d)", p=P), EC)]
                    for dst, n in zeroed:
                        e.dma_start(dst, zero[:, 0:n]).then_inc(s_zd, 16)
                    e.wait_ge(s_a, NGR)
                    full = NTL // P
                    if full:
                        e.dma_start(rel_row[0:full * P * P].rearrange("(g t e) -> t g e", t=P, e=P), rel_t[:, 0:full, :]).then_inc(s_o, 16)
                    if NTL % P:
                        e.dma_start(rel_row[full * P * P:].rearrange("(t e) -> t e", e=P), rel_t[0:NTL % P, full, :]).then_inc(s_o, 16)
                    e.wait_ge(s_o, 16 * ((1 if full else 0) + (1 if NTL % P else 0)))
                    e.wait_ge(s_zd, 16 * len(zeroed))

                @block.gpsimd
                def _(e):
                    e.memset(zero[:, :], 0.0).then_inc(s_z, 1)
                    e.memset(upto_m[:, :], 1.0).then_inc(s_p, 1)
                    e.memset(before_m[:, :], 1.0).then_inc(s_p, 1)
                    e.wait_ge(s_p, 2)
                    e.affine_select(out=upto_m[:, :], in_=upto_m[:, :], compare_op=ALU.is_ge, fill=0.0, base=0,
                                    pattern=[[1, P]], channel_multiplier=-1).then_inc(s_p, 1)
                    e.affine_select(out=before_m[:, :], in_=before_m[:, :], compare_op=ALU.is_gt, fill=0.0, base=0,
                                    pattern=[[1, P]], channel_multiplier=-1).then_inc(s_p, 1)
                    e.wait_ge(s_p, 4)
                    e.memset(upto_m[0:1, :], 0.0).then_inc(s_p, 1)
                    e.wait_ge(s_p, 5)

                @block.vector
                def _(e):
                    n = [0]

                    def then(ins):
                        n[0] += 1
                        ins.then_inc(s_v, 1)
                        e.wait_ge(s_v, n[0])
                    then(e.memset(one_b[:, :], 1.0))
                    then(e.memset(one_f[:, :], 1.0))
                    then(e.memset(ones_row[:, :], 1.0))
                    e.wait_ge(s_ld, 32)
                    then(e.tensor_tensor(begin[:, :], dst_t[:, :], prev_t[:, :], ALU.not_equal))
                    then(e.tensor_copy(first[:, :], begin[0:1, :]))
                    e.wait_ge(s_t, 1)
                    then(e.tensor_copy(cnt[:, :], CR[0:1, :, :].rearrange("p a b -> p (a b)")[:, 0:NTL]))
                    then(e.tensor_tensor_scan(incl[:, :], ones_row[:, :], cnt[:, :], 0.0, ALU.mult, ALU.add))
                    then(e.tensor_tensor(incl[:, :], incl[:, :], cnt[:, :], ALU.subtract))
                    then(e.tensor_tensor(incl[:, :], incl[:, :], first[:, :], ALU.add))
                    then(e.tensor_scalar(win_row[:, :], incl[:, :], -1.0, None, ALU.add))
                    e.wait_ge(s_t, 2)
                    then(e.tensor_copy(rel_f[:, :], CR[:, :, :].rearrange("p a b -> p (a b)")[:, 0:NTL]))
                    then(e.tensor_copy(tot[:, :], NS[0:1, 0:NT]))
                    then(e.tensor_tensor_scan(toti[:, :], ones_row[:, 0:NT], tot[:, :], 0.0, ALU.mult, ALU.add))
                    then(e.tensor_tensor(toti[:, :], toti[:, :], tot[:, :], ALU.subtract))
                    then(e.tensor_copy(rank_f[:, :], NS[:, 64:64 + NT]))
                    then(e.tensor_scalar(rank_g[:, :], flag[:, :], -4.0 * NROW, 4.0 * NROW, ALU.mult, ALU.add))
                    then(e.tensor_tensor(rank_f[:, :], rank_f[:, :], rank_g[:, :], ALU.add))
                    e.wait_ge(s_t, 3)
                    then(e.tensor_tensor(used_idx[:, :], NS[:, 128:128 + NT], rank_f[:, :], ALU.add))

                @block.tensor
                def _(e):
                    e.wait_ge(s_v, 4)
                    for i, (a, b) in enumerate(pieces):
                        ins = e.matmul(CR[0:1, i, 0:b - a], one_b[:, :], begin[:, a:b], start=True, stop=True)
                    ins.then_inc(s_t, 1)
                    e.wait_ge(s_p, 5)
                    e.matmul(NS[0:1, 0:NT], one_f[:, :], flag[:, :], start=True, stop=True)
                    e.matmul(NS[:, 64:64 + NT], before_m[:, :], flag[:, :], start=True, stop=True)
                    e.wait_ge(s_v, 6)
                    for i, (a, b) in enumerate(pieces):
                        ins = e.matmul(CR[:, i, 0:b - a], upto_m[:, :], begin[:, a:b], start=True, stop=True)
                    ins.then_inc(s_t, 1)
                    e.wait_ge(s_v, 15)
                    e.matmul(NS[:, 128:128 + NT], ones_f[:, :], toti[:, :], start=True, stop=True).then_inc(s_t, 1)
                    for g in range(NGR):
                        if g >= 2:
                            e.wait_ge(s_a, g - 1)
                        w = min(P, NTL - g * P)
                        e.transpose(RT[g % 2][0:w, 0:P], rel_f[:, g * P:g * P + w], ident[:, :]).then_inc(s_t, 1)

                @block.scalar
                def _(e):
                    for g in range(NGR):
                        w = min(P, NTL - g * P)
                        e.wait_ge(s_t, 4 + g)
                        e.activation(rel_t[0:w, g, :], RT[g % 2][0:w, 0:P], ACT.Copy).then_inc(s_a, 1)

        with Phase("n1") as ph:
            xg = ph.sb("xg", [P, G, D])
            xT = ph.sb("xT", [D, G * P])
            q_rows = ph.sb("q_rows", [P, G, D])
            kv_rows = ph.sb("kv_rows", [P, G, 2 * D])
            tab = [q_rows[:, :, :], kv_rows[:, :, 0:D], kv_rows[:, :, D:2 * D]]
            used_g = ph.sb("used_g", [P, G], I32)
            s_kv = ph.sem("kv")
            TP = ph.ps("TP", [P, 1024])
            O = [ph.ps(f"O{i}", [P, 2, 512]) for i in range(3)]
            V = ph.steps("V", ["xg", "used"])
            T = ph.steps("T", ["tr", "mm0", "mm1", "mm2"])
            A = ph.steps("A", ["xT", "o0", "o1", "o2"])
            s_o = ph.sem("o")
            with nc.Block() as block:
                @block.vector
                def _(e):
                    def body(it):
                        T.wait(e, "tr", it, 1)
                        V.give(e.tensor_scalar(xg[:, :, :], X[:, bass.ds(it * G, G), :], 1.0, None, ALU.mult), "xg")
                        wait_count(e, s_kv, it, 16 * G, 0)
                        V.give(e.tensor_scalar(used_g[:, :], used_idx[:, bass.ds(it * G, G)], 1.0, None, ALU.mult), "used")
                    loop(e, NG, body)

                @block.tensor
                def _(e):
                    def body(it):
                        V.wait(e, "xg", it)
                        A.wait(e, "xT", it, 1)
                        pe_transpose_group(e, T, TP, xg, it, "tr")
                        A.wait(e, "xT", it)
                        for i, n in enumerate(("qW", "kW", "vW")):
                            for g in range(G):
                                ins = e.matmul(O[i][:, g // 4, (g % 4) * P:(g % 4) * P + D], xT[:, g * P:(g + 1) * P],
                                               w96[n][:, :], start=True, stop=True)
                            T.give(ins, f"mm{i}")
                    loop(e, NG, body)

                @block.scalar
                def _(e):
                    def body(it):
                        T.wait(e, "tr", it)
                        A.give(e.activation(xT[:, :], TP[0:D, 0:G * P], ACT.Copy), "xT")
                        for i in range(3):
                            T.wait(e, f"mm{i}", it)
                            if i == 0:
                                wait_count(e, s_o, it, 16, 0)
                            if i == 1:
                                wait_count(e, s_kv, it, 16 * G, 0)
                            e.activation(tab[i][:, 0:4, :], O[i][:, 0, :].rearrange("p (g c) -> p g c", c=P)[:, :, 0:D], ACT.Copy)
                            A.give(e.activation(tab[i][:, 4:G, :], O[i][:, 1, :].rearrange("p (g c) -> p g c", c=P)[:, 0:G - 4, 0:D], ACT.Copy), f"o{i}")
                    loop(e, NG, body)

                @block.sync
                def _(e):
                    def body(it):
                        A.wait(e, "o0", it)
                        e.dma_start(q_tab[bass.ds(it * (G * P), G * P), :].rearrange("(g p) d -> p g d", p=P), q_rows[:, :, :]).then_inc(s_o, 16)
                    loop(e, NG, body)
                    e.wait_ge(s_o, 16 * NG)

                @block.gpsimd
                def _(e):
                    def body(it):
                        A.wait(e, "o2", it)
                        V.wait(e, "used", it)
                        for g in range(G):
                            e.indirect_dma_start(kv_used, bass.IndirectOffsetOnAxis(used_g[:, g:g + 1], axis=0), kv_rows[:, g, :], None,
                                                 bounds_check=TROW - 1, oob_is_err=False).then_inc(s_kv, 16)
                    loop(e, NG, body)
                    e.wait_ge(s_kv, 16 * G * NG)

        with Phase("e0") as ph:
            NI = NCH // LANES
            two = range(LANES)
            src_i = [ph.sb(f"src_i{s}", [P, K], I32) for s in two]
            src_bc = [ph.sb(f"src_bc{s}", [P, K, P], I32) for s in two]
            src_f = [ph.sb(f"src_f{s}", [P, K]) for s in two]
            rel = [ph.sb(f"rel{s}", [1, CH], BF16) for s in two]
            window = [ph.sb(f"window{s}", [P, K, 2 * D]) for s in two]
            pick = [ph.sb(f"pick{s}", [P, K, P]) for s in two]
            qg = [ph.sb(f"qg{s}", [P, K, D]) for s in two]
            prod = [ph.sb(f"prod{s}", [P, K, D]) for s in two]
            score = [ph.sb(f"score{s}", [P, K, HEADS]) for s in two]
            pay = [ph.sb(f"pay{s}", [P, K, PAY]) for s in two]
            same = [ph.sb(f"same{s}", [P, K, P]) for s in two]
            junk = [ph.sb(f"junk{s}", [P, K, P]) for s in two]
            dup = [ph.sb(f"dup{s}", [P, K]) for s in two]
            away = [ph.sb(f"away{s}", [P, K]) for s in two]
            srow = [ph.sb(f"srow{s}", [P, K], I32) for s in two]
            comb = [ph.sb(f"comb{s}", [P, K, PAY]) for s in two]
            C = [ph.ps(f"C{s}", [P, 512]) for s in two]
            Z = [ph.ps(f"Z{s}", [P, CH]) for s in two]
            KV = [ph.ps(f"KV{s}", [P, K, 256]) for s in two]
            s_ix = ph.sem("ix")
            s_ld = [ph.sem(f"ld{s}") for s in two]
            s_w = [ph.sem(f"w{s}") for s in two]
            s_g = [ph.sem(f"g{s}") for s in two]
            s_tab = [ph.sem(f"tab{j}") for j in range(NTAB)]
            V = [ph.steps(f"V{s}", ["pick", "eq", "srcf", "dup", "away", "f", "mul", "row", "prod", "red", "clip", "pay"]) for s in two]
            A = [ph.steps(f"A{s}", ["exp", "comb"]) for s in two]
            T = [ph.steps(f"T{s}", ["bc", "kv", "mm"]) for s in two]
            src_r = t["src_pad"].rearrange("(c e) -> c e", e=CH)
            rel_r = rel_row.rearrange("(c e) -> c e", e=CH)
            with nc.Block() as block:
                @block.sync
                def _(e):
                    def body(it):
                        for s in two:
                            c = it * LANES + s
                            T[s].wait(e, "bc", it, 1)
                            e.dma_start(rel[s][:, :], rel_r[bass.ds(c, 1)]).then_inc(s_ld[s], 16)
                            V[s].wait(e, "eq", it, 1)
                            e.dma_start(src_bc[s][:, :, :].rearrange("p k e -> p (k e)"), src_r[bass.ds(c, 1)].to_broadcast([P, CH])).then_inc(s_ld[s], 16)
                    loop(e, NI, body)

                @block.gpsimd
                def _(e):
                    def scatter(s, it, back):
                        A[s].wait(e, "comb", it, back)
                        for k in range(K):
                            wait_count(e, s_tab[k], it, 16 * LANES, 16 * (s - LANES * back))
                            e.indirect_dma_start(sum_tab[k], bass.IndirectOffsetOnAxis(srow[s][:, k:k + 1], axis=0),
                                                 comb[s][:, k, :], None, bounds_check=TROW - 1, oob_is_err=True,
                                                 compute_op=ALU.add).then_inc(s_tab[k], 16)

                    def body(it):
                        for s in two:
                            wait_count(e, s_ix, it, LANES, s + 1)
                            V[s].wait(e, "prod", it, 1)
                            for k in range(K):
                                e.indirect_dma_start(qg[s][:, k, :], None, q_tab,
                                                     bass.IndirectOffsetOnAxis(src_i[s][:, k:k + 1], axis=0),
                                                     bounds_check=NROW - 1, oob_is_err=False).then_inc(s_g[s], 16)
                            if s == 1:
                                scatter(0, it, 0)
                            elif not isinstance(it, int) or it > 0:
                                scatter(1, it, 1)
                    loop(e, NI, body, apart=2)
                    scatter(1, NI, 1)
                    for j in range(NTAB):
                        e.wait_ge(s_tab[j], 16 * NCH)

                @block.vector
                def _(e):
                    e.tensor_scalar(src_i[0][:, :], src_tcols[:, 0:K], 1.0, None, ALU.mult).then_inc(s_ix, 1)
                    e.tensor_scalar(src_i[1][:, :], src_tcols[:, K:2 * K], 1.0, None, ALU.mult).then_inc(s_ix, 1)

                    def body(it):
                        for s in two:
                            W = V[s]
                            T[s].wait(e, "bc", it)
                            W.give(e.tensor_scalar(pick[s][:, :, :].rearrange("p k e -> p (k e)"), Z[s][:, :], part_col[:, 0:1], None, ALU.is_equal), "pick")
                            wait_count(e, s_ld[s], it, 32, 32)
                            T[s].wait(e, "mm", it, 1)
                            W.give(e.tensor_tensor(same[s][:, :, :], src_bc[s][:, :, :],
                                                   src_tcols[:, bass.ds((it * LANES + s) * K, K)].unsqueeze(2).to_broadcast([P, K, P]), ALU.is_equal), "eq")
                            W.give(e.tensor_scalar(src_f[s][:, :], src_tcols[:, bass.ds((it * LANES + s) * K, K)], 1.0, None, ALU.mult), "srcf")
                            W.wait(e, "srcf", it)
                            for k in range(K):
                                ins = e.scalar_tensor_tensor(junk[s][:, k, :], same[s][:, k, :], 1.0, tri[:, :], ALU.mult, ALU.mult,
                                                             accum_out=dup[s][:, k:k + 1])
                            W.give(ins, "dup")
                            W.give(e.tensor_scalar(away[s][:, :], src_f[s][:, :], -1.0, dump_col[:, 0:1], ALU.mult, ALU.add), "away")
                            W.wait(e, "away", it)
                            W.give(e.tensor_scalar(dup[s][:, :], dup[s][:, :], 1.0, None, ALU.min), "f")
                            W.wait(e, "f", it)
                            W.give(e.tensor_tensor(away[s][:, :], away[s][:, :], dup[s][:, :], ALU.mult), "mul")
                            W.wait(e, "mul", it)
                            for k in range(K):
                                wait_count(e, s_tab[k], it, 16 * LANES, 16 * (s + 1 - LANES))
                            W.give(e.tensor_tensor(srow[s][:, :], src_f[s][:, :], away[s][:, :], ALU.add), "row")
                            T[s].wait(e, "kv", it)
                            wait_count(e, s_g[s], it, 16 * K, 16 * K)
                            W.give(e.tensor_tensor(prod[s][:, :, :], KV[s][:, :, 0:D], qg[s][:, :, :], ALU.mult), "prod")
                            if last_ahead(it, s):
                                e.tensor_scalar(src_i[s][:, :], src_tcols[:, bass.ds((it * LANES + s + 2) * K, K)], 1.0, None, ALU.mult).then_inc(s_ix, 1)
                            W.wait(e, "prod", it)
                            W.give(e.tensor_reduce(score[s][:, :, :], prod[s][:, :, :].rearrange("p k (h d) -> p k h d", h=HEADS),
                                                   AX_X, ALU.add), "red")
                            W.wait(e, "red", it)
                            W.give(e.tensor_scalar(score[s][:, :, :], score[s][:, :, :], -10.0, 10.0, ALU.max, ALU.min), "clip")
                            A[s].wait(e, "exp", it)
                            W.give(e.tensor_tensor(pay[s][:, :, 0:D].rearrange("p k (h d) -> p k h d", h=HEADS),
                                                   KV[s][:, :, D:2 * D].rearrange("p k (h d) -> p k h d", h=HEADS),
                                                   pay[s][:, :, D:PAY].unsqueeze(3).to_broadcast([P, K, HEADS, DH]), ALU.mult), "pay")

                    def last_ahead(it, s):
                        return not isinstance(it, int) or it < NI - 1
                    loop(e, NI, body, last_apart=True)

                @block.scalar
                def _(e):
                    def windows(it, s, free):
                        free()
                        for k in range(K):
                            row = e.value_load(win_row[0:1, bass.ds((it * LANES + s) * K + k, 1)], min_val=0, max_val=TROW - P)
                            e.dma_start(window[s][:, k, :], kv_used[bass.ds(row, P), :]).then_inc(s_w[s], 16)

                    def body(it):
                        for s in two:
                            if s == 0:
                                windows(it, 1, lambda: T[1].wait(e, "kv", it, 1))
                            elif not isinstance(it, int) or it < NI - 1:
                                windows(it + 1, 0, lambda: T[0].wait(e, "kv", it))
                            V[s].wait(e, "clip", it)
                            T[s].wait(e, "mm", it, 1)
                            A[s].give(e.activation(pay[s][:, :, D:PAY], score[s][:, :, :], ACT.Exp), "exp")
                            T[s].wait(e, "mm", it)
                            for k in range(K):
                                wait_count(e, s_tab[k], it, 16 * LANES, 16 * (s + 1 - LANES))
                            A[s].give(e.activation(comb[s][:, :, :], C[s][:, 0:K * PAY].rearrange("p (k c) -> p k c", k=K), ACT.Copy), "comb")
                    windows(0, 0, lambda: None)
                    loop(e, NI, body, last_apart=True)

                @block.tensor
                def _(e):
                    def body(it):
                        for s in two:
                            wait_count(e, s_ld[s], it, 32, 32)
                            V[s].wait(e, "pick", it, 1)
                            T[s].give(e.matmul(Z[s][:, :], ones_b[:, :], rel[s][:, :], start=True, stop=True), "bc")
                            V[s].wait(e, "pick", it)
                            wait_count(e, s_w[s], it, 16 * K, 16 * K)
                            for k in range(K):
                                ins = e.matmul(KV[s][:, k, 0:2 * D], pick[s][:, k, :], window[s][:, k, :], start=True, stop=True)
                            T[s].give(ins, "kv")
                            V[s].wait(e, "pay", it)
                            A[s].wait(e, "comb", it, 1)
                            for k in range(K):
                                ins = e.matmul(C[s][:, k * PAY:(k + 1) * PAY], same[s][:, k, :], pay[s][:, k, :], start=True, stop=True)
                            T[s].give(ins, "mm")
                    loop(e, NI, body)

        with Phase("n2") as ph:
            part = [ph.sb(f"part{j}", [P, G, PAY]) for j in range(NTAB)]
            acc = ph.sb("acc", [P, G, PAY])
            den = ph.sb("den", [P, G, HEADS])
            y = ph.sb("y", [P, G, D])
            d = ph.sb("d", [P, G, D])
            sq = ph.sb("sq", [P, G, D])
            s1, s2 = ph.sb("s1", [P, G]), ph.sb("s2", [P, G])
            xo = ph.sb("xo", [P, G, D])
            V = ph.steps("V", [f"add{j}" for j in range(1, NTAB)] + ["den", "rden", "res", "x2", "y"] + LN + ["keep"])
            A = ph.steps("A", ["ln_std"])
            s_ld, s_o = [ph.sem(f"ld{j}") for j in range(NTAB)], ph.sem("o")
            with nc.Block() as block:
                @block.sync
                def _(e):
                    def body(it):
                        for j in range(NTAB):
                            V.wait(e, f"add{max(j, 1)}", it, 1)
                            e.dma_start(part[j][:, :, :], sum_tab[j][bass.ds(it * (G * P), G * P), :].rearrange("(g p) d -> p g d", p=P)).then_inc(s_ld[j], 16)
                    loop(e, NG, body)

                @block.vector
                def _(e):
                    def body(it):
                        wait_count(e, s_ld[0], it, 16, 16)
                        for j in range(1, NTAB):
                            wait_count(e, s_ld[j], it, 16, 16)
                            a = part[0] if j == 1 else acc
                            if j > 1:
                                V.wait(e, f"add{j - 1}", it)
                            V.give(e.tensor_tensor(acc[:, :, :], a[:, :, :], part[j][:, :, :], ALU.add), f"add{j}")
                        V.wait(e, f"add{NTAB - 1}", it)
                        V.give(e.tensor_scalar(den[:, :, :], acc[:, :, D:PAY], 1e-8, None, ALU.add), "den")
                        V.wait(e, "den", it)
                        V.give(e.reciprocal(den[:, :, :], den[:, :, :]), "rden")
                        V.wait(e, "rden", it)
                        V.give(e.tensor_tensor(y[:, :, :].rearrange("p g (h d) -> p g h d", h=HEADS),
                                               acc[:, :, 0:D].rearrange("p g (h d) -> p g h d", h=HEADS),
                                               den[:, :, :].unsqueeze(3).to_broadcast([P, G, HEADS, DH]), ALU.mult), "res")
                        V.wait(e, "res", it)
                        V.give(e.tensor_tensor(y[:, :, :], y[:, :, :], X[:, bass.ds(it * G, G), :], ALU.add), "x2")
                        V.wait(e, "x2", it)
                        V.give(e.tensor_tensor(y[:, :, :], y[:, :, :], X[:, bass.ds(it * G, G), :], ALU.add), "y")
                        wait_count(e, s_o, it, 16, 0)
                        dve_layernorm(e, V, it, y[:, :, :], d[:, :, :], sq[:, :, :], s1, s2, xo[:, :, :], "y", A)
                        V.give(e.tensor_scalar(X[:, bass.ds(it * G, G), :], xo[:, :, :], 1.0, None, ALU.mult), "keep")
                    loop(e, NG, body)

                @block.scalar
                def _(e):
                    def body(it):
                        act_std(e, A, V, it, s2)
                        V.wait(e, "ln_out", it)
                        e.dma_start(x_tab[bass.ds(it * (G * P), G * P), :].rearrange("(g p) d -> p g d", p=P), xo[:, :, :]).then_inc(s_o, 16)
                    loop(e, NG, body)
                    e.wait_ge(s_o, 16 * NG)

        def edge_pass(name, func, mask_row, op0, op1, edge_w):
            with Phase(name, edge=True) as ph:
                NI = NCH // U

                def turn_back_last(e, part):
                    part(NI, 0)
                idx = [ph.sb(f"idx{u}", [P, K], I32) for u in range(U)]
                got = [ph.sb(f"got{u}", [P, K, D]) for u in range(U)]
                attr = [ph.sb(f"attr{u}", [DE + 1, CH]) for u in range(U)]
                mask = [ph.sb(f"mask{u}", [1, CH], BF16) for u in range(U)]
                emsg = [ph.sb(f"emsg{s}", [P, K, D]) for s in range(2)]
                msg = [ph.sb(f"msg{s}", [D, CH]) for s in range(2)]
                run = [ph.sb(f"run{s}", [D, CH]) for s in range(2)]
                out = [ph.sb(f"out{u}", [P, K, D]) for u in range(U)]
                EA = [ph.ps(f"EA{s}", [P, CH]) for s in range(2)]
                M = [ph.ps(f"M{s}", [P, CH]) for s in range(2)]
                Z = [ph.ps(f"Z{s}", [P, CH]) for s in range(2)]
                B = [ph.ps(f"B{s}", [P, CH]) for s in range(2)]
                s_ix = ph.sem("ix")
                s_init = ph.sem("init")
                s_ld = [ph.sem(f"ld{u}") for u in range(U)]
                s_g = [ph.sem(f"g{u}") for u in range(U)]
                s_st = [ph.sem(f"st{u}") for u in range(U)]
                T = [ph.steps(f"T{u}", ["attr", "fwd", "back"]) for u in range(U)]
                A = [ph.steps(f"A{u}", ["msg", "out"]) for u in range(U)]
                V = [ph.steps(f"V{u}", ["add", "scan"]) for u in range(U)]
                mask_c = mask_row.rearrange("(c e) -> c e", e=CH)
                out_c = scan_out.rearrange("(c p k) d -> c p (k d)", p=P, k=K)
                with nc.Block() as block:
                    @block.sync
                    def _(e):
                        def store(it, u, lag):
                            v, back = behind(u, lag)
                            A[v].wait(e, "out", it, back)
                            e.dma_start(out_c[bass.ds(it * U + (u - lag), 1)].rearrange("a p x -> (a p) x"),
                                        out[v][:, :, :].rearrange("p k d -> p (k d)")).then_inc(s_st[v], 16)

                        def step(it, u):
                            c = it * U + u
                            T[u].wait(e, "fwd", it, 1)
                            e.dma_start(mask[u][:, :], mask_c[bass.ds(c, 1)]).then_inc(s_ld[u], 16)
                            e.dma_start(attr[u][:, :], t["attr_T"][:, bass.ds(c * CH, CH)]).then_inc(s_ld[u], 16)
                            if started(it, u, U - 1):
                                store(it, u, U - 1)
                        loop(e, NI, lambda it: [step(it, u) for u in range(U)])
                        for lag in range(U - 2, -1, -1):
                            store(NI - 1, U - 1, lag)
                        for u in range(U):
                            e.wait_ge(s_st[u], 16 * NI)

                    @block.gpsimd
                    def _(e):
                        def step(it, u):
                            wait_count(e, s_ix, it, U, u + 1)
                            V[u].wait(e, "add", it, 1)
                            for k in range(K):
                                e.indirect_dma_start(got[u][:, k, :], None, x_tab,
                                                     bass.IndirectOffsetOnAxis(idx[u][:, k:k + 1], axis=0),
                                                     bounds_check=NROW - 1, oob_is_err=False).then_inc(s_g[u], 16)
                        loop(e, NI, lambda it: [step(it, u) for u in range(U)])

                    @block.tensor
                    def _(e):
                        def turn_back(it, u):
                            v, back = behind(u, 1)
                            V[v].wait(e, "scan", it, back)
                            w, back2 = behind(u, 3)
                            A[w].wait(e, "out", it, back2)
                            for k in range(K):
                                ins = e.transpose(B[v % 2][:, k * D:(k + 1) * D], run[v % 2][:, k::K], ident[0:D, 0:D])
                            T[v].give(ins, "back")

                        def attributes(it, u, free):
                            wait_count(e, s_ld[u], it, 32, 32)
                            free()
                            for k in range(K):
                                ins = e.matmul(EA[u % 2][:, k * D:(k + 1) * D], attr[u][:, k::K], edge_w[:, :], start=True, stop=True)
                            T[u].give(ins, "attr")

                        def step(it, u):
                            s = u % 2
                            v, back = behind(u, 2)
                            w, back1 = behind(u, 1)
                            if u + 1 < U:
                                attributes(it, u + 1, lambda: V[w].wait(e, "add", it, back1))
                            elif not isinstance(it, int) or it + 1 < NI:
                                attributes(it + 1, 0, lambda: V[w].wait(e, "add", it, back1))
                            V[v].wait(e, "scan", it, back)
                            e.matmul(Z[s][0:D, :], ones_b[:, 0:D], mask[u][:, :], start=True, stop=True)
                            V[u].wait(e, "add", it)
                            A[v].wait(e, "msg", it, back)
                            for k in range(K):
                                ins = e.transpose(M[s][0:D, k::K], emsg[s][:, k, :], ident[:, :])
                            T[u].give(ins, "fwd")
                            if started(it, u, 1):
                                turn_back(it, u)
                        attributes(0, 0, lambda: None)
                        loop(e, NI, lambda it: [step(it, u) for u in range(U)], last_apart=True)
                        turn_back_last(e, turn_back)

                    @block.vector
                    def _(e):
                        e.memset(run[1][:, :], 0.0).then_inc(s_init, 1)
                        for u in range(2):
                            e.tensor_scalar(idx[u][:, :], src_cols[:, u * K:(u + 1) * K], 1.0, None, ALU.mult).then_inc(s_ix, 1)
                        e.wait_ge(s_init, 1)

                        def scan(it, u):
                            v, back = behind(u, 1)
                            w, back2 = behind(u, 2)
                            x, back3 = behind(u, 3)
                            A[v].wait(e, "msg", it, back)
                            T[v].wait(e, "fwd", it, back)
                            V[w].wait(e, "scan", it, back2)
                            T[x].wait(e, "back", it, back3)
                            p, q = v % 2, w % 2
                            V[v].give(e.tensor_tensor_scan(run[p][:, :], Z[p][0:D, :], msg[p][:, :], run[q][:, CH - 1:CH], op0, op1), "scan")

                        def step(it, u):
                            s = u % 2
                            v, back = behind(u, 2)
                            e.tensor_scalar(idx[(u + 2) % U][:, :], src_cols[:, bass.ds((it * U + u + 2) * K, K)], 1.0, None, ALU.mult).then_inc(s_ix, 1)
                            T[u].wait(e, "attr", it)
                            wait_count(e, s_g[u], it, 16 * K, 16 * K)
                            T[v].wait(e, "fwd", it, back)
                            V[u].give(e.tensor_tensor(emsg[s][:, :, :], EA[s][:, 0:K * D].rearrange("p (k d) -> p k d", k=K),
                                                      got[u][:, :, :], ALU.add), "add")
                            if started(it, u, 1):
                                scan(it, u)
                        loop(e, NI, lambda it: [step(it, u) for u in range(U)])
                        turn_back_last(e, scan)

                    @block.scalar
                    def _(e):
                        def to_out(it, u):
                            v, back = behind(u, 1)
                            T[v].wait(e, "back", it, back)
                            wait_stored(e, s_st[v], it, back)
                            A[v].give(e.activation(out[v][:, :, :], B[v % 2][:, 0:K * D].rearrange("p (k d) -> p k d", k=K), ACT.Copy), "out")

                        def step(it, u):
                            v, back = behind(u, 2)
                            T[u].wait(e, "fwd", it)
                            V[v].wait(e, "scan", it, back)
                            A[u].give(e.activation(msg[u % 2][:, :], M[u % 2][0:D, :], func), "msg")
                            if started(it, u, 1):
                                to_out(it, u)
                        loop(e, NI, lambda it: [step(it, u) for u in range(U)], apart=2)
                        turn_back_last(e, to_out)

        def pool_gather_ends(e, E, ends, V, parts, sem):
            def body(it):
                E.wait(e, "ends", it)
                for dst, lin, used in parts:
                    V.wait(e, used, it, 1)
                    for g in range(G):
                        e.indirect_dma_start(dst[:, g, :], None, lin, bass.IndirectOffsetOnAxis(ends[:, g:g + 1], axis=0),
                                             bounds_check=EP - 1, oob_is_err=False).then_inc(sem, 16)
            loop(e, NG, body)

        def first_ends(e, E, ends):
            E.give(e.tensor_scalar(ends[:, :], end_idx[:, 0:G], 1.0, None, ALU.mult), "ends")

        def next_ends(e, E, ends, it):
            E.give(e.tensor_scalar(ends[:, :], end_idx[:, bass.ds(it * G + G, G)], 1.0, None, ALU.mult), "ends")

        edge_pass("e1", ACT.Relu, keep_row, ALU.mult, ALU.add, we["We"])

        class Projection:

            def __init__(self, ph, w_msg, w_root, bias_row, O=None):
                self.w, self.bias_row = (w_msg, w_root), bias_row
                self.xT = ph.sb("proj_xT", [D, G * P])
                self.tab = ph.sb("proj_tab", [P, G, D])
                self.TP = ph.ps("proj_TP", [P, 1024])
                self.O = O or [ph.ps(f"proj_O{i}", [P, 1024]) for i in range(2)]
                self.V = ph.steps("proj_V", ["root"])
                self.T = ph.steps("proj_T", ["tr", "mm0", "mm1"])
                self.A = ph.steps("proj_A", ["xT", "tab"])
                self.stored = ph.sem("proj_o")

            def tensor(self, e, it, src, src_ready):
                src_ready(it)
                self.A.wait(e, "xT", it, 1)
                pe_transpose_group(e, self.T, self.TP, src, it, "tr")
                self.A.wait(e, "xT", it)
                for i in range(2):
                    if i == 0:
                        self.A.wait(e, "tab", it, 1)
                    else:
                        self.V.wait(e, "root", it, 1)
                    for g in range(G):
                        ins = e.matmul(self.O[i][:, g * P:g * P + D], self.xT[:, g * P:(g + 1) * P], self.w[i][:, :], start=True, stop=True)
                    self.T.give(ins, f"mm{i}")

            def scalar(self, e, it):
                self.T.wait(e, "tr", it)
                self.A.give(e.activation(self.xT[:, :], self.TP[0:D, 0:G * P], ACT.Copy), "xT")
                self.T.wait(e, "mm0", it)
                wait_count(e, self.stored, it, 16, 0)
                self.A.give(e.activation(self.tab[:, :, :], self.O[0][:, 0:G * P].rearrange("p (g c) -> p g c", c=P)[:, :, 0:D], ACT.Copy), "tab")

            def sync(self, e, it):
                self.A.wait(e, "tab", it)
                e.dma_start(x_tab[bass.ds(it * (G * P), G * P), :].rearrange("(g p) d -> p g d", p=P), self.tab[:, :, :]).then_inc(self.stored, 16)

            def vector(self, e, it, back):
                self.T.wait(e, "mm1", it, back)
                self.V.give(e.tensor_tensor(R[:, bass.ds((it - back) * G, G), :], self.O[1][:, 0:G * P].rearrange("p (g c) -> p g c", c=P)[:, :, 0:D],
                                            self.bias_row[:, :].unsqueeze(1).to_broadcast([P, G, D]), ALU.add), "root")

        with Phase("n3") as ph:
            ends = ph.sb("ends", [P, G], I32)
            agg = ph.sb("agg", [P, G, D])
            h = ph.sb("h", [P, G, D])
            hT = ph.sb("hT", [D, G * P])
            rT = ph.sb("rT", [D, G * P])
            HT = ph.sb("HT", [D, NT * P])
            TP = ph.ps("TP", [P, 1024])
            O1 = ph.ps("O1", [P, 1024])
            O2 = ph.ps("O2", [P, 1024])
            E = ph.steps("E", ["ends"])
            V = ph.steps("V", ["flag", "h"])
            T = ph.steps("T", ["tr", "m1", "m2"])
            A = ph.steps("A", ["hT", "r1", "h2"])
            s_g = ph.sem("g")
            HALF = [(0, 512), (512, G * P)]
            with nc.Block() as block:
                @block.gpsimd
                def _(e):
                    pool_gather_ends(e, E, ends, V, [(agg, scan_out, "flag")], s_g)

                @block.vector
                def _(e):
                    def body(it):
                        wait_count(e, s_g, it, 16 * G, 16 * G)
                        T.wait(e, "tr", it, 1)
                        next_ends(e, E, ends, it)
                        V.give(e.tensor_tensor(h[:, :, :], agg[:, :, :], flag[:, bass.ds(it * G, G)].unsqueeze(2).to_broadcast([P, G, D]), ALU.mult), "flag")
                        V.wait(e, "flag", it)
                        V.give(e.tensor_tensor(h[:, :, :], h[:, :, :], X[:, bass.ds(it * G, G), :], ALU.add), "h")
                    first_ends(e, E, ends)
                    loop(e, NG, body)

                @block.tensor
                def _(e):
                    def body(it):
                        V.wait(e, "h", it)
                        A.wait(e, "hT", it, 1)
                        pe_transpose_group(e, T, TP, h, it, "tr")
                        A.wait(e, "hT", it)
                        for a, b in HALF:
                            ins = e.matmul(O1[0:D, a:b], w96["W1"][:, :], hT[:, a:b], start=True, stop=True)
                        T.give(ins, "m1")
                        A.wait(e, "r1", it)
                        for a, b in HALF:
                            ins = e.matmul(O2[0:D, a:b], w96["W2"][:, :], rT[:, a:b], start=True, stop=True)
                        T.give(ins, "m2")
                    loop(e, NG, body)

                @block.scalar
                def _(e):
                    def body(it):
                        T.wait(e, "tr", it)
                        A.give(e.activation(hT[:, :], TP[0:D, 0:G * P], ACT.Copy), "hT")
                        T.wait(e, "m1", it)
                        A.give(e.activation(rT[:, :], O1[0:D, 0:G * P], ACT.Relu, bias=cols["b1"][:, 0:1]), "r1")
                        T.wait(e, "m2", it)
                        A.give(e.activation(HT[:, bass.ds(it * (G * P), G * P)], O2[0:D, 0:G * P], ACT.Identity, bias=cols["b2"][:, 0:1]), "h2")
                    loop(e, NG, body)

            mean = ph.sb("mean", [D, 1])
            var = ph.sb("var", [D, 1])
            gain = ph.sb("gain", [D, 1])
            shift = ph.sb("shift", [D, 1])
            SQ = ph.sb("SQ", [D, NT * P])
            s_v, s_a = ph.sem("bv"), ph.sem("ba")
            with nc.Block() as block:
                @block.vector
                def _(e):
                    e.tensor_reduce(mean[:, :], HT[:, 0:n_nodes], AX_X, ALU.add).then_inc(s_v, 1)
                    e.wait_ge(s_v, 1)
                    e.tensor_scalar(mean[:, :], mean[:, :], 1.0 / n_nodes, None, ALU.mult).then_inc(s_v, 1)
                    e.wait_ge(s_v, 2)
                    e.tensor_scalar(HT[:, :], HT[:, :], mean[:, 0:1], None, ALU.subtract).then_inc(s_v, 1)
                    e.wait_ge(s_v, 3)
                    e.tensor_tensor(SQ[:, 0:n_nodes], HT[:, 0:n_nodes], HT[:, 0:n_nodes], ALU.mult).then_inc(s_v, 1)
                    e.wait_ge(s_v, 4)
                    e.tensor_reduce(var[:, :], SQ[:, 0:n_nodes], AX_X, ALU.add).then_inc(s_v, 1)
                    e.wait_ge(s_a, 1)
                    e.reciprocal(var[:, :], var[:, :]).then_inc(s_v, 1)
                    e.wait_ge(s_v, 6)
                    e.tensor_tensor(gain[:, :], var[:, :], cols["gamma"][:, :], ALU.mult).then_inc(s_v, 1)
                    e.wait_ge(s_v, 7)

                @block.scalar
                def _(e):
                    e.wait_ge(s_v, 5)
                    e.activation(var[:, :], var[:, :], ACT.Sqrt, bias=eps_col[0:D, 0:1], scale=1.0 / n_nodes).then_inc(s_a, 1)
                    e.wait_ge(s_v, 7)
                    e.activation(SQ[:, :], HT[:, :], ACT.Relu, bias=cols["beta"][:, 0:1], scale=gain[:, 0:1]).then_inc(s_a, 1)
                    e.wait_ge(s_a, 2)

            y_src = ph.sb("y_src", [D, G * P])
            with Phase("n3b") as p2:
                y = p2.sb("y", [P, G, D])
                d = p2.sb("d", [P, G, D])
                sq = p2.sb("sq", [P, G, D])
                x_new = p2.sb("x_new", [P, G, D])
                s1, s2 = p2.sb("s1", [P, G]), p2.sb("s2", [P, G])
                S = p2.steps("S", ["source"])
                V = p2.steps("V", ["y"] + LN + ["keep"])
                A = p2.steps("A", ["ln_std"])
                T = p2.steps("T", ["tr"])
                proj = Projection(p2, w96["W1_msg"], w96["W1_root"], rows["l2b1"], O=[O1, O2])
                with nc.Block() as block:
                    @block.tensor
                    def _(e):
                        def turn(it):
                            S.wait(e, "source", it)
                            V.wait(e, "y", it, 1)
                            for g in range(G):
                                ins = e.transpose(TP[:, g * P:g * P + D], y_src[:, g * P:(g + 1) * P], ident[0:D, 0:D])
                            T.give(ins, "tr")

                        def body(it):
                            if not isinstance(it, int) or it < NG - 1:
                                turn(it + 1)
                            proj.tensor(e, it, x_new, lambda i: V.wait(e, "ln_out", i))
                        turn(0)
                        loop(e, NG, body, last_apart=True)

                    @block.vector
                    def _(e):
                        def source(it):
                            S.give(e.tensor_scalar(y_src[:, :], SQ[:, bass.ds(it * (G * P), G * P)], 1.0, None, ALU.mult), "source")

                        def body(it):
                            T.wait(e, "tr", it)
                            V.give(e.tensor_tensor(y[:, :, :], TP[:, 0:G * P].rearrange("p (g c) -> p g c", c=P)[:, :, 0:D],
                                                   X[:, bass.ds(it * G, G), :], ALU.add), "y")
                            if not isinstance(it, int) or it < NG - 1:
                                source(it + 1)
                            dve_layernorm(e, V, it, y[:, :, :], d[:, :, :], sq[:, :, :], s1, s2, x_new[:, :, :], "y", A,
                                          out_free=lambda: proj.T.wait(e, "tr", it, 1))
                            V.give(e.tensor_scalar(X[:, bass.ds(it * G, G), :], x_new[:, :, :], 1.0, None, ALU.mult), "keep")
                            if not isinstance(it, int) or it > 0:
                                proj.vector(e, it, 1)
                        source(0)
                        loop(e, NG, body, last_apart=True)
                        proj.vector(e, NG, 1)

                    @block.scalar
                    def _(e):
                        loop(e, NG, lambda it: (act_std(e, A, V, it, s2), proj.scalar(e, it)))

                    @block.sync
                    def _(e):
                        loop(e, NG, lambda it: proj.sync(e, it))
                        e.wait_ge(proj.stored, 16 * NG)

        edge_pass("e2a", ACT.Copy, neg_row, ALU.add, ALU.max, we["W1_edge"])

        def dve_conv(e, V, it, agg, both, conv):
            at = bass.ds(it * G, G)
            V.give(e.tensor_tensor(both[:, :, :], agg[:, :, :], flag[:, at].unsqueeze(2).to_broadcast([P, G, D]), ALU.mult), "flag")
            V.wait(e, "flag", it)
            V.give(e.tensor_tensor(both[:, :, :], both[:, :, :], R[:, at, :], ALU.add), "sum")
            V.wait(e, "sum", it)
            V.give(e.scalar_tensor_tensor(conv[:, :, :], both[:, :, :], 0.01, both[:, :, :], ALU.mult, ALU.max), "leaky")

        with Phase("n4") as ph:
            ends = ph.sb("ends", [P, G], I32)
            agg, both, conv = (ph.sb(n, [P, G, D]) for n in ("agg", "both", "conv"))
            E = ph.steps("E", ["ends"])
            V = ph.steps("V", ["flag", "sum", "leaky"])
            s_g = ph.sem("g")
            proj = Projection(ph, w96["W2_msg"], w96["W2_root"], rows["l2b2"])
            with nc.Block() as block:
                @block.gpsimd
                def _(e):
                    pool_gather_ends(e, E, ends, V, [(agg, scan_out, "flag")], s_g)

                @block.vector
                def _(e):
                    def body(it):
                        if not isinstance(it, int) or it > 0:
                            proj.vector(e, it, 1)
                        wait_count(e, s_g, it, 16 * G, 16 * G)
                        next_ends(e, E, ends, it)
                        proj.T.wait(e, "tr", it, 1)
                        dve_conv(e, V, it, agg, both, conv)
                    first_ends(e, E, ends)
                    loop(e, NG, body)
                    proj.vector(e, NG, 1)

                @block.tensor
                def _(e):
                    loop(e, NG, lambda it: proj.tensor(e, it, conv, lambda i: V.wait(e, "leaky", i)))

                @block.scalar
                def _(e):
                    loop(e, NG, lambda it: proj.scalar(e, it))

                @block.sync
                def _(e):
                    loop(e, NG, lambda it: proj.sync(e, it))
                    e.wait_ge(proj.stored, 16 * NG)

        edge_pass("e2b", ACT.Copy, neg_row, ALU.add, ALU.max, we["W2_edge"])

        with Phase("n6") as ph:
            ends = ph.sb("ends", [P, G], I32)
            agg, both, conv, d, sq, x_new = (ph.sb(n, [P, G, D]) for n in ("agg", "both", "conv", "d", "sq", "x_new"))
            s1, s2 = ph.sb("s1", [P, G]), ph.sb("s2", [P, G])
            xT = ph.sb("xT", [D, G * P])
            tab = ph.sb("tab", [P, G, HW])
            pr_src, pr_dst = ph.sb("pr_src", [P, G, D]), ph.sb("pr_dst", [P, G, D])
            starts = ph.sb("starts", [P, G], I32)
            ad = ph.sb("ad", [P, G])
            TP = ph.ps("TP", [P, 1024])
            O = ph.ps("O", [P, 1024])
            E = ph.steps("E", ["ends"])
            V = ph.steps("V", ["flag", "sum", "leaky", "y"] + LN + ["keep"])
            H = ph.steps("H", ["starts", "times_src", "times_dst", "asrc", "adst", "keep_asrc", "keep_adst"])
            T = ph.steps("T", ["tr", "mm"])
            A = ph.steps("A", ["ln_std"])
            AH = ph.steps("AH", ["xT", "h", "keep_h"])
            s_g, s_one, s_o, s_sc = ph.sem("g"), ph.sem("one"), ph.sem("o"), ph.sem("gsc")
            with nc.Block() as block:
                @block.vector
                def _(e):
                    def scores(it, back):
                        at = bass.ds((it - back) * G, G)
                        wait_count(e, s_sc, it, 16 * G, -16 * G * back)
                        H.give(e.tensor_scalar(starts[:, :], start_idx[:, at], 1.0, None, ALU.mult), "starts")
                        AH.wait(e, "h", it, back)
                        H.give(e.tensor_tensor(pr_src[:, :, :], tab[:, :, 0:D], rows["att_src"][:, :].unsqueeze(1).to_broadcast([P, G, D]), ALU.mult), "times_src")
                        H.give(e.tensor_tensor(pr_dst[:, :, :], tab[:, :, 0:D], rows["att_dst"][:, :].unsqueeze(1).to_broadcast([P, G, D]), ALU.mult), "times_dst")
                        H.wait(e, "times_src", it, back)
                        H.give(e.tensor_reduce(tab[:, :, D + 1], pr_src[:, :, :], AX_X, ALU.add), "asrc")
                        H.wait(e, "times_dst", it, back)
                        H.give(e.tensor_reduce(ad[:, :], pr_dst[:, :, :], AX_X, ALU.add), "adst")
                        H.wait(e, "adst", it, back)
                        H.give(e.tensor_scalar(asrc[:, at], tab[:, :, D + 1], 1.0, None, ALU.mult), "keep_asrc")
                        H.give(e.tensor_scalar(adst[:, at], ad[:, :], 1.0, None, ALU.mult), "keep_adst")

                    def body(it):
                        wait_count(e, s_g, it, 16 * G, 16 * G)
                        next_ends(e, E, ends, it)
                        dve_conv(e, V, it, agg, both, conv)
                        V.wait(e, "leaky", it)
                        V.give(e.tensor_tensor(conv[:, :, :], conv[:, :, :], X[:, bass.ds(it * G, G), :], ALU.add), "y")
                        dve_layernorm(e, V, it, conv[:, :, :], d[:, :, :], sq[:, :, :], s1, s2, x_new[:, :, :], "y", A,
                                      out_free=lambda: T.wait(e, "tr", it, 1))
                        V.give(e.tensor_scalar(X[:, bass.ds(it * G, G), :], x_new[:, :, :], 1.0, None, ALU.mult), "keep")
                        if not isinstance(it, int) or it > 0:
                            scores(it, 1)
                    first_ends(e, E, ends)
                    e.memset(tab[:, :, D:D + 1], 1.0).then_inc(s_one, 1)
                    loop(e, NG, body, apart=2)
                    scores(NG, 1)

                @block.tensor
                def _(e):
                    def body(it):
                        V.wait(e, "ln_out", it)
                        AH.wait(e, "xT", it, 1)
                        pe_transpose_group(e, T, TP, x_new, it, "tr")
                        AH.wait(e, "xT", it)
                        AH.wait(e, "keep_h", it, 1)
                        for g in range(G):
                            ins = e.matmul(O[:, g * P:g * P + D], xT[:, g * P:(g + 1) * P], w96["W"][:, :], start=True, stop=True)
                        T.give(ins, "mm")
                    loop(e, NG, body)

                @block.scalar
                def _(e):
                    def body(it):
                        act_std(e, A, V, it, s2)
                        T.wait(e, "tr", it)
                        AH.give(e.activation(xT[:, :], TP[0:D, 0:G * P], ACT.Copy), "xT")
                        T.wait(e, "mm", it)
                        wait_count(e, s_o, it, 16, 0)
                        h = O[:, 0:G * P].rearrange("p (g c) -> p g c", c=P)[:, :, 0:D]
                        H.wait(e, "keep_asrc", it, 1)
                        AH.give(e.activation(tab[:, :, 0:D], h, ACT.Copy), "h")
                        AH.give(e.activation(R[:, bass.ds(it * G, G), :], h, ACT.Copy), "keep_h")
                    loop(e, NG, body)

                @block.sync
                def _(e):
                    def body(it):
                        H.wait(e, "asrc", it)
                        e.dma_start(h_tab[bass.ds(it * (G * P), G * P), :].rearrange("(g p) d -> p g d", p=P), tab[:, :, :]).then_inc(s_o, 16)
                    e.wait_ge(s_one, 1)
                    loop(e, NG, body)
                    e.wait_ge(s_o, 16 * NG)

                @block.gpsimd
                def _(e):
                    def scatter(it, back):
                        H.wait(e, "adst", it, back)
                        for g in range(G):
                            e.indirect_dma_start(adst_lin, bass.IndirectOffsetOnAxis(starts[:, g:g + 1], axis=0), ad[:, g:g + 1],
                                                 None, bounds_check=EP - 1, oob_is_err=False).then_inc(s_sc, 16)

                    def body(it):
                        E.wait(e, "ends", it)
                        V.wait(e, "flag", it, 1)
                        for g in range(G):
                            e.indirect_dma_start(agg[:, g, :], None, scan_out, bass.IndirectOffsetOnAxis(ends[:, g:g + 1], axis=0),
                                                 bounds_check=EP - 1, oob_is_err=False).then_inc(s_g, 16)
                        if not isinstance(it, int) or it > 1:
                            scatter(it, 2)
                    loop(e, NG, body, apart=2)
                    scatter(NG, 2)
                    scatter(NG, 1)
                    e.wait_ge(s_sc, 16 * G * NG)

        with Phase("d3") as ph:
            first = ph.sb("first", [P, EC])
            keep_b = ph.sb("keep_b", [P, EC], BF16)
            ad_e = ph.sb("ad_e", [P, EC])
            still = ph.sb("still", [P, EC])
            zeros = ph.sb("zeros", [P, EC])
            row = ph.sb("row", [1, 3, P])
            prev = ph.sb("prev", [P, 1])
            s_ld, s_z, s_v, s_c, s_o = ph.sem("ld"), ph.sem("z"), ph.sem("v"), ph.sem("c"), ph.sem("o")
            pm = lambda ap: ap.rearrange("(p c) -> p c", p=P)
            col = lambda ap: ap.rearrange("(p a) -> p a", a=1)
            with nc.Block() as block:
                @block.vector
                def _(e):
                    e.memset(zeros[:, :], 0.0).then_inc(s_z, 1)
                    e.memset(row[:, 2, :], 0.0).then_inc(s_z, 1)
                    e.wait_ge(s_z, 2)
                    e.wait_ge(s_ld, 32)
                    e.tensor_tensor_scan(still[:, :], keep_b[:, :], zeros[:, :], 1.0, ALU.mult, ALU.add).then_inc(s_v, 1)
                    e.tensor_tensor_scan(ad_e[:, :], keep_b[:, :], first[:, :], 0.0, ALU.mult, ALU.add).then_inc(s_v, 1)
                    e.wait_ge(s_c, 64)
                    e.tensor_tensor_scan(row[:, 2, 1:P], row[:, 1, 0:P - 1], row[:, 0, 0:P - 1], 0.0, ALU.mult, ALU.add).then_inc(s_v, 1)
                    e.wait_ge(s_c, 96)
                    e.wait_ge(s_v, 2)
                    e.scalar_tensor_tensor(ad_e[:, :], still[:, :], prev[:, 0:1], ad_e[:, :], ALU.mult, ALU.add).then_inc(s_v, 1)

                @block.sync
                def _(e):
                    e.dma_start(first[:, :], adst_lin.rearrange("(p c) d -> p (c d)", p=P)).then_inc(s_ld, 16)
                    e.dma_start(keep_b[:, :], pm(keep_row)).then_inc(s_ld, 16)
                    e.wait_ge(s_v, 2)
                    e.dma_start(col(carry_dram[0, :]), ad_e[:, EC - 1:EC]).then_inc(s_c, 16)
                    e.dma_start(col(carry_dram[1, :]), still[:, EC - 1:EC]).then_inc(s_c, 16)
                    e.wait_ge(s_c, 32)
                    e.dma_start(row[:, 0, :], carry_dram[0:1, :]).then_inc(s_c, 16)
                    e.dma_start(row[:, 1, :], carry_dram[1:2, :]).then_inc(s_c, 16)
                    e.wait_ge(s_v, 3)
                    e.wait_ge(s_c, 64)
                    e.dma_start(carry_dram[2:3, :], row[:, 2, :]).then_inc(s_c, 16)
                    e.wait_ge(s_c, 80)
                    e.dma_start(prev[:, :], col(carry_dram[2, :])).then_inc(s_c, 16)
                    e.wait_ge(s_v, 4)
                    e.dma_start(pm(ad_row), ad_e[:, :]).then_inc(s_o, 16)
                    e.wait_ge(s_o, 16)

        with Phase("e3", edge=True) as ph:
            NI, BT = NCH // U, U * K
            s_passed = ph.sem("passed")
            idx = [ph.sb(f"idx{u}", [P, K], I32) for u in range(U)]
            got = [ph.sb(f"got{u}", [P, K, HW]) for u in range(U)]
            hold = ph.sb("hold", [P, BT, HW])
            ad_t = ph.sb("ad_t", [BT, P])
            neg_t = ph.sb("neg_t", [BT, P], BF16)
            z = ph.sb("z", [BT, P])
            zl = ph.sb("zl", [BT, P])
            own = ph.sb("own", [BT, P])
            opened = ph.sb("opened", [BT, 1])
            open_row = ph.sb("open_row", [1, BT])
            carry = ph.sb("carry", [1, BT + 1])
            rm = ph.sb("rm", [BT, P + 1])
            wd = ph.sb("wd", [BT, 2, P])
            parts = ph.sb("parts", [64 + BT, P], BF16)
            mid = ph.sb("mid", [BT, P], BF16)
            sel = ph.sb("sel", [64 + BT, BT, DN], BF16)
            emsg = [ph.sb(f"emsg{s}", [P, K, DN]) for s in range(2)]
            msg = [ph.sb(f"msg{s}", [DN, CH]) for s in range(2)]
            run = [ph.sb(f"run{s}", [DN, CH]) for s in range(2)]
            out = [ph.sb(f"out{u}", [P, K, DN]) for u in range(U)]
            M = [ph.ps(f"M{s}", [P, CH]) for s in range(2)]
            Z = [ph.ps(f"Z{s}", [P, CH]) for s in range(2)]
            B = [ph.ps(f"B{s}", [P, CH]) for s in range(2)]
            small = ph.ps("small", [P, 512])
            ST, CT, PV = small[0:BT, 0:P], small[0:1, P:P + 2 * BT], small[0:BT, 2 * P:2 * P + 1]
            WT = ph.ps("WT", [P, 512])
            s_ix, s_init, s_row, s_rm = ph.sem("ix"), ph.sem("init"), ph.sem("row"), ph.sem("rm")
            s_g = [ph.sem(f"g{u}") for u in range(U)]
            s_st = [ph.sem(f"st{u}") for u in range(U)]
            T = [ph.steps(f"T{u}", ["fwd", "back"]) for u in range(U)]
            A = [ph.steps(f"A{u}", ["msg", "out"]) for u in range(U)]
            V = [ph.steps(f"V{u}", ["add", "scan"]) for u in range(U)]
            H = ph.steps("H", [f"hold{u}" for u in range(U)] + ["exp"])
            TB = ph.steps("TB", ["scores", "last", "carry", "weights"])
            VB = ph.steps("VB", ["z", "leaky", "own", "open", "carry0", "openrow", "carry", "rm0", "rm", "before", "w", "d",
                                  "high", "rest", "mid", "mid32", "low"])
            ad_b = ad_row.rearrange("(b t e) -> b t e", t=BT, e=P)
            neg_b = neg_row.rearrange("(b t e) -> b t e", t=BT, e=P)
            rmax_b = rmax_lin.rearrange("(b t e) d -> b t (e d)", t=BT, e=P)
            out_c = scan_out3.rearrange("(c p k) d -> c p (k d)", p=P, k=K)

            def summed(it, u, lag):
                return not isinstance(it, int) or (it - 1) * U + u >= lag

            def lagging(u, lag):
                v, back = behind(u, lag)
                return v, back + 1

            with nc.Block() as block:
                @block.sync
                def _(e):
                    def store(it, u):
                        v, back = lagging(u, 1)
                        A[v].wait(e, "out", it, back)
                        e.dma_start(out_c[bass.ds(it * U + (u - 1 - U), 1)].rearrange("a p x -> (a p) x"),
                                    out[v][:, :, :].rearrange("p k d -> p (k d)")).then_inc(s_st[v], 16)

                    def rm_store(it):
                        VB.wait(e, "d", it, 1)
                        e.dma_start(rmax_b[bass.ds(it - 1, 1)].rearrange("a t e -> (a t) e"), rm[:, 1:P + 1]).then_inc(s_rm, 16)

                    def body(it):
                        if not isinstance(it, int) or it > 0:
                            rm_store(it)
                        e.dma_start(ad_t[:, :], ad_b[bass.ds(it, 1)].rearrange("a t e -> (a t) e")).then_inc(s_row, 16)
                        e.dma_start(neg_t[:, :], neg_b[bass.ds(it, 1)].rearrange("a t e -> (a t) e")).then_inc(s_row, 16)
                        for u in range(U):
                            if summed(it, u, 1):
                                store(it, u)
                    loop(e, NI, body, apart=4)
                    rm_store(NI)
                    for u in range(U):
                        store(NI, u)
                    store(NI + 1, 0)
                    e.wait_ge(s_rm, 16 * NI)
                    for u in range(U):
                        e.wait_ge(s_st[u], 16 * NI)

                @block.gpsimd
                def _(e):
                    def step(it, u):
                        wait_count(e, s_ix, it, U, u + 1)
                        H.wait(e, f"hold{u}", it, 1)
                        for k in range(K):
                            e.indirect_dma_start(got[u][:, k, :], None, h_tab, bass.IndirectOffsetOnAxis(idx[u][:, k:k + 1], axis=0),
                                                 bounds_check=NROW - 1, oob_is_err=False).then_inc(s_g[u], 16)
                    loop(e, NI, lambda it: [step(it, u) for u in range(U)])

                @block.tensor
                def _(e):
                    def turn_back(it, u):
                        v, back = lagging(u, 1)
                        V[v].wait(e, "scan", it, back)
                        w, back2 = lagging(u, 3)
                        A[w].wait(e, "out", it, back2)
                        for k in range(K):
                            ins = e.transpose(B[v % 2][:, k * DN:(k + 1) * DN], run[v % 2][:, k::K], ident[0:DN, 0:DN])
                        T[v].give(ins, "back")

                    def step(it, u):
                        s = u % 2
                        v, back = lagging(u, 2)
                        if u == 0:
                            VB.wait(e, "low", it, 1)
                        V[v].wait(e, "scan", it, back)
                        for k in range(K):
                            e.matmul(Z[s][0:DN, k * P:(k + 1) * P], sel[:, u * K + k, :], parts[:, :], start=True, stop=True)
                        V[u].wait(e, "add", it, 1)
                        A[v].wait(e, "msg", it, back)
                        for k in range(K):
                            ins = e.transpose(M[s][0:DN, k * P:(k + 1) * P], emsg[s][:, k, :], ident[:, :])
                        T[u].give(ins, "fwd")
                        if summed(it, u, 1):
                            turn_back(it, u)

                    def batch(it):
                        H.wait(e, f"hold{U - 1}", it)
                        TB.give(e.transpose(ST, hold[:, :, D + 1], ident[:, :]), "scores")
                        VB.wait(e, "open", it)
                        e.sem_inc(s_passed, 1)
                        e.transpose(CT[:, 0:BT], own[:, P - 1:P], ident[0:BT, 0:BT])
                        TB.give(e.transpose(CT[:, BT:2 * BT], opened[:, :], ident[0:BT, 0:BT]), "last")
                        VB.wait(e, "carry", it)
                        e.sem_inc(s_passed, 1)
                        TB.give(e.transpose(PV, carry[:, 0:BT], ident[0:1, 0:1]), "carry")
                        H.wait(e, "exp", it)
                        e.sem_inc(s_passed, 1)
                        TB.give(e.transpose(WT[:, 0:BT], wd[:, 0, :], ident[0:BT, 0:BT]), "weights")

                    def body(it):
                        if not isinstance(it, int) or it > 0:
                            for u in range(U):
                                step(it, u)
                        batch(it)
                    e.wait_ge(s_init, 7)
                    loop(e, NI, body, apart=4)
                    for u in range(U):
                        step(NI, u)
                    turn_back(NI + 1, 0)

                @block.vector
                def _(e):
                    e.memset(run[1][:, :], 0.0).then_inc(s_init, 1)
                    e.memset(carry[:, :], 0.0).then_inc(s_init, 1)
                    e.memset(sel[:, :, :], 0.0).then_inc(s_init, 1)
                    e.memset(parts[:, :], 0.0).then_inc(s_init, 1)
                    for u in range(U):
                        e.tensor_scalar(idx[u][:, :], src_tcols[:, u * K:(u + 1) * K], 1.0, None, ALU.mult).then_inc(s_ix, 1)
                    e.wait_ge(s_init, 4)
                    for at in (0, 32, 64):
                        e.tensor_copy(sel[at:at + BT, :, :], ident[at:at + BT, at:at + BT].unsqueeze(2).to_broadcast([BT, BT, DN])).then_inc(s_init, 1)
                    e.wait_ge(s_init, 7)

                    def scan(it, u):
                        v, back = lagging(u, 1)
                        w, back2 = lagging(u, 2)
                        x, back3 = lagging(u, 3)
                        A[v].wait(e, "msg", it, back)
                        T[v].wait(e, "fwd", it, back)
                        V[w].wait(e, "scan", it, back2)
                        T[x].wait(e, "back", it, back3)
                        p, q = v % 2, w % 2
                        V[v].give(e.tensor_tensor_scan(run[p][:, :], Z[p][0:DN, :], msg[p][:, :], run[q][:, CH - 1:CH], ALU.mult, ALU.add), "scan")

                    def step(it, u):
                        v, back = lagging(u, 2)
                        if u == 0:
                            TB.wait(e, "weights", it, 1)
                        T[v].wait(e, "fwd", it, back)
                        V[u].give(e.tensor_tensor(emsg[u % 2][:, :, :], hold[:, u * K:(u + 1) * K, 0:DN],
                                                  WT[:, u * K:(u + 1) * K].unsqueeze(2).to_broadcast([P, K, DN]), ALU.mult), "add")
                        if summed(it, u, 1):
                            scan(it, u)

                    def refill(it, u):
                        wait_count(e, s_g[u], it, 16 * K, 16 * K)
                        e.tensor_scalar(idx[u][:, :], src_tcols[:, bass.ds((it * U + U + u) * K, K)], 1.0, None, ALU.mult).then_inc(s_ix, 1)

                    def batch(it):
                        def op(ins, name):
                            VB.give(ins, name)
                            VB.wait(e, name, it)
                        wait_count(e, s_row, it, 32, 32)
                        TB.wait(e, "scores", it)
                        op(e.tensor_tensor(z[:, :], ST, ad_t[:, :], ALU.add), "z")
                        op(e.scalar_tensor_tensor(zl[:, :], z[:, :], 0.2, z[:, :], ALU.mult, ALU.max), "leaky")
                        VB.give(e.tensor_tensor_scan(own[:, :], neg_t[:, :], zl[:, :], NEG, ALU.add, ALU.max), "own")
                        VB.give(e.tensor_reduce(opened[:, :], neg_t[:, :], AX_X, ALU.min), "open")
                        op(e.tensor_copy(carry[:, 0:1], carry[:, BT:BT + 1]), "carry0")
                        TB.wait(e, "last", it)
                        op(e.tensor_copy(open_row[:, :], CT[:, BT:2 * BT]), "openrow")
                        VB.give(e.tensor_tensor_scan(carry[:, 1:BT + 1], open_row[:, :], CT[:, 0:BT], carry[:, 0:1], ALU.add, ALU.max), "carry")
                        TB.wait(e, "carry", it)
                        wait_count(e, s_rm, it, 16, 0)
                        op(e.tensor_copy(rm[:, 0:1], PV), "rm0")
                        op(e.tensor_tensor_scan(rm[:, 1:P + 1], neg_t[:, :], zl[:, :], rm[:, 0:1], ALU.add, ALU.max), "rm")
                        VB.give(e.tensor_tensor(z[:, :], rm[:, 0:P], neg_t[:, :], ALU.add), "before")
                        VB.give(e.tensor_tensor(wd[:, 0, :], zl[:, :], rm[:, 1:P + 1], ALU.subtract), "w")
                        VB.wait(e, "before", it)
                        VB.give(e.tensor_tensor(wd[:, 1, :], z[:, :], rm[:, 1:P + 1], ALU.subtract), "d")
                        H.wait(e, "exp", it)
                        op(e.tensor_copy(parts[0:BT, :], wd[:, 1, :]), "high")
                        op(e.tensor_tensor(z[:, :], wd[:, 1, :], parts[0:BT, :], ALU.subtract), "rest")
                        op(e.tensor_copy(mid[:, :], z[:, :]), "mid")
                        VB.give(e.tensor_copy(parts[32:32 + BT, :], mid[:, :]), "mid32")
                        VB.give(e.tensor_tensor(parts[64:64 + BT, :], z[:, :], mid[:, :], ALU.subtract), "low")

                    def body(it):
                        for u in range(U):
                            if not isinstance(it, int) or it > 0:
                                step(it, u)
                            refill(it, u)
                        batch(it)
                    loop(e, NI, body, apart=4)
                    for u in range(U):
                        step(NI, u)
                    scan(NI + 1, 0)

                @block.scalar
                def _(e):
                    def to_out(it, u):
                        v, back = lagging(u, 1)
                        T[v].wait(e, "back", it, back)
                        wait_stored(e, s_st[v], it, back)
                        A[v].give(e.activation(out[v][:, :, :], B[v % 2][:, 0:K * DN].rearrange("p (k d) -> p k d", k=K), ACT.Copy), "out")

                    def step(it, u):
                        v, back = lagging(u, 2)
                        T[u].wait(e, "fwd", it, 1)
                        V[v].wait(e, "scan", it, back)
                        A[u].give(e.activation(msg[u % 2][:, :], M[u % 2][0:DN, :], ACT.Copy), "msg")
                        if summed(it, u, 1):
                            to_out(it, u)

                    def body(it):
                        for u in range(U):
                            if not isinstance(it, int) or it > 0:
                                step(it, u)
                            wait_count(e, s_g[u], it, 16 * K, 16 * K)
                            V[u].wait(e, "add", it, 1)
                            H.give(e.activation(hold[:, u * K:(u + 1) * K, :], got[u][:, :, :], ACT.Copy), f"hold{u}")
                        VB.wait(e, "d", it)
                        H.give(e.activation(wd[:, :, :], wd[:, :, :], ACT.Exp), "exp")
                    loop(e, NI, body, apart=4)
                    for u in range(U):
                        step(NI, u)
                    to_out(NI + 1, 0)

        with Phase("n7") as ph:
            ends = ph.sb("ends", [P, G], I32)
            agg = ph.sb("agg", [P, G, DN])
            edges = ph.sb("edges", [P, G, DN])
            mx = ph.sb("mx", [P, G, 1])
            zs, z2, m2, em, es, fl = (ph.sb(n, [P, G]) for n in ("zs", "z2", "m2", "em", "es", "fl"))
            y = ph.sb("y", [P, G, D])
            d = ph.sb("d", [P, G, D])
            sq = ph.sb("sq", [P, G, D])
            ob = ph.sb("ob", [P, G, D])
            s1, s2 = ph.sb("s1", [P, G]), ph.sb("s2", [P, G])
            E = ph.steps("E", ["ends"])
            V = ph.steps("V", ["fl", "own_z", "own_leaky", "edge_max", "no_edges", "edge_max_or_neg", "max", "edge_exponent", "own_exponent",
                               "edge_scale", "edge_sums", "own_h", "numerator", "denominator", "one_over", "ratio", "y"] + LN)
            A = ph.steps("A", ["em", "es", "tanh", "ln_std"])
            s_g, s_o = ph.sem("g"), ph.sem("o")
            bc = lambda ap, n: ap.unsqueeze(2).to_broadcast([P, G, n])
            with nc.Block() as block:
                @block.gpsimd
                def _(e):
                    pool_gather_ends(e, E, ends, V, [(mx, rmax_lin, "edge_max"), (agg, scan_out3, "edge_sums")], s_g)

                @block.vector
                def _(e):
                    def body(it):
                        at = bass.ds(it * G, G)

                        def op(ins, name):
                            V.give(ins, name)
                            V.wait(e, name, it)
                        op(e.tensor_scalar(fl[:, :], flag[:, at], 1.0, None, ALU.mult), "fl")
                        op(e.tensor_tensor(zs[:, :], asrc[:, at], adst[:, at], ALU.add), "own_z")
                        op(e.scalar_tensor_tensor(z2[:, :], zs[:, :], 0.2, zs[:, :], ALU.mult, ALU.max), "own_leaky")
                        wait_count(e, s_g, it, 32 * G, 32 * G)
                        next_ends(e, E, ends, it)
                        op(e.tensor_tensor(m2[:, :], mx[:, :, 0], fl[:, :], ALU.mult), "edge_max")
                        op(e.tensor_scalar(zs[:, :], fl[:, :], -NEG, NEG, ALU.mult, ALU.add), "no_edges")
                        op(e.tensor_tensor(m2[:, :], m2[:, :], zs[:, :], ALU.add), "edge_max_or_neg")
                        op(e.tensor_tensor(zs[:, :], m2[:, :], z2[:, :], ALU.max), "max")
                        op(e.tensor_tensor(m2[:, :], m2[:, :], zs[:, :], ALU.subtract), "edge_exponent")
                        op(e.tensor_tensor(z2[:, :], z2[:, :], zs[:, :], ALU.subtract), "own_exponent")
                        A.wait(e, "es", it)
                        op(e.tensor_tensor(em[:, :], em[:, :], fl[:, :], ALU.mult), "edge_scale")
                        op(e.tensor_tensor(edges[:, :, :], agg[:, :, :], bc(em[:, :], DN), ALU.mult), "edge_sums")
                        op(e.tensor_tensor(d[:, :, :], R[:, at, :], bc(es[:, :], D), ALU.mult), "own_h")
                        op(e.tensor_tensor(d[:, :, :], edges[:, :, 0:D], d[:, :, :], ALU.add), "numerator")
                        op(e.scalar_tensor_tensor(es[:, :], edges[:, :, D], 1e-16, es[:, :], ALU.add, ALU.add), "denominator")
                        op(e.reciprocal(es[:, :], es[:, :]), "one_over")
                        op(e.tensor_tensor(d[:, :, :], d[:, :, :], bc(es[:, :], D), ALU.mult), "ratio")
                        op(e.tensor_tensor(y[:, :, :], d[:, :, :], rows["bias"][:, :].unsqueeze(1).to_broadcast([P, G, D]), ALU.add), "y")
                        A.wait(e, "tanh", it)
                        wait_count(e, s_o, it, 16, 0)
                        e.tensor_tensor(sq[:, :, :], ob[:, :, :], X[:, at, :], ALU.add).then_inc(s_y, 1)
                        wait_count(e, s_y, it, 1, 1)
                        dve_layernorm(e, V, it, sq[:, :, :], d[:, :, :], y[:, :, :], s1, s2, sq[:, :, :], "y", A)
                    s_y = ph.sem("y")
                    first_ends(e, E, ends)
                    loop(e, NG, body)

                @block.scalar
                def _(e):
                    def body(it):
                        V.wait(e, "own_exponent", it)
                        A.give(e.activation(em[:, :], m2[:, :], ACT.Exp), "em")
                        A.give(e.activation(es[:, :], z2[:, :], ACT.Exp), "es")
                        V.wait(e, "y", it)
                        A.give(e.activation(ob[:, :, :], y[:, :, :], ACT.Tanh), "tanh")
                        act_std(e, A, V, it, s2)
                        V.wait(e, "ln_out", it)
                        e.dma_start(t["out"][bass.ds(it * (G * P), G * P), :].rearrange("(g p) d -> p g d", p=P), sq[:, :, :]).then_inc(s_o, 16)
                    loop(e, NG, body)
                    e.wait_ge(s_o, 16 * NG)


_WEIGHTS = ["L0_gnn_qW", "L0_gnn_kW", "L0_gnn_vW", "L1_gnn_We", "L1_gnn_be", "L1_gnn_W1", "L1_gnn_b1", "L1_gnn_W2", "L1_gnn_b2",
            "L1_gnn_gamma", "L1_gnn_beta", "L2_gnn_W1_msg", "L2_gnn_W1_edge", "L2_gnn_W1_root", "L2_gnn_b1", "L2_gnn_W2_msg",
            "L2_gnn_W2_edge", "L2_gnn_W2_root", "L2_gnn_b2", "L3_gnn_W", "L3_gnn_att_src", "L3_gnn_att_dst", "L3_gnn_bias"]


def kernel(**inputs):
    import concourse.bacc as bacc
    from concourse.bass_utils import run_bass_kernel_spmd

    x, src, dst, attr = (np.asarray(inputs[n]) for n in ("x", "src", "dst", "edge_attr_32"))
    n_nodes, D = x.shape
    n_edges, DE = attr.shape
    NT, NCH = padded_sizes(n_nodes, n_edges)
    n_rows, n_padded = NT * P, NCH * CH
    x_pad = np.zeros((n_rows, D), x.dtype)
    x_pad[:n_nodes] = x
    src_pad = np.full(n_padded, n_nodes, src.dtype)
    src_pad[:n_edges] = src
    src_cols = np.ascontiguousarray(src_pad.reshape(NCH, P, K).transpose(1, 0, 2).reshape(P, NCH * K))
    dst_pad = np.full(n_padded, n_nodes, dst.dtype)
    dst_pad[:n_edges] = dst
    dst_prev = np.full(n_padded, -1, dst.dtype)
    dst_prev[1:] = dst_pad[:-1]
    def tile_cols(a):
        return np.ascontiguousarray(a.reshape(NCH * K, P).T)

    attr_T = np.zeros((DE + 1, n_padded), attr.dtype)
    attr_T[:DE, :n_edges] = attr.T
    attr_T[DE] = 1
    arrays = {"x": x_pad, "src_pad": src_pad, "src_cols": src_cols, "src_tcols": tile_cols(src_pad),
              "dst_tcols": tile_cols(dst_pad), "prev_tcols": tile_cols(dst_prev), "dst_pad": dst_pad, "dst_prev": dst_prev, "attr_T": attr_T}
    for n in _WEIGHTS:
        arrays[n] = np.ascontiguousarray(inputs[n])

    nc = bacc.Bacc("TRN2", target_bir_lowering=False, num_devices=1)
    t = {n: nc.dram_tensor(f"in_{n}", a.shape, mybir.dt.from_np(a.dtype), kind="ExternalInput").ap() for n, a in arrays.items()}
    t["out"] = nc.dram_tensor("out_nodes", (n_rows, D), F32, kind="ExternalOutput").ap()
    build(nc, t, n_nodes, n_edges, D, DE)
    r = run_bass_kernel_spmd(nc, [{f"in_{n}": a for n, a in arrays.items()}], core_ids=[0])
    return r.results[0]["out_nodes"][:n_nodes]
```
